# Optimizing a Trainium2 kernel written in Bass

```python
import numpy as np
import jax
import jax.numpy as jnp

def _softmax(x, axis=-1):
    return jax.nn.softmax(x, axis=axis)

def _gelu(x):
    return jax.nn.gelu(x, approximate=True)

def _silu(x):
    return jax.nn.silu(x)

def _sigmoid(x):
    return jax.nn.sigmoid(x)

def _layernorm(x, axis=-1, eps=1e-05):
    m = jnp.mean(x, axis=axis, keepdims=True)
    v = jnp.var(x, axis=axis, keepdims=True)
    return (x - m) / jnp.sqrt(v + eps)

def _scatter_add(tgt, idx, src, axis=0):
    return tgt.at[idx].add(src)

def _segment_sum(src, seg, n):
    return jax.ops.segment_sum(src, seg, n)
kernel_name = 'mk_hybrid_d1_jaxref_r8_aa8dd6'

def setup_inputs(seed: int=0):
    np.random.seed(seed)
    _w = jnp.asarray

    def _L0_attn_a_setup():
        import jax, jax.numpy as jnp
        import numpy as np
        B, T, D = (8, 256, 128)

        def rmsnorm(x, gamma):
            n = jnp.maximum(jnp.linalg.norm(x, axis=-1, keepdims=True), 1e-12)
            return x / n * D ** 0.5 * (gamma + 1.0)

        def lru_cell_pointwise(x_in, hidden, Wi, Wif, Whf, bhf):
            ni = jnp.tanh(x_in @ Wi.T)
            g = jax.nn.sigmoid(hidden @ Whf.T + bhf + x_in @ Wif.T)
            return hidden + g * (jnp.tanh(ni) - hidden)

        def lru_layer(x, Wi, Wif, Whf, bhf, h0):
            ni = jnp.tanh(jnp.einsum('btd,hd->bth', x, Wi))
            fi = jnp.einsum('btd,hd->bth', x, Wif)
            h_init = jnp.broadcast_to(h0, (x.shape[0], h0.shape[0]))

            def step(h, inp):
                ni_t, fi_t = inp
                g = jax.nn.sigmoid(h @ Whf.T + bhf + fi_t)
                h_next = h + g * (jnp.tanh(ni_t) - h)
                return (h_next, h_next)
            _, hs = jax.lax.scan(step, h_init, (ni.transpose(1, 0, 2), fi.transpose(1, 0, 2)))
            return hs.transpose(1, 0, 2)
        key = jax.random.key(seed)
        ks = jax.random.split(key, 8)
        s = 1.0 / np.sqrt(D)
        return {'x': jax.random.normal(ks[0], (B, T, D), jnp.float32), 'gamma': jnp.zeros((D,), jnp.float32), 'gWi': jax.random.normal(ks[1], (D, D), jnp.float32) * s, 'gWif': jax.random.normal(ks[2], (D, D), jnp.float32) * s, 'gWhf': jax.random.normal(ks[3], (D, D), jnp.float32) * s, 'gbhf': jnp.zeros((D,), jnp.float32), 'lWi': jax.random.normal(ks[4], (2, D, D), jnp.float32) * s, 'lWif': jax.random.normal(ks[5], (2, D, D), jnp.float32) * s, 'lWhf': jax.random.normal(ks[6], (2, D, D), jnp.float32) * s, 'lbhf': jnp.zeros((2, D), jnp.float32), 'l_init_hidden': jnp.zeros((2, D), jnp.float32)}
    _L0_attn_a_in = _L0_attn_a_setup()

    def _L0_attn_b_setup():
        import jax, jax.numpy as jnp
        import numpy as np
        EPS = 1e-06

        def _phi(x):
            return jax.nn.elu(x) + 1.0

        def chunked_causal_linear_attention(q, k, v, chunk=128):
            B, H, N, D = q.shape
            qp, kp = (_phi(q), _phi(k))
            NC = N // chunk

            def to_chunks(t):
                return t.reshape(B, H, NC, chunk, D).transpose(2, 0, 1, 3, 4)
            qs, ks, vs = (to_chunks(qp), to_chunks(kp), to_chunks(v))

            def step(carry, inp):
                s_kv, s_k = carry
                qc, kc, vc = inp
                kv_c = jnp.einsum('bhcd,bhce->bhcde', kc, vc)
                kv_scan = jnp.cumsum(kv_c, axis=2)
                out = jnp.einsum('bhcd,bhde->bhce', qc, s_kv) + jnp.einsum('bhcd,bhcde->bhce', qc, kv_scan)
                norm = jnp.sum(qc * s_k[:, :, None, :], axis=-1, keepdims=True) + jnp.sum(qc * jnp.cumsum(kc, axis=2), axis=-1, keepdims=True)
                out = out / jnp.maximum(norm, EPS)
                return ((s_kv + kv_c.sum(axis=2), s_k + kc.sum(axis=2)), out)
            init = (jnp.zeros((B, H, D, D), q.dtype), jnp.zeros((B, H, D), q.dtype))
            _, outs = jax.lax.scan(step, init, (qs, ks, vs))
            return outs.transpose(1, 2, 0, 3, 4).reshape(B, H, N, D)

        def causal_block_mean(x, block):
            B, H, N, D = x.shape
            prefix = jnp.cumsum(x, axis=2)
            idx = jnp.arange(N)
            start = idx // block * block
            prev_idx = jnp.clip(start - 1, 0, None)
            prev = prefix[:, :, prev_idx, :]
            prev = jnp.where((start > 0)[None, None, :, None], prev, 0.0)
            sums = prefix - prev
            lengths = (idx - start + 1).astype(x.dtype)[None, None, :, None]
            return sums / lengths

        def local_attention(q, k, v, window):
            B, H, N, D = q.shape
            scale = 1.0 / np.sqrt(D)
            scores = jnp.einsum('bhqd,bhkd->bhqk', q, k) * scale
            rows = jnp.arange(N)[:, None]
            cols = jnp.arange(N)[None, :]
            mask = (cols <= rows) & (cols > rows - window)
            scores = jnp.where(mask[None, None], scores, -1e+30)
            probs = jax.nn.softmax(scores, axis=-1)
            return jnp.einsum('bhqk,bhkd->bhqd', probs, v)

        def hale_forward(x, Wq, Wk, Wv, Wkl, Wvl, haar_Wk, haar_Wv, haar_scale, Wg, bg, Wgo, bgo, Wo, bo, num_heads=16, local_window=64, chunk_size=128):
            B, N, Dm = x.shape
            Dh = Dm // num_heads

            def heads(t):
                return t.reshape(B, N, num_heads, Dh).transpose(0, 2, 1, 3)

            def merge(t):
                return t.transpose(0, 2, 1, 3).reshape(B, N, Dm)
            q = heads(x @ Wq.T)
            k = heads(x @ Wk.T)
            v = heads(x @ Wv.T)
            k_loc = heads(x @ Wkl.T)
            v_loc = heads(x @ Wvl.T)
            local_out = local_attention(q, k_loc, v_loc, min(local_window, N))
            glob = chunked_causal_linear_attention(q, k, v, chunk=chunk_size)
            scale_w = jax.nn.softmax(haar_scale)
            num_levels = haar_scale.shape[0]
            for lvl in range(num_levels):
                block = 2 ** (lvl + 1)
                k_lvl = causal_block_mean(k, block) @ haar_Wk[lvl].T
                v_lvl = causal_block_mean(v, block) @ haar_Wv[lvl].T
                glob = glob + scale_w[lvl] * chunked_causal_linear_attention(q, k_lvl, v_lvl, chunk=chunk_size)
            local_m = merge(local_out)
            glob_m = merge(glob)
            diff = local_m - glob_m
            gate_h = jax.nn.silu(jnp.concatenate([x, diff], axis=-1) @ Wg.T + bg)
            alpha = jax.nn.sigmoid(gate_h @ Wgo.T + bgo)
            mixed = alpha * local_m + (1.0 - alpha) * glob_m
            return mixed @ Wo.T + bo
        key = jax.random.key(seed)
        B, N, Dm, H, L = (1, 256, 128, 16, 4)
        Dh = Dm // H
        ks = jax.random.split(key, 16)
        s_dm = 1.0 / np.sqrt(Dm)
        s_dh = 1.0 / np.sqrt(Dh)
        return {'x': jax.random.normal(ks[0], (B, N, Dm), jnp.float32), 'Wq': jax.random.normal(ks[1], (Dm, Dm), jnp.float32) * s_dm, 'Wk': jax.random.normal(ks[2], (Dm, Dm), jnp.float32) * s_dm, 'Wv': jax.random.normal(ks[3], (Dm, Dm), jnp.float32) * s_dm, 'Wkl': jax.random.normal(ks[4], (Dm, Dm), jnp.float32) * s_dm, 'Wvl': jax.random.normal(ks[5], (Dm, Dm), jnp.float32) * s_dm, 'haar_Wk': jax.random.normal(ks[6], (L, Dh, Dh), jnp.float32) * s_dh, 'haar_Wv': jax.random.normal(ks[7], (L, Dh, Dh), jnp.float32) * s_dh, 'haar_scale': jax.random.normal(ks[8], (L,), jnp.float32) * 0.1, 'Wg': jax.random.normal(ks[9], (Dm, 2 * Dm), jnp.float32) * (1.0 / np.sqrt(2 * Dm)), 'bg': jnp.zeros((Dm,), jnp.float32), 'Wgo': jax.random.normal(ks[10], (1, Dm), jnp.float32) * s_dm, 'bgo': jnp.zeros((1,), jnp.float32), 'Wo': jax.random.normal(ks[11], (Dm, Dm), jnp.float32) * s_dm, 'bo': jnp.zeros((Dm,), jnp.float32)}
    _L0_attn_b_in = _L0_attn_b_setup()

    def _L0_ffn_setup():
        import jax, jax.numpy as jnp
        import numpy as np
        EPS = 1e-05

        @jax.custom_vjp
        def ste_quantize(w):
            scale = jnp.maximum(jnp.mean(jnp.abs(w)), EPS)
            return jnp.clip(jnp.round(w / scale), -1.0, 1.0)

        def _ste_fwd(w):
            return (ste_quantize(w), None)

        def _ste_bwd(_, g):
            return (g,)
        ste_quantize.defvjp(_ste_fwd, _ste_bwd)
        key = jax.random.key(seed)
        k1, k2 = jax.random.split(key)
        x = jax.random.normal(k1, (8, 1024, 128), dtype=jnp.float32)
        weight = jax.random.normal(k2, (128, 128), dtype=jnp.float32) * 0.02
        return {'x': x, 'weight': weight}
    _L0_ffn_in = _L0_ffn_setup()
    _d = {'L0_attn_a_x': _L0_attn_a_in['x'], 'L0_attn_a_gamma': _L0_attn_a_in['gamma'], 'L0_attn_a_gWi': _L0_attn_a_in['gWi'], 'L0_attn_a_gWif': _L0_attn_a_in['gWif'], 'L0_attn_a_gWhf': _L0_attn_a_in['gWhf'], 'L0_attn_a_gbhf': _L0_attn_a_in['gbhf'], 'L0_attn_a_lWi': _L0_attn_a_in['lWi'], 'L0_attn_a_lWif': _L0_attn_a_in['lWif'], 'L0_attn_a_lWhf': _L0_attn_a_in['lWhf'], 'L0_attn_a_lbhf': _L0_attn_a_in['lbhf'], 'L0_attn_a_l_init_hidden': _L0_attn_a_in['l_init_hidden'], 'L0_attn_b_Wq': _L0_attn_b_in['Wq'], 'L0_attn_b_Wk': _L0_attn_b_in['Wk'], 'L0_attn_b_Wv': _L0_attn_b_in['Wv'], 'L0_attn_b_Wkl': _L0_attn_b_in['Wkl'], 'L0_attn_b_Wvl': _L0_attn_b_in['Wvl'], 'L0_attn_b_haar_Wk': _L0_attn_b_in['haar_Wk'], 'L0_attn_b_haar_Wv': _L0_attn_b_in['haar_Wv'], 'L0_attn_b_haar_scale': _L0_attn_b_in['haar_scale'], 'L0_attn_b_Wg': _L0_attn_b_in['Wg'], 'L0_attn_b_bg': _L0_attn_b_in['bg'], 'L0_attn_b_Wgo': _L0_attn_b_in['Wgo'], 'L0_attn_b_bgo': _L0_attn_b_in['bgo'], 'L0_attn_b_Wo': _L0_attn_b_in['Wo'], 'L0_attn_b_bo': _L0_attn_b_in['bo'], 'L0_ffn_weight': _L0_ffn_in['weight']}
    _x0 = _d['L0_attn_a_x']
    _d['L0_attn_a_x'] = jax.random.normal(jax.random.fold_in(jax.random.key(seed), 1), (4, 1024, 128), dtype=_x0.dtype)
    del _x0
    return _d

def reference(L0_attn_a_x, L0_attn_a_gamma, L0_attn_a_gWi, L0_attn_a_gWif, L0_attn_a_gWhf, L0_attn_a_gbhf, L0_attn_a_lWi, L0_attn_a_lWif, L0_attn_a_lWhf, L0_attn_a_lbhf, L0_attn_a_l_init_hidden, L0_attn_b_Wq, L0_attn_b_Wk, L0_attn_b_Wv, L0_attn_b_Wkl, L0_attn_b_Wvl, L0_attn_b_haar_Wk, L0_attn_b_haar_Wv, L0_attn_b_haar_scale, L0_attn_b_Wg, L0_attn_b_bg, L0_attn_b_Wgo, L0_attn_b_bgo, L0_attn_b_Wo, L0_attn_b_bo, L0_ffn_weight):

    def _L0_attn_a_ref(x, gamma, gWi, gWif, gWhf, gbhf, lWi, lWif, lWhf, lbhf, l_init_hidden):
        import jax, jax.numpy as jnp
        import numpy as np
        B, T, D = (8, 256, 128)

        def rmsnorm(x, gamma):
            n = jnp.maximum(jnp.linalg.norm(x, axis=-1, keepdims=True), 1e-12)
            return x / n * D ** 0.5 * (gamma + 1.0)

        def lru_cell_pointwise(x_in, hidden, Wi, Wif, Whf, bhf):
            ni = jnp.tanh(x_in @ Wi.T)
            g = jax.nn.sigmoid(hidden @ Whf.T + bhf + x_in @ Wif.T)
            return hidden + g * (jnp.tanh(ni) - hidden)

        def lru_layer(x, Wi, Wif, Whf, bhf, h0):
            ni = jnp.tanh(jnp.einsum('btd,hd->bth', x, Wi))
            fi = jnp.einsum('btd,hd->bth', x, Wif)
            h_init = jnp.broadcast_to(h0, (x.shape[0], h0.shape[0]))

            def step(h, inp):
                ni_t, fi_t = inp
                g = jax.nn.sigmoid(h @ Whf.T + bhf + fi_t)
                h_next = h + g * (jnp.tanh(ni_t) - h)
                return (h_next, h_next)
            _, hs = jax.lax.scan(step, h_init, (ni.transpose(1, 0, 2), fi.transpose(1, 0, 2)))
            return hs.transpose(1, 0, 2)
        xn = rmsnorm(x, gamma)
        h = xn
        for i in range(2):
            h = lru_layer(h, lWi[i], lWif[i], lWhf[i], lbhf[i], l_init_hidden[i])
        y = lru_cell_pointwise(h, xn, gWi, gWif, gWhf, gbhf)
        return y + x

    def _L0_attn_b_ref(x, Wq, Wk, Wv, Wkl, Wvl, haar_Wk, haar_Wv, haar_scale, Wg, bg, Wgo, bgo, Wo, bo):
        import jax, jax.numpy as jnp
        import numpy as np
        EPS = 1e-06

        def _phi(x):
            return jax.nn.elu(x) + 1.0

        def chunked_causal_linear_attention(q, k, v, chunk=128):
            B, H, N, D = q.shape
            qp, kp = (_phi(q), _phi(k))
            NC = N // chunk

            def to_chunks(t):
                return t.reshape(B, H, NC, chunk, D).transpose(2, 0, 1, 3, 4)
            qs, ks, vs = (to_chunks(qp), to_chunks(kp), to_chunks(v))

            def step(carry, inp):
                s_kv, s_k = carry
                qc, kc, vc = inp
                kv_c = jnp.einsum('bhcd,bhce->bhcde', kc, vc)
                kv_scan = jnp.cumsum(kv_c, axis=2)
                out = jnp.einsum('bhcd,bhde->bhce', qc, s_kv) + jnp.einsum('bhcd,bhcde->bhce', qc, kv_scan)
                norm = jnp.sum(qc * s_k[:, :, None, :], axis=-1, keepdims=True) + jnp.sum(qc * jnp.cumsum(kc, axis=2), axis=-1, keepdims=True)
                out = out / jnp.maximum(norm, EPS)
                return ((s_kv + kv_c.sum(axis=2), s_k + kc.sum(axis=2)), out)
            init = (jnp.zeros((B, H, D, D), q.dtype), jnp.zeros((B, H, D), q.dtype))
            _, outs = jax.lax.scan(step, init, (qs, ks, vs))
            return outs.transpose(1, 2, 0, 3, 4).reshape(B, H, N, D)

        def causal_block_mean(x, block):
            B, H, N, D = x.shape
            prefix = jnp.cumsum(x, axis=2)
            idx = jnp.arange(N)
            start = idx // block * block
            prev_idx = jnp.clip(start - 1, 0, None)
            prev = prefix[:, :, prev_idx, :]
            prev = jnp.where((start > 0)[None, None, :, None], prev, 0.0)
            sums = prefix - prev
            lengths = (idx - start + 1).astype(x.dtype)[None, None, :, None]
            return sums / lengths

        def local_attention(q, k, v, window):
            B, H, N, D = q.shape
            scale = 1.0 / np.sqrt(D)
            scores = jnp.einsum('bhqd,bhkd->bhqk', q, k) * scale
            rows = jnp.arange(N)[:, None]
            cols = jnp.arange(N)[None, :]
            mask = (cols <= rows) & (cols > rows - window)
            scores = jnp.where(mask[None, None], scores, -1e+30)
            probs = jax.nn.softmax(scores, axis=-1)
            return jnp.einsum('bhqk,bhkd->bhqd', probs, v)

        def hale_forward(x, Wq, Wk, Wv, Wkl, Wvl, haar_Wk, haar_Wv, haar_scale, Wg, bg, Wgo, bgo, Wo, bo, num_heads=16, local_window=64, chunk_size=128):
            B, N, Dm = x.shape
            Dh = Dm // num_heads

            def heads(t):
                return t.reshape(B, N, num_heads, Dh).transpose(0, 2, 1, 3)

            def merge(t):
                return t.transpose(0, 2, 1, 3).reshape(B, N, Dm)
            q = heads(x @ Wq.T)
            k = heads(x @ Wk.T)
            v = heads(x @ Wv.T)
            k_loc = heads(x @ Wkl.T)
            v_loc = heads(x @ Wvl.T)
            local_out = local_attention(q, k_loc, v_loc, min(local_window, N))
            glob = chunked_causal_linear_attention(q, k, v, chunk=chunk_size)
            scale_w = jax.nn.softmax(haar_scale)
            num_levels = haar_scale.shape[0]
            for lvl in range(num_levels):
                block = 2 ** (lvl + 1)
                k_lvl = causal_block_mean(k, block) @ haar_Wk[lvl].T
                v_lvl = causal_block_mean(v, block) @ haar_Wv[lvl].T
                glob = glob + scale_w[lvl] * chunked_causal_linear_attention(q, k_lvl, v_lvl, chunk=chunk_size)
            local_m = merge(local_out)
            glob_m = merge(glob)
            diff = local_m - glob_m
            gate_h = jax.nn.silu(jnp.concatenate([x, diff], axis=-1) @ Wg.T + bg)
            alpha = jax.nn.sigmoid(gate_h @ Wgo.T + bgo)
            mixed = alpha * local_m + (1.0 - alpha) * glob_m
            return mixed @ Wo.T + bo
        return hale_forward(x, Wq, Wk, Wv, Wkl, Wvl, haar_Wk, haar_Wv, haar_scale, Wg, bg, Wgo, bgo, Wo, bo)

    def _L0_ffn_ref(x, weight):
        import jax, jax.numpy as jnp
        import numpy as np
        EPS = 1e-05

        @jax.custom_vjp
        def ste_quantize(w):
            scale = jnp.maximum(jnp.mean(jnp.abs(w)), EPS)
            return jnp.clip(jnp.round(w / scale), -1.0, 1.0)

        def _ste_fwd(w):
            return (ste_quantize(w), None)

        def _ste_bwd(_, g):
            return (g,)
        ste_quantize.defvjp(_ste_fwd, _ste_bwd)
        w_ternary = ste_quantize(weight)
        scale = jnp.maximum(jnp.mean(jnp.abs(weight)), EPS)
        return jnp.einsum('bsi,oi->bso', x, w_ternary * scale)
    x = L0_attn_a_x
    x = x + _L0_attn_a_ref(_layernorm(x, axis=-1), L0_attn_a_gamma, L0_attn_a_gWi, L0_attn_a_gWif, L0_attn_a_gWhf, L0_attn_a_gbhf, L0_attn_a_lWi, L0_attn_a_lWif, L0_attn_a_lWhf, L0_attn_a_lbhf, L0_attn_a_l_init_hidden)
    x = x + _L0_ffn_ref(_layernorm(x, axis=-1), L0_ffn_weight)
    x = x + _L0_attn_b_ref(_layernorm(x, axis=-1), L0_attn_b_Wq, L0_attn_b_Wk, L0_attn_b_Wv, L0_attn_b_Wkl, L0_attn_b_Wvl, L0_attn_b_haar_Wk, L0_attn_b_haar_Wv, L0_attn_b_haar_scale, L0_attn_b_Wg, L0_attn_b_bg, L0_attn_b_Wgo, L0_attn_b_bgo, L0_attn_b_Wo, L0_attn_b_bo)
    x = x + _L0_ffn_ref(_layernorm(x, axis=-1), L0_ffn_weight)
    return x

_drawn_inputs = setup_inputs


def setup_inputs(seed=0):
    import zlib

    import numpy as np

    out = dict(_drawn_inputs(seed))
    spreads = {'L0_attn_a_gamma': (0.0, 0.329),
     'L0_attn_a_gbhf': (0.0, 0.8),
     'L0_attn_a_lbhf': (0.0, 0.8),
     'L0_attn_a_l_init_hidden': (0.0, 2.0),
     'L0_attn_b_bg': (0.0, 2.0),
     'L0_attn_b_bo': (0.0, 0.1)}
    factors = {'L0_attn_a_gWif': 3.007,
     'L0_attn_a_lWhf': 7.201,
     'L0_attn_b_Wk': 7.691,
     'L0_attn_b_haar_Wk': 8.0,
     'L0_attn_b_haar_Wv': 4.834,
     'L0_attn_b_haar_scale': 8.0,
     'L0_attn_b_Wg': 5.327,
     'L0_attn_b_Wgo': 4.793}
    for name, (base, spread) in spreads.items():
        noise = np.random.default_rng([zlib.crc32(name.encode()), seed]).standard_normal(out[name].shape)
        drawn = base * np.exp(spread * noise) if base else spread * noise
        out[name] = jnp.asarray(drawn.astype(out[name].dtype))
    for name, factor in factors.items():
        out[name] = (out[name] * factor).astype(out[name].dtype)
    return out
```

```python
from contextlib import ExitStack

import concourse.bass as bass
from concourse import mybir

ALU = mybir.AluOpType
ACT = mybir.ActivationFunctionType
AX = mybir.AxisListType
F32 = mybir.dt.float32

BATCH, TOKENS, D = 4, 1024, 128
TC = 32
CHUNKS = TOKENS // TC
HEADS, DH = 16, 8
E9 = DH + 1
HG = 4
LEVELS = 5
LAG = 2
TURNS = CHUNKS + LAG
SV = BATCH * E9
VW = HEADS * SV
HALF = VW // 2
QW = HEADS * TC
OW = BATCH * HG * E9
NEG = -1.0e30
LN_EPS = 1.0e-5
ROUND = 1.5 * 2.0 ** 23
NORM_FLOOR = 1.0e-24 / D

MATS = ["i1", "f1", "r1", "i2", "f2", "r2", "gi", "gf", "gh", "wk", "wv", "qT", "klT", "vlT", "kT", "vT",
        "g1T", "g2T", "oT", "tern", "go"] + [f"hk{l}" for l in range(4)] + [f"hv{l}" for l in range(4)]
CONSTS = {"ident": 128, "means": LEVELS * 128, "causal": TC, "hmask": HEADS, "bmask": BATCH,
          "addmask": 3 * TC, "neghalf": 2, "ones": 128}



def build(nc, ins, out):
    with ExitStack() as ctx:
        def sb(name, shape):
            return ctx.enter_context(nc.sbuf_tensor(name, shape, F32))

        def ps(name, shape=(128, 512)):
            return ctx.enter_context(nc.psum_tensor(name, list(shape), F32))

        sems = {}

        def S(name):
            if name not in sems:
                sems[name] = ctx.enter_context(nc.semaphore(name))
            return sems[name]

        W = sb("W", [128, len(MATS) * 128])
        w = {n: W[:, 128 * k:128 * k + 128] for k, n in enumerate(MATS)}
        C = sb("C", [128, sum(CONSTS.values())])
        c_, at = {}, 0
        for n, k in CONSTS.items():
            c_[n] = C[:, at:at + k]
            at += k
        COLS = sb("COLS", [128, 12])
        ROWS = sb("ROWS", [2, 5 * 128 + 256])
        G1 = sb("G1", [128, 128])
        X = sb("X", [128, CHUNKS, 128])
        xn = sb("xn", [128, 128])
        XNT = sb("XNT", [128, CHUNKS, 128])
        H2 = sb("H2", [128, CHUNKS, 128])
        GX = [sb(f"GX{p}", [128, 128]) for p in range(2)]
        HH = [sb(f"HH{p}", [128, TC + 1, 8, 2]) for p in range(2)]
        EF = [sb(f"EF{p}", [128, 8, 2]) for p in range(2)]
        TH = [sb(f"TH{p}", [128, 8, 2]) for p in range(2)]
        NH = [sb(f"NH{p}", [128, TC, 8]) for p in range(2)]
        TN = [sb(f"TN{p}", [128, TC, 8]) for p in range(2)]
        st = sb("st", [128, 6])
        sm = sb("sm", [128, 16])
        xl = sb("xl", [128, 128])

        wtmp = sb("wtmp", [128, 128])
        ws = sb("ws", [128, 18])
        hb = sb("hb", [128, 2])
        WL = sb("WL", [128, 6, BATCH * HG])
        WKL = W[:, 128 * MATS.index("hk0"):128 * MATS.index("hk0") + 512]
        WVL = W[:, 128 * MATS.index("hv0"):128 * MATS.index("hv0") + 512]
        lnb = {n: sb("ln_" + n, [128, 10]) for n in "abd"}
        VE = [sb(f"VE{p}", [128, LEVELS, HEADS, BATCH, E9]) for p in range(2)]
        VEL = [sb(f"VEL{p}", [128, HEADS, BATCH, E9]) for p in range(4)]
        KL = [sb(f"KL{p}", [128, 128]) for p in range(4)]
        KP = [sb(f"KP{p}", [128, 768]) for p in range(2)]
        KR = [sb(f"KR{p}", [128, 640]) for p in range(2)]
        QL = sb("QL", [128, BATCH, HEADS, TC])
        QG = [sb(f"QG{p}", [128, BATCH, HEADS, TC]) for p in range(2)]
        STt = [sb(f"ST{l}", [128, HEADS, BATCH, E9]) for l in range(LEVELS)]
        DT = [sb(f"DT{p}", [128, HEADS, SV]) for p in range(2)]
        A = [sb(f"A{p}", [128, HEADS, TC]) for p in range(2)]
        SL, SR = sb("SL", [128, 3, HEADS, TC]), sb("SR", [128, 3, HEADS, TC])
        lmx = sb("lmx", [128, HEADS])
        RN, GO = sb("RN", [128, 96]), sb("GO", [128, 96, DH])
        GS, LT, GT, DF, h2s, xts, cd, la, laT, xb, gu, gu2, gt_, sg, ta, m2, mix, x3, ld, ldT = (
            sb(n, [128, 128]) for n in ("GS LT GT DF h2s xts cd la laT xb gu gu2 gt_ sg ta m2 mix x3 ld ldT").split())
        x4 = [sb(f"x4{p}", [128, 128]) for p in range(2)]
        ct = sb("ct", [128, 384])
        XM = sb("XM", [128, 640])
        EX = sb("EX", [128, 768])

        Z = [ps(f"Z{p}") for p in range(2)]
        DL = ps("DL", (128, 2, 512))
        OB = ps("OB", (128, 2, 512))
        FR = [ps(f"FR{p}") for p in range(2)]
        PN, PT = DL[:, 0, :], DL[:, 1, :]
        SC = Z

        ident, ones = c_["ident"], c_["ones"]
        zv = [Z[p][:, 0:256].rearrange("p (t l b) -> p t l b", l=2, b=4) for p in range(2)]
        pnv = PN[:, 0:256].rearrange("p (t l b) -> p t l b", l=2, b=4)

        block = ctx.enter_context(nc.Block())

        def layers(i, j=None):
            return slice(0 if i < CHUNKS else 4, 8 if i >= LAG else 4)

        def turns(eng, body, last=None):
            for i in range(4):
                body(i, i % 2, i)
            with eng.Fori(4, CHUNKS - 3, 2) as i:
                for p in range(2):
                    body(i + p, p, 4)
            for i in range(CHUNKS - 2, TURNS):
                body(i, i % 2, i)

        def weights_vector(v):
            tern = w["tern"]
            v.wait_ge(S("mats"), 16)
            v.scalar_tensor_tensor(out=wtmp[:], in0=tern, scalar=-1.0, in1=tern, op0=ALU.mult, op1=ALU.max).then_inc(S("w1"), 1)
            v.wait_ge(S("w1"), 1)
            v.tensor_reduce(ws[:, 0:1], wtmp[:], AX.X, ALU.add).then_inc(S("w2"), 1)
            for n in ["hk0", "hk1", "hk2", "hk3", "hv0", "hv1", "hv2", "hv3"]:
                blk = w[n].rearrange("p (h e) -> p h e", e=DH)
                v.tensor_tensor(blk, blk, c_["hmask"].rearrange("p (h o) -> p h o", o=1).broadcast_to([128, HEADS, DH]),
                                ALU.mult).then_inc(S("w_blk"), 1)
            v.wait_ge(S("w_tot"), 1)
            v.tensor_scalar(ws[:, 1:2], PT[:, 256:257], 1.0 / (D * D), LN_EPS, ALU.mult, ALU.max).then_inc(S("w3"), 1)
            v.wait_ge(S("w3"), 1)
            v.reciprocal(ws[:, 2:3], ws[:, 1:2]).then_inc(S("w4"), 1)
            v.wait_ge(S("w4"), 1)
            v.tensor_scalar(wtmp[:], tern, ws[:, 2:3], None, ALU.mult).then_inc(S("w5"), 1)
            v.wait_ge(S("w5"), 1)
            v.tensor_scalar(wtmp[:], wtmp[:], ROUND, None, ALU.add).then_inc(S("w5"), 1)
            v.wait_ge(S("w5"), 2)
            v.tensor_scalar(wtmp[:], wtmp[:], ROUND, None, ALU.subtract).then_inc(S("w5"), 1)
            v.wait_ge(S("w5"), 3)
            v.tensor_scalar(wtmp[:], wtmp[:], 1.0, -1.0, ALU.min, ALU.max).then_inc(S("w5"), 1)
            v.wait_ge(S("w5"), 4)
            v.tensor_scalar(tern, wtmp[:], ws[:, 1:2], None, ALU.mult).then_inc(S("w_tern"), 1)
            hs = COLS[:, 4:8]
            v.tensor_reduce(ws[:, 3:4], hs, AX.X, ALU.max).then_inc(S("w6"), 1)
            v.wait_ge(S("w6"), 1)
            v.tensor_scalar(ws[:, 4:8], hs, ws[:, 3:4], None, ALU.subtract).then_inc(S("w6"), 1)
            v.wait_ge(S("w_exp"), 1)
            v.tensor_reduce(ws[:, 12:13], ws[:, 8:12], AX.X, ALU.add).then_inc(S("w6"), 1)
            v.wait_ge(S("w6"), 3)
            v.reciprocal(ws[:, 13:14], ws[:, 12:13]).then_inc(S("w6"), 1)
            v.wait_ge(S("w6"), 4)
            v.tensor_scalar(ws[:, 14:18], ws[:, 8:12], ws[:, 13:14], None, ALU.mult).then_inc(S("w6"), 1)
            v.memset(WL[:], 1.0).then_inc(S("w6"), 1)
            v.wait_ge(S("w6"), 6)
            for l in range(1, LEVELS):
                v.tensor_scalar(WL[:, l, :], WL[:, l, :], ws[:, 13 + l:14 + l], None, ALU.mult).then_inc(S("w7"), 1)
            v.tensor_scalar(hb[:], COLS[:, 2:4], 0.5, None, ALU.mult).then_inc(S("w7"), 1)
            for p in range(2):
                v.memset(VE[p][:], 1.0).then_inc(S("w7"), 1)
            for p in range(4):
                v.memset(VEL[p][:], 1.0).then_inc(S("w7"), 1)
            v.wait_ge(S("w7"), 11)
            for t_ in [VE[p][:, l] for p in range(2) for l in range(LEVELS)] + [VEL[p][:] for p in range(4)]:
                v.tensor_tensor(t_, t_, c_["bmask"].rearrange("p (o b q) -> p o b q", o=1, q=1).broadcast_to(
                    [128, HEADS, BATCH, E9]), ALU.mult).then_inc(S("w8"), 1)

        def weights_tensor(pe):
            pe.wait_ge(S("w2"), 1)
            nc.tensor.matmul(PT[:, 256:257], ones, ws[:, 0:1], start=True, stop=True).then_inc(S("w_tot"), 1)
            pe.wait_ge(S("w_blk"), 8)
            for n in range(4):
                nc.tensor.matmul(FR[0][:, 128 * n:128 * n + 128], w["wk"], w[f"hk{n}"], start=True, stop=True)
            for n in range(4):
                mm = nc.tensor.matmul(FR[1][:, 128 * n:128 * n + 128], w["wv"], w[f"hv{n}"], start=True, stop=True)
            mm.then_inc(S("w_lev"), 1)

        def weights_scalar(act):
            act.wait_ge(S("w6"), 2)
            nc.scalar.activation(ws[:, 8:12], ws[:, 4:8], ACT.Exp).then_inc(S("w_exp"), 1)
            act.wait_ge(S("w_lev"), 1)
            nc.scalar.copy(WKL, FR[0][:]).then_inc(S("w_kvl"), 1)
            nc.scalar.copy(WVL, FR[1][:]).then_inc(S("w_kvl"), 1)

        def wk_of(l):
            return w["kT"] if l == 0 else WKL[:, 128 * l - 128:128 * l]

        def wv_of(l):
            return w["vT"] if l == 0 else WVL[:, 128 * l - 128:128 * l]

        def ln_vector_1(v, c, tag, src):
            q = lnb[tag]
            v.bn_stats(q[:, 0:6], src).then_inc(S(tag + "_st"), 1)
            v.wait_ge(S(tag + "_st"), c + 1)
            v.sem_inc(S("alone"), 1)
            v.bn_aggr(q[:, 6:8], q[:, 0:6]).then_inc(S(tag + "_ag"), 1)
            v.wait_ge(S(tag + "_ag"), c + 1)
            v.tensor_scalar(q[:, 8:9], q[:, 7:8], LN_EPS, None, ALU.add).then_inc(S(tag + "_ve"), 1)

        def ln_pool(g, c, tag):
            q = lnb[tag]
            g.wait_ge(S(tag + "_ve"), c + 1)
            g.tensor_tensor(q[:, 9:10], q[:, 8:9], c_["neghalf"][:, 0:1], ALU.pow).then_inc(S(tag + "_rs"), 1)

        def ln_vector_2(v, c, tag, src, dst):
            q = lnb[tag]
            v.wait_ge(S(tag + "_rs"), c + 1)
            v.tensor_scalar(dst, src, q[:, 6:7], q[:, 9:10], ALU.subtract, ALU.mult).then_inc(S(tag + "_ln"), 1)

        def front_pool(g, c):
            g.wait_ge(S("h2"), c + 1)
            g.wait_ge(S("cell_mm"), c)
            g.tensor_copy(h2s[:], H2[:, c, :])
            g.tensor_copy(xts[:], XNT[:, c, :]).then_inc(S("f_in"), 1)

        def cell_tensor(pe, c):
            pe.wait_ge(S("f_in"), c + 1)
            pe.wait_ge(S("dd_out"), c)
            nc.tensor.transpose(FR[1][:, 256:384], xts[:], ident)
            nc.tensor.matmul(FR[1][:, 0:128], h2s[:], w["gi"], start=True, stop=True)
            nc.tensor.matmul(FR[1][:, 128:256], ones[0:1, :], ROWS[0:1, 128:256], start=True, stop=False)
            nc.tensor.matmul(FR[1][:, 128:256], h2s[:], w["gf"], start=False, stop=False)
            nc.tensor.matmul(FR[1][:, 128:256], xts[:], w["gh"], start=False, stop=True).then_inc(S("cell_mm"), 1)

        def cell_scalar(act, c):
            act.wait_ge(S("cell_mm"), c + 1)
            act.wait_ge(S("x1"), c)
            nc.scalar.activation(ct[:, 0:128], FR[1][:, 0:128], ACT.Tanh).then_inc(S("ct1"), 1)
            nc.scalar.activation(ct[:, 256:384], FR[1][:, 128:256], ACT.Tanh, scale=0.5).then_inc(S("ct2"), 1)
            act.wait_ge(S("ct1"), c + 1)
            nc.scalar.activation(ct[:, 128:256], ct[:, 0:128], ACT.Tanh).then_inc(S("ct3"), 1)

        def cell_vector(v, c):
            v.wait_ge(S("ct3"), c + 1)
            v.wait_ge(S("ct2"), c + 1)
            v.tensor_tensor(cd[:], ct[:, 128:256], FR[1][:, 256:384], ALU.subtract).then_inc(S("cd1"), 1)
            v.wait_ge(S("cd1"), c + 1)
            v.scalar_tensor_tensor(out=cd[:], in0=ct[:, 256:384], scalar=1.0, in1=cd[:], op0=ALU.add,
                                   op1=ALU.mult).then_inc(S("cd2"), 1)
            v.wait_ge(S("cd2"), c + 1)
            v.scalar_tensor_tensor(out=X[:, c, :], in0=cd[:], scalar=0.5, in1=X[:, c, :], op0=ALU.mult,
                                   op1=ALU.add).then_inc(S("x1"), 1)
            v.wait_ge(S("v_init"), 2)
            v.wait_ge(S("x1"), c + 1)
            ln_vector_1(v, c, "a", X[:, c, :])

        def cell_vector_2(v, c):
            v.wait_ge(S("t1"), c)
            ln_vector_2(v, c, "a", X[:, c, :], la[:])

        def t1_tensor(pe, c):
            pe.wait_ge(S("a_ln"), c + 1)
            pe.wait_ge(S("ta"), c - 1 if not isinstance(c, int) or c >= 1 else 0)
            nc.tensor.transpose(FR[0][:, 256:384], la[:], ident).then_inc(S("t1"), 1)

        def t1_scalar(act, c):
            act.wait_ge(S("t1"), c + 1)
            nc.scalar.copy(laT[:], FR[0][:, 256:384]).then_inc(S("t1_out"), 1)

        def y1_tensor(pe, c):
            pe.wait_ge(S("t1_out"), c + 1)
            nc.tensor.matmul(FR[0][:, 384:512], laT[:], w["tern"], start=True, stop=True).then_inc(S("y1"), 1)

        def x2_vector(v, c):
            v.wait_ge(S("y1"), c + 1)
            v.tensor_tensor(X[:, c, :], X[:, c, :], FR[0][:, 384:512], ALU.add).then_inc(S("x2"), 1)
            v.wait_ge(S("v_init"), 2)
            v.wait_ge(S("x2"), c + 1)
            ln_vector_1(v, c, "b", X[:, c, :])

        def x2_vector_2(v, c):
            v.wait_ge(S("xm"), c)
            ln_vector_2(v, c, "b", X[:, c, :], xb[:])

        def xm_tensor(pe, c):
            pe.wait_ge(S("b_ln"), c + 1)
            pe.wait_ge(S("x2"), c + 1)
            if not isinstance(c, int) or c >= 2:
                pe.wait_ge(S("x4"), c - 1)
            nc.tensor.matmul(FR[0][:], xb[:], c_["means"][:, 0:512], start=True, stop=True)
            nc.tensor.matmul(FR[1][:, 128:256], xb[:], c_["means"][:, 512:640], start=True, stop=True).then_inc(S("xm"), 1)

        def xm_scalar(act, c):
            act.wait_ge(S("xm"), c + 1)
            act.wait_ge(S("kr4"), c)
            nc.scalar.copy(XM[:, 0:512], FR[0][:]).then_inc(S("xm1"), 1)
            nc.scalar.copy(XM[:, 512:640], FR[1][:, 128:256]).then_inc(S("xm2"), 1)

        def xl_(l):
            return XM[:, 128 * l:128 * l + 128]

        def ab_tensor(pe, c):
            pe.wait_ge(S("xm1"), c + 1)
            mm = [(w["qT"], 0)] + [(wk_of(l), l) for l in range(3)]
            for n, (wt, l) in enumerate(mm):
                m = nc.tensor.matmul(FR[0][:, 128 * n:128 * n + 128], wt, xl_(l), start=True, stop=True)
            m.then_inc(S("pa"), 1)
            pe.wait_ge(S("xm2"), c + 1)
            for n, (wt, l) in enumerate([(wk_of(3), 3), (wk_of(4), 4), (w["klT"], 0)]):
                nc.tensor.matmul(FR[1][:, 128 * n:128 * n + 128], wt, xl_(l), start=True, stop=True)
            nc.tensor.matmul(FR[1][:, 384:512], xl_(0), w["vlT"], start=True, stop=True).then_inc(S("pb"), 1)

        def expand_values(act, src, dst, semname):
            for b in range(BATCH):
                a = nc.scalar.activation(dst[:, :, b, 0:DH], src.rearrange("p (h e) -> p h e", e=DH), ACT.Copy,
                                         scale=c_["bmask"][:, b:b + 1])
            return a

        def ab_scalar(act, c, k):
            p = k % 2
            act.wait_ge(S("pa"), c + 1)
            if not isinstance(c, int) or c >= 1:
                act.wait_ge(S("am"), 5 * c - 4)
            qsrc = FR[0][:, 0:128].rearrange("p (b t) -> p b t", b=BATCH)
            for h in range(HEADS):
                a = nc.scalar.activation(QL[:, :, h, :], qsrc, ACT.Copy, scale=c_["hmask"][:, h:h + 1])
            a.then_inc(S("ql"), 1)
            act.wait_ge(S("mna"), c + 1)
            nc.scalar.activation(EX[:, 0:512], EX[:, 0:512], ACT.Exp).then_inc(S("ea"), 1)
            act.wait_ge(S("mnb"), c + 1)
            nc.scalar.activation(EX[:, 512:768], EX[:, 512:768], ACT.Exp).then_inc(S("eb"), 1)
            nc.scalar.copy(KL[k][:], FR[1][:, 256:384]).then_inc(S("kl"), 1)
            expand_values(act, FR[1][:, 384:512], VEL[k], None).then_inc(S("vl"), 1)

        def phi_vector(v, c, k):
            p = k % 2
            v.wait_ge(S("pa"), c + 1)
            v.wait_ge(S("ql"), c + 1)
            v.tensor_scalar(EX[:, 0:512], FR[0][:], 0.0, None, ALU.min).then_inc(S("mna"), 1)
            v.wait_ge(S("pb"), c + 1)
            v.tensor_scalar(EX[:, 512:768], FR[1][:, 0:256], 0.0, None, ALU.min).then_inc(S("mnb"), 1)
            v.wait_ge(S("ea"), c + 1)
            v.scalar_tensor_tensor(out=KP[p][:, 0:512], in0=FR[0][:], scalar=0.0, in1=EX[:, 0:512], op0=ALU.max,
                                   op1=ALU.add).then_inc(S("phi_a"), 1)
            v.wait_ge(S("eb"), c + 1)
            v.wait_ge(S("vl"), c + 1)
            v.scalar_tensor_tensor(out=KP[p][:, 512:768], in0=FR[1][:, 0:256], scalar=0.0, in1=EX[:, 512:768],
                                   op0=ALU.max, op1=ALU.add).then_inc(S("phi_b"), 1)

        def qe_pool(g, c, k):
            p = k % 2
            g.wait_ge(S("phi_a"), c + 1)
            for b in range(BATCH):
                src = KP[p][:, TC * b:TC * b + TC].rearrange("p (o t) -> p o t", o=1).broadcast_to([128, HEADS, TC])
                a = g.tensor_tensor(QG[p][:, b, :, :], src,
                                    c_["hmask"].rearrange("p (h o) -> p h o", o=1).broadcast_to([128, HEADS, TC]), ALU.mult)
            a.then_inc(S("qg"), 1)

        def cd_tensor(pe, c, k):
            p = k % 2
            pe.wait_ge(S("phi_a"), c + 1)
            for l in range(4):
                m = nc.tensor.matmul(FR[0][:, 128 * l:128 * l + 128], xl_(l), wv_of(l), start=True, stop=True)
            m.then_inc(S("pc"), 1)
            pe.wait_ge(S("phi_b"), c + 1)
            nc.tensor.matmul(FR[1][:, 0:128], xl_(4), wv_of(4), start=True, stop=True)
            for l in range(3):
                m = nc.tensor.transpose(FR[1][:, 128 * l + 128:128 * l + 256], KP[p][:, 128 * l + 128:128 * l + 256], ident)
            m.then_inc(S("pd"), 1)
            pe.wait_ge(S("ve3"), c + 1)
            for l in range(3, 5):
                m = nc.tensor.transpose(FR[0][:, 128 * l - 384:128 * l - 256], KP[p][:, 128 * l + 128:128 * l + 256], ident)
            nc.tensor.matmul(FR[0][:, 256:384], w["g1T"], xl_(0), start=True, stop=True).then_inc(S("kr4"), 1)

        def cd_scalar(act, c, k):
            p = k % 2
            act.wait_ge(S("pc"), c + 1)
            for l in range(4):
                a = expand_values(act, FR[0][:, 128 * l:128 * l + 128], VE[p][:, l], None)
            a.then_inc(S("ve3"), 1)
            act.wait_ge(S("pd"), c + 1)
            expand_values(act, FR[1][:, 0:128], VE[p][:, 4], None)
            nc.scalar.copy(KR[p][:, 0:384], FR[1][:, 128:512]).then_inc(S("dd_out"), 1)
            act.wait_ge(S("kr4"), c + 1)
            nc.scalar.copy(KR[p][:, 384:640], FR[0][:, 0:256])
            nc.scalar.copy(GX[p][:], FR[0][:, 256:384]).then_inc(S("kr_out"), 1)

        def blocks_of(cc):
            return min(cc, 2) + 1

        def loc_base(c, cc):
            return 3 * c - 3 if cc >= 2 else cc

        def sc_local(pe, c, cc, k, r):
            p = k % 2
            if r == 0:
                pe.wait_ge(S("ql"), c + 1)
                pe.wait_ge(S("kl"), c + 1)
            if r < 2 and cc >= 1:
                pe.wait_ge(S("am"), 5 * c - 1 + r)
            if r == 2:
                pe.wait_ge(S("le"), loc_base(c, cc) + 1)
            for b in range(BATCH):
                m = nc.tensor.matmul(SC[r % 2][TC * b:TC * b + TC, :], KL[(k - r) % 4][:, TC * b:TC * b + TC],
                                     QL[:, b, :, :].rearrange("p h t -> p (h t)"), start=True, stop=True)
            m.then_inc(S("scl"), 1)

        def sc_level(pe, c, cc, k, l):
            p = k % 2
            if l == 0:
                pe.wait_ge(S("qg"), c + 1)
                pe.wait_ge(S("phi_b"), c + 1)
            if l < 2:
                pe.wait_ge(S("le"), loc_base(c, cc) + min(blocks_of(cc), l + 2))
            else:
                pe.wait_ge(S("am"), 5 * c + l - 1)
            for b in range(BATCH):
                m = nc.tensor.matmul(SC[(l + 1) % 2][TC * b:TC * b + TC, :],
                                     KP[p][:, 128 * l + 128 + TC * b:128 * l + 128 + TC * b + TC],
                                     QG[p][:, b, :, :].rearrange("p h t -> p (h t)"), start=True, stop=True)
            m.then_inc(S("scg"), 1)

        def local_evac(v, c, cc, r):
            v.wait_ge(S("scl"), loc_base(c, cc) + r + 1)
            if r == 0:
                v.wait_ge(S("avl"), c)
            v.scalar_tensor_tensor(out=SL[:, r], in0=SC[r % 2][:].rearrange("p (h t) -> p h t", t=TC), scalar=DH ** -0.5,
                                   in1=c_["addmask"][:, TC * r:TC * r + TC].rearrange("p (o t) -> p o t", o=1)
                                   .broadcast_to([128, HEADS, TC]), op0=ALU.mult, op1=ALU.add).then_inc(S("le"), 1)

        def local_soft_1(v, c, cc):
            R = blocks_of(cc)
            flat = lambda a: a[:, 0:R].rearrange("p r h t -> p (r h t)")
            v.wait_ge(S("le"), loc_base(c, cc) + R)
            v.transpose(flat(SR), flat(SL)).then_inc(S("lt"), 1)
            v.wait_ge(S("lt"), c + 1)
            v.tensor_reduce(lmx[:], SR[:, 0:R].rearrange("p r h t -> p h r t"), AX.XY, ALU.max).then_inc(S("lm"), 1)
            v.wait_ge(S("lm"), c + 1)
            v.tensor_tensor(SR[:, 0:R], SR[:, 0:R], lmx[:].rearrange("p (o h q) -> p o h q", o=1, q=1).broadcast_to(
                [128, R, HEADS, TC]), ALU.subtract).then_inc(S("ls"), 1)

        def local_exp(act, c, cc):
            R = blocks_of(cc)
            flat = lambda a: a[:, 0:R].rearrange("p r h t -> p (r h t)")
            act.wait_ge(S("ls"), c + 1)
            nc.scalar.activation(flat(SR), flat(SR), ACT.Exp).then_inc(S("lx"), 1)

        def local_soft_2(v, c, cc):
            R = blocks_of(cc)
            flat = lambda a: a[:, 0:R].rearrange("p r h t -> p (r h t)")
            v.wait_ge(S("lx"), c + 1)
            v.transpose(flat(SL), flat(SR)).then_inc(S("pl"), 1)

        def mask_level(v, c, cc, l):
            v.wait_ge(S("scg"), 5 * c + l + 1)
            if cc >= 1 or l >= 2:
                v.wait_ge(S("av"), 5 * c + l - 1)
            v.tensor_tensor(A[l % 2][:], SC[(l + 1) % 2][:].rearrange("p (h t) -> p h t", t=TC),
                            c_["causal"].rearrange("p (o t) -> p o t", o=1).broadcast_to([128, HEADS, TC]),
                            ALU.mult).then_inc(S("am"), 1)

        def out_of(n):
            return OB[:, n // 3, OW * (n % 3):OW * (n % 3) + OW].rearrange("p (b g e) -> p b g e", b=BATCH, e=E9)

        def av_level(pe, c, cc, k, l):
            p = k % 2
            o = out_of(l)
            first = l % 3 == 0
            if l == 0:
                pe.wait_ge(S("go"), c)
            if cc >= 1:
                pe.wait_ge(S("st"), 5 * c + l - 4)
                for b in range(BATCH):
                    for i in range(HG):
                        nc.tensor.matmul(o[TC * i:TC * i + TC, b, :, :], KP[p][:, TC * b:TC * b + TC],
                                         STt[l][:, HG * i:HG * i + HG, b, :],
                                         start=first and b == 0, stop=False, skip_group_check=True)
            pe.wait_ge(S("am"), 5 * c + l + 1)
            pe.wait_ge(S("ve3") if l < 4 else S("dd_out"), c + 1)
            for g in range(HG):
                for i in range(HG):
                    m = nc.tensor.matmul(o[TC * i:TC * i + TC, :, g, :], A[l % 2][:, HG * i + g, :],
                                         VE[p][:, l, HG * i + g, :, :],
                                         start=first and cc == 0 and g == 0, stop=True, skip_group_check=True)
            m.then_inc(S("av"), 1)

        def av_local(pe, c, cc, k):
            o = out_of(LEVELS)
            pe.wait_ge(S("pl"), c + 1)
            pe.wait_ge(S("vl"), c + 1)
            for r in range(blocks_of(cc)):
                for g in range(HG):
                    for i in range(HG):
                        m = nc.tensor.matmul(o[TC * i:TC * i + TC, :, g, :], SL[:, r, HG * i + g, :],
                                             VEL[(k - r) % 4][:, HG * i + g, :, :], start=False, stop=True,
                                             skip_group_check=True)
            m.then_inc(S("avl"), 1)

        def dl_level(pe, c, cc, k, l):
            p = k % 2
            pe.wait_ge(S("dt"), 5 * c + l)
            pe.wait_ge(S("kr_out"), c + 1)
            v_ = VE[p][:, l].rearrange("p h b e -> p (h b e)")
            for n in range(2):
                m = nc.tensor.matmul(DL[:, n, 0:HALF], KR[p][:, 128 * l:128 * l + 128], v_[:, HALF * n:HALF * n + HALF],
                                     start=True, stop=True)
            m.then_inc(S("dl"), 1)

        def dt_level(v, c, cc, l):
            v.wait_ge(S("dl"), 5 * c + l + 1)
            if cc >= 1 or l >= 2:
                v.wait_ge(S("st"), 5 * c + l - 1)
            v.tensor_tensor(DT[l % 2][:].rearrange("p (n h) q -> p n h q", n=2),
                            DL[:, :, 0:HALF].rearrange("p n (h q) -> p n h q", q=SV),
                            c_["hmask"].rearrange("p (n h o) -> p n h o", n=2, o=1).broadcast_to([128, 2, HEADS // 2, SV]),
                            ALU.mult).then_inc(S("dt"), 1)

        def st_level(g, c, cc, l):
            g.wait_ge(S("dt"), 5 * c + l + 1)
            flat = STt[l][:].rearrange("p h b e -> p (h b e)")
            src = DT[l % 2][:].rearrange("p h q -> p (h q)")
            if cc == 0:
                g.tensor_copy(flat, src).then_inc(S("st"), 1)
            else:
                g.tensor_tensor(flat, flat, src, ALU.add).then_inc(S("st"), 1)

        def norm_out(v, c, cc):
            ob = OB[:, :, 0:3 * OW].rearrange("p n (m e) -> p n m e", e=E9)
            v.wait_ge(S("av"), 5 * c + 5)
            v.wait_ge(S("avl"), c + 1)
            rn2 = RN[:].rearrange("p (n m) -> p n m", n=2)
            v.tensor_scalar(rn2, ob[:, :, :, DH], 1.0e-6, None, ALU.max).then_inc(S("r1"), 1)
            v.wait_ge(S("r1"), c + 1)
            v.reciprocal(RN[:], RN[:]).then_inc(S("r2"), 1)
            v.wait_ge(S("r2"), c + 1)
            v.tensor_tensor(RN[:], RN[:], WL[:].rearrange("p l m -> p (l m)"), ALU.mult).then_inc(S("r3"), 1)
            v.wait_ge(S("r3"), c + 1)
            v.tensor_tensor(GO[:].rearrange("p (n m) e -> p n m e", n=2), ob[:, :, :, 0:DH],
                            RN[:].rearrange("p (n m o) -> p n m o", n=2, o=1).broadcast_to([128, 2, 3 * BATCH * HG, DH]),
                            ALU.mult).then_inc(S("go"), 1)
            v.wait_ge(S("go"), c + 1)
            gof = GO[:].rearrange("p (l m) e -> p l (m e)", l=6)
            v.tensor_reduce(GS[:], gof[:, 0:LEVELS, :].rearrange("p l q -> p q l"), AX.X, ALU.add).then_inc(S("gs"), 1)
            v.transpose(LT[:], gof[:, LEVELS, :]).then_inc(S("ltr"), 1)
            v.wait_ge(S("gs"), c + 1)
            v.transpose(GT[:], GS[:]).then_inc(S("gtr"), 1)
            v.wait_ge(S("gtr"), c + 1)
            v.wait_ge(S("ltr"), c + 1)
            v.tensor_tensor(DF[:], LT[:], GT[:], ALU.subtract).then_inc(S("df"), 1)

        def gate_tensor(pe, c):
            pe.wait_ge(S("df"), c + 1)
            pe.wait_ge(S("kr_out"), c + 2 if not (isinstance(c, int) and c == CHUNKS - 1) else c + 1)
            nc.tensor.matmul(FR[0][:, 0:128], w["g2T"], DF[:], start=True, stop=True).then_inc(S("gh"), 1)

        def gate_vector(v, c, p):
            v.wait_ge(S("gh"), c + 1)
            v.tensor_tensor(gu[:], FR[0][:, 0:128], GX[p][:], ALU.add).then_inc(S("gu"), 1)

        def gate_scalar(act, c):
            act.wait_ge(S("gu"), c + 1)
            act.wait_ge(S("sg"), c)
            nc.scalar.activation(gt_[:], gu[:], ACT.Tanh, scale=0.5, bias=hb[:, 0:1]).then_inc(S("gth"), 1)

        def gate_vector_2(v, c):
            v.wait_ge(S("gu"), c + 1)
            v.tensor_scalar(gu2[:], gu[:], COLS[:, 2:3], None, ALU.add).then_inc(S("gu2"), 1)
            v.wait_ge(S("gu2"), c + 1)
            v.wait_ge(S("gth"), c + 1)
            v.wait_ge(S("al"), c)
            v.scalar_tensor_tensor(out=sg[:], in0=gt_[:], scalar=1.0, in1=gu2[:], op0=ALU.add,
                                   op1=ALU.mult).then_inc(S("sg"), 1)

        def alpha_tensor(pe, c):
            pe.wait_ge(S("sg"), c + 1)
            nc.tensor.matmul(FR[0][:, 128:256], w["go"], sg[:], start=True, stop=True).then_inc(S("al"), 1)

        def alpha_scalar(act, c):
            act.wait_ge(S("al"), c + 1)
            act.wait_ge(S("m2"), c)
            nc.scalar.activation(ta[:], FR[0][:, 128:256], ACT.Tanh, scale=0.25, bias=hb[:, 1:2]).then_inc(S("ta"), 1)

        def mix_vector(v, c):
            v.wait_ge(S("ta"), c + 1)
            v.scalar_tensor_tensor(out=m2[:], in0=ta[:], scalar=1.0, in1=DF[:], op0=ALU.add, op1=ALU.mult).then_inc(S("m2"), 1)
            v.wait_ge(S("m2"), c + 1)
            v.scalar_tensor_tensor(out=mix[:], in0=m2[:], scalar=0.5, in1=GT[:], op0=ALU.mult, op1=ALU.add)\
                .then_inc(S("mix"), 1)

        def proj_tensor(pe, c):
            pe.wait_ge(S("mix"), c + 1)
            if isinstance(c, int) and c == CHUNKS - 1:
                pe.wait_ge(S("cd1"), c + 1)
            else:
                pe.wait_ge(S("cd1"), c + 2)
            nc.tensor.matmul(FR[1][:, 256:384], ones[0:1, :], ROWS[0:1, 256:384], start=True, stop=False)
            nc.tensor.matmul(FR[1][:, 256:384], mix[:], w["oT"], start=False, stop=True).then_inc(S("po"), 1)

        def x3_vector(v, c):
            v.wait_ge(S("po"), c + 1)
            v.tensor_tensor(x3[:], FR[1][:, 256:384], X[:, c, :], ALU.add).then_inc(S("x3"), 1)
            v.wait_ge(S("x3"), c + 1)
            ln_vector_1(v, c, "d", x3[:])

        def x3_vector_2(v, c):
            ln_vector_2(v, c, "d", x3[:], ld[:])

        def t2_tensor(pe, c):
            pe.wait_ge(S("d_ln"), c + 1)
            nc.tensor.transpose(FR[1][:, 384:512], ld[:], ident).then_inc(S("t2"), 1)

        def t2_scalar(act, c):
            act.wait_ge(S("t2"), c + 1)
            nc.scalar.copy(ldT[:], FR[1][:, 384:512]).then_inc(S("t2_out"), 1)

        def y2_tensor(pe, c):
            pe.wait_ge(S("t2_out"), c + 1)
            nc.tensor.matmul(FR[1][:, 0:128], ldT[:], w["tern"], start=True, stop=True).then_inc(S("y2"), 1)

        def x4_vector(v, c, cc, k):
            v.wait_ge(S("y2"), c + 1)
            if cc >= 2:
                v.wait_ge(S(f"out{k % 2}"), 32 * (c - k % 2))
            v.tensor_tensor(x4[k % 2][:], FR[1][:, 0:128], x3[:], ALU.add).then_inc(S("x4"), 1)

        def store(sp, c, k):
            sp.wait_ge(S("x4"), c + 1)
            for b in range(BATCH):
                sp.dma_start(out[b].rearrange("(c t) d -> t c d", t=TC)[:, c, :], x4[k % 2][TC * b:TC * b + TC, :])\
                    .then_inc(S(f"out{k % 2}"), 16)

        def chunks(eng, body):
            for c in range(3):
                body(c, c % 4, c)
            with eng.Fori(3, CHUNKS - 4, 4) as c:
                for n in range(4):
                    body(c + n, (3 + n) % 4, 3)
            body(CHUNKS - 1, (CHUNKS - 1) % 4, CHUNKS - 1)

        def finish_sync(sp):
            chunks(sp, lambda c, k, cc: store(sp, c, k))
            for p in range(2):
                sp.wait_ge(S(f"out{p}"), 32 * CHUNKS)

        def finish_tensor(pe):
            cell_tensor(pe, 0)
            t1_tensor(pe, 0)
            y1_tensor(pe, 0)
            xm_tensor(pe, 0)
            ab_tensor(pe, 0)
            cd_tensor(pe, 0, 0)

            def body(c, k, cc):
                R, tail, more = blocks_of(cc), cc >= 1, cc < CHUNKS - 1
                for r in range(min(R, 2)):
                    sc_local(pe, c, cc, k, r)
                if tail:
                    gate_tensor(pe, c - 1)
                if R > 2:
                    sc_local(pe, c, cc, k, 2)
                if more:
                    cell_tensor(pe, c + 1)
                sc_level(pe, c, cc, k, 0)
                if tail:
                    alpha_tensor(pe, c - 1)
                sc_level(pe, c, cc, k, 1)
                av_level(pe, c, cc, k, 0)
                dl_level(pe, c, cc, k, 0)
                if tail:
                    proj_tensor(pe, c - 1)
                if more:
                    t1_tensor(pe, c + 1)
                sc_level(pe, c, cc, k, 2)
                av_level(pe, c, cc, k, 1)
                dl_level(pe, c, cc, k, 1)
                if tail:
                    t2_tensor(pe, c - 1)
                if more:
                    y1_tensor(pe, c + 1)
                sc_level(pe, c, cc, k, 3)
                av_level(pe, c, cc, k, 2)
                dl_level(pe, c, cc, k, 2)
                if tail:
                    y2_tensor(pe, c - 1)
                sc_level(pe, c, cc, k, 4)
                av_level(pe, c, cc, k, 3)
                dl_level(pe, c, cc, k, 3)
                if more:
                    xm_tensor(pe, c + 1)
                av_level(pe, c, cc, k, 4)
                dl_level(pe, c, cc, k, 4)
                if more:
                    ab_tensor(pe, c + 1)
                av_local(pe, c, cc, k)
                if more:
                    cd_tensor(pe, c + 1, (k + 1) % 4)
            chunks(pe, body)
            c = CHUNKS - 1
            gate_tensor(pe, c)
            alpha_tensor(pe, c)
            proj_tensor(pe, c)
            t2_tensor(pe, c)
            y2_tensor(pe, c)

        def finish_scalar(act):
            cell_scalar(act, 0)
            t1_scalar(act, 0)
            xm_scalar(act, 0)
            ab_scalar(act, 0, 0)
            cd_scalar(act, 0, 0)

            def body(c, k, cc):
                tail, more = cc >= 1, cc < CHUNKS - 1
                if tail:
                    gate_scalar(act, c - 1)
                if more:
                    cell_scalar(act, c + 1)
                if tail:
                    alpha_scalar(act, c - 1)
                local_exp(act, c, cc)
                if more:
                    t1_scalar(act, c + 1)
                if tail:
                    t2_scalar(act, c - 1)
                if more:
                    xm_scalar(act, c + 1)
                    ab_scalar(act, c + 1, (k + 1) % 4)
                    cd_scalar(act, c + 1, (k + 1) % 4)
            chunks(act, body)
            c = CHUNKS - 1
            gate_scalar(act, c)
            alpha_scalar(act, c)
            t2_scalar(act, c)

        def finish_vector(v):
            cell_vector(v, 0)
            cell_vector_2(v, 0)
            x2_vector(v, 0)
            x2_vector_2(v, 0)
            phi_vector(v, 0, 0)

            def body(c, k, cc):
                R, tail, more = blocks_of(cc), cc >= 1, cc < CHUNKS - 1
                for r in range(min(R, 2)):
                    local_evac(v, c, cc, r)
                if tail:
                    gate_vector(v, c - 1, (k - 1) % 2)
                if R > 2:
                    local_evac(v, c, cc, 2)
                if tail:
                    gate_vector_2(v, c - 1)
                if more:
                    cell_vector(v, c + 1)
                local_soft_1(v, c, cc)
                mask_level(v, c, cc, 0)
                if tail:
                    mix_vector(v, c - 1)
                if more:
                    cell_vector_2(v, c + 1)
                mask_level(v, c, cc, 1)
                dt_level(v, c, cc, 0)
                if tail:
                    x3_vector(v, c - 1)
                mask_level(v, c, cc, 2)
                dt_level(v, c, cc, 1)
                if tail:
                    x3_vector_2(v, c - 1)
                if more:
                    x2_vector(v, c + 1)
                mask_level(v, c, cc, 3)
                dt_level(v, c, cc, 2)
                if more:
                    x2_vector_2(v, c + 1)
                if tail:
                    x4_vector(v, c - 1, cc - 1, (k - 1) % 4)
                mask_level(v, c, cc, 4)
                dt_level(v, c, cc, 3)
                local_soft_2(v, c, cc)
                dt_level(v, c, cc, 4)
                if more:
                    phi_vector(v, c + 1, (k + 1) % 4)
                norm_out(v, c, cc)
            chunks(v, body)
            c, k = CHUNKS - 1, (CHUNKS - 1) % 4
            gate_vector(v, c, k % 2)
            gate_vector_2(v, c)
            mix_vector(v, c)
            x3_vector(v, c)
            x3_vector_2(v, c)
            x4_vector(v, c, 2, k)

        def finish_pool(g):
            front_pool(g, 0)
            ln_pool(g, 0, "a")
            ln_pool(g, 0, "b")
            qe_pool(g, 0, 0)

            def body(c, k, cc):
                tail, more = cc >= 1, cc < CHUNKS - 1
                if more:
                    front_pool(g, c + 1)
                    ln_pool(g, c + 1, "a")
                st_level(g, c, cc, 0)
                if tail:
                    ln_pool(g, c - 1, "d")
                st_level(g, c, cc, 1)
                if more:
                    ln_pool(g, c + 1, "b")
                for l in range(2, LEVELS):
                    st_level(g, c, cc, l)
                if more:
                    qe_pool(g, c + 1, (k + 1) % 4)
            chunks(g, body)
            ln_pool(g, CHUNKS - 1, "d")

        @block.sync
        def _(sp):
            sp.dma_start(C[:], ins["consts"]).then_inc(S("consts"), 16)
            for b in range(BATCH):
                sp.dma_start(X[TC * b:TC * b + TC, :, :],
                             ins["x"][b].rearrange("(c t) d -> t c d", t=TC)).then_inc(S("x_in"), 16)
            sp.dma_start(G1[:], ins["gamma_rows"]).then_inc(S("consts"), 16)
            sp.dma_start(COLS[:], ins["cols"]).then_inc(S("consts"), 16)
            sp.dma_start(ROWS[:], ins["rows"]).then_inc(S("consts"), 16)
            sp.dma_start(W[:], ins["mats"]).then_inc(S("mats"), 16)
            finish_sync(sp)

        def norm_vector_1(v, c):
            v.bn_stats(st[:], X[:, c, :]).then_inc(S("n_st"), 1)
            v.wait_ge(S("n_st"), c + 1)
            v.sem_inc(S("alone"), 1)
            v.bn_aggr(sm[:, 0:2], st[:]).then_inc(S("n_ag"), 1)
            v.wait_ge(S("n_ag"), c + 1)
            v.tensor_scalar(sm[:, 2:3], sm[:, 1:2], LN_EPS, None, ALU.add).then_inc(S("n_ve"), 1)

        def norm_pool_1(g, c):
            g.wait_ge(S("n_ve"), c + 1)
            g.tensor_tensor(sm[:, 3:4], sm[:, 2:3], c_["neghalf"][:, 0:1], ALU.pow).then_inc(S("n_rs"), 1)

        def norm_vector_2(v, c):
            v.wait_ge(S("n_rs"), c + 1)
            v.tensor_scalar(xl[:], X[:, c, :], sm[:, 0:1], sm[:, 3:4], ALU.subtract, ALU.mult).then_inc(S("n_xl"), 1)
            v.scalar_tensor_tensor(out=sm[:, 4:5], in0=sm[:, 1:2], scalar=sm[:, 3:4], in1=sm[:, 3:4],
                                   op0=ALU.mult, op1=ALU.mult).then_inc(S("n_v2"), 1)
            v.wait_ge(S("n_v2"), c + 1)
            v.tensor_scalar(sm[:, 5:6], sm[:, 4:5], NORM_FLOOR, None, ALU.max).then_inc(S("n_mx"), 1)

        def norm_pool_2(g, c):
            g.wait_ge(S("n_mx"), c + 1)
            g.tensor_tensor(sm[:, 6:7], sm[:, 5:6], c_["neghalf"][:, 0:1], ALU.pow).then_inc(S("n_rn"), 1)

        def norm_vector_3(v, c):
            v.wait_ge(S("n_rn"), c + 1)
            v.wait_ge(S("n_xl"), c + 1)
            v.wait_ge(S("n_t"), c)
            v.scalar_tensor_tensor(out=xn[:], in0=xl[:], scalar=sm[:, 6:7], in1=G1[:],
                                   op0=ALU.mult, op1=ALU.mult).then_inc(S("n_xn"), 1)
            v.tensor_tensor(X[:, c, :], X[:, c, :], xl[:], ALU.add).then_inc(S("n_r1"), 1)
            v.wait_ge(S("n_xn"), c + 1)
            v.wait_ge(S("n_r1"), c + 1)
            v.tensor_tensor(X[:, c, :], X[:, c, :], xn[:], ALU.add).then_inc(S("n_r2"), 1)

        def norm_tensor(pe, c):
            pe.wait_ge(S("n_xn"), c + 1)
            nc.tensor.transpose(PT[:, 0:128], xn[:], ident).then_inc(S("n_t"), 1)

        def norm_scalar(act, c):
            act.wait_ge(S("n_t"), c + 1)
            nc.scalar.copy(XNT[:, c, :], PT[:, 0:128]).then_inc(S("n_xt"), 1)

        def bias_tensor(pe, j, q):
            for k in range(2):
                nc.tensor.matmul(Z[q][:, 128 * k:128 * k + 128], ROWS[0:2, 0:128], ROWS[0:2, 640 + 128 * k:768 + 128 * k],
                                 start=(k == 0), stop=False, skip_group_check=True)

        def gates_tensor(pe, j, jj, q, step):
            if step < 2 and jj < CHUNKS:
                rhs = XNT[:, j, :].rearrange("p (b t) -> p t b", b=BATCH)
                pe.wait_ge(S("n_xt"), j + 1)
            elif step >= 2 and jj >= LAG:
                rhs = HH[q][:, 1:TC + 1, 0:4, 1]
            else:
                rhs = None
            if rhs is not None:
                lay = step // 2
                if step % 2:
                    if (j is not None) and step == (1 if jj < CHUNKS else 3):
                        pass
                    mm = nc.tensor.matmul(pnv[:, :, lay, :], w[f"i{lay + 1}"], rhs,
                                          start=(step == (1 if jj < CHUNKS else 3)), stop=False, skip_group_check=True)
                else:
                    mm = nc.tensor.matmul(zv[q][:, :, lay, :], w[f"f{lay + 1}"], rhs,
                                          start=False, stop=False, skip_group_check=True)
            if step == (3 if jj >= LAG else 1):
                mm.then_inc(S("pre_mm"), 1)

        def cand_scalar(act, j, jj, q, step):
            lo = layers(jj)
            if step == 0:
                act.wait_ge(S("pre_mm"), j + 1)
                nc.scalar.activation(TN[0][:, :, lo], PN[:, 0:256].rearrange("p (t c) -> p t c", c=8)[:, :, lo],
                                     ACT.Tanh).then_inc(S("tn1"), 1)
            if step == 1:
                act.wait_ge(S("tn1"), j + 1)
                nc.scalar.activation(TN[1][:, :, lo], TN[0][:, :, lo], ACT.Tanh).then_inc(S("tn2"), 1)
            if step == 2:
                act.wait_ge(S("tn2"), j + 1)
                nc.scalar.mul(NH[q][:, :, lo], TN[1][:, :, lo], 0.5).then_inc(S("nh"), 1)

        def ef(v, n, hprev, nh, cols, done):
            v.scalar_tensor_tensor(out=EF[n % 2][:, cols, 0], in0=hprev[:, cols], scalar=-0.5, in1=nh[:, cols],
                                   op0=ALU.mult, op1=ALU.add)
            v.scalar_tensor_tensor(out=EF[n % 2][:, cols, 1], in0=hprev[:, cols], scalar=0.5, in1=nh[:, cols],
                                   op0=ALU.mult, op1=ALU.add).then_inc(S("ef"), 1)

        @block.vector
        def _(v):
            for p in range(2):
                v.memset(TH[p][:], 0.0).then_inc(S("v_init"), 1)
            v.wait_ge(S("consts"), 64)
            for l in range(2):
                v.tensor_scalar(HH[1][:, TC, 4 * l:4 * l + 4, 1], ones[:, 0:4], COLS[:, l:l + 1], None,
                                ALU.mult).then_inc(S("v_init"), 1)
            v.tensor_scalar(G1[:], G1[:], 1.0, None, ALU.add).then_inc(S("v_init"), 1)
            v.wait_ge(S("x_in"), 64)
            norm_vector_1(v, 0)
            norm_vector_2(v, 0)
            v.wait_ge(S("v_init"), 5)
            norm_vector_3(v, 0)
            v.wait_ge(S("nh"), 1)
            ef(v, 0, HH[1][:, TC, :, 1], NH[0][:, 0, :], slice(0, 4), S)

            def turn(i, p, ii):
                cols = layers(ii)
                for t in range(TC):
                    v.wait_ge(S("th"), i * TC + t + 1)
                    v.wait_ge(S("ef"), i * TC + t + 1)
                    if t == 0 and ii >= LAG + 2:
                        v.wait_ge(S("h2"), i - LAG - 1)
                    flat = lambda a: a.rearrange("p a b -> p (a b)")
                    v.tensor_tensor_scan(out=flat(HH[p][:, t + 1, cols, :]), data0=flat(TH[t % 2][:, cols, :]),
                                         data1=flat(EF[t % 2][:, cols, :]), initial=0.0, op0=ALU.mult,
                                         op1=ALU.add).then_inc(S("h"), 1)
                    v.wait_ge(S("h"), i * TC + t + 1)
                    if t < TC - 1:
                        ef(v, t + 1, HH[p][:, t + 1, :, 1], NH[p][:, t + 1, :], cols, S)
                    elif ii < TURNS - 1:
                        v.wait_ge(S("nh"), i + 2)
                        ef(v, 0, HH[p][:, TC, :, 1], NH[1 - p][:, 0, :], layers(ii + 1), S)
                    if ii + 1 < CHUNKS:
                        if t == 0:
                            norm_vector_1(v, i + 1)
                        if t == 2:
                            norm_vector_2(v, i + 1)
                        if t == 4:
                            norm_vector_3(v, i + 1)
            weights_vector(v)
            turns(v, turn)
            finish_vector(v)

        @block.gpsimd
        def _(g):
            g.wait_ge(S("consts"), 64)
            norm_pool_1(g, 0)
            norm_pool_2(g, 0)

            def turn(i, p, ii):
                if ii + 1 < CHUNKS:
                    norm_pool_1(g, i + 1)
                    norm_pool_2(g, i + 1)
                if ii >= LAG + 1:
                    copy_h2(i - 1, 1 - p)

            def copy_h2(i, p):
                g.wait_ge(S("h"), i * TC + TC)
                g.tensor_copy(H2[:, i - LAG, :].rearrange("p (b t) -> p b t", b=BATCH),
                              HH[p][:, 1:TC + 1, 4:8, 1].rearrange("p t b -> p b t")).then_inc(S("h2"), 1)
            turns(g, turn)
            copy_h2(TURNS - 1, (TURNS - 1) % 2)
            finish_pool(g)

        @block.scalar
        def _(act):
            act.wait_ge(S("v_init"), 2)
            norm_scalar(act, 0)
            for k in range(3):
                cand_scalar(act, 0, 0, 0, k)

            def turn(i, p, ii):
                cols = layers(ii)
                for t in range(TC):
                    act.wait_ge(S("z"), i * TC + t + 1)
                    nc.scalar.activation(TH[t % 2][:, cols, 1], Z[p][:, 8 * t + cols.start:8 * t + cols.stop],
                                         ACT.Tanh, scale=0.5).then_inc(S("th"), 1)
                    if t == 7 and ii + 1 < CHUNKS:
                        norm_scalar(act, i + 1)
                    if t in (18, 20, 22) and ii + 1 < TURNS:
                        cand_scalar(act, i + 1, ii + 1, 1 - p, (t - 18) // 2)
            weights_scalar(act)
            turns(act, turn)
            finish_scalar(act)

        @block.tensor
        def _(pe):
            pe.wait_ge(S("consts"), 64)
            pe.wait_ge(S("mats"), 16)
            norm_tensor(pe, 0)
            bias_tensor(pe, 0, 0)
            for k in range(4):
                gates_tensor(pe, 0, 0, 0, k)

            def turn(i, p, ii):
                for t in range(TC):
                    pe.wait_ge(S("h") if (ii or t) else S("v_init"), i * TC + t if (ii or t) else 5)
                    prev = HH[p][:, t, :, 1] if t else HH[1 - p][:, TC, :, 1]
                    for lay in range(2):
                        if 4 * lay < layers(ii).start or 4 * lay >= layers(ii).stop:
                            continue
                        for m in range(0, 128, 32):
                            mm = nc.tensor.matmul(Z[p][m:m + 32, 8 * t + 4 * lay:8 * t + 4 * lay + 4],
                                                  w[f"r{lay + 1}"][:, m:m + 32], prev[:, 4 * lay:4 * lay + 4],
                                                  start=False, stop=False, skip_group_check=True)
                    mm.then_inc(S("z"), 1)
                    if t == 6 and ii + 1 < CHUNKS:
                        norm_tensor(pe, i + 1)
                    if t == 9 and ii + 1 < TURNS:
                        bias_tensor(pe, i + 1, 1 - p)
                    if t in (10, 11, 12, 13) and ii + 1 < TURNS:
                        gates_tensor(pe, i + 1, ii + 1, 1 - p, t - 10)
            weights_tensor(pe)
            turns(pe, turn)
            finish_tensor(pe)


def kernel(**inputs):
    import numpy as np
    import concourse.bacc as bacc
    from concourse.bass_utils import run_bass_kernel_spmd

    a = {k: np.asarray(v) for k, v in inputs.items()}
    A, B_ = "L0_attn_a_", "L0_attn_b_"
    lWi, lWif, lWhf = a[A + "lWi"], a[A + "lWif"], a[A + "lWhf"]
    Wg = a[B_ + "Wg"]
    hk, hv = a[B_ + "haar_Wk"], a[B_ + "haar_Wv"]
    mats = {"i1": lWi[0].T, "f1": lWif[0].T, "r1": lWhf[0].T, "i2": lWi[1].T, "f2": lWif[1].T, "r2": lWhf[1].T,
            "gi": a[A + "gWi"].T, "gf": a[A + "gWif"].T, "gh": a[A + "gWhf"].T,
            "wk": a[B_ + "Wk"], "wv": a[B_ + "Wv"], "qT": a[B_ + "Wq"].T, "klT": a[B_ + "Wkl"].T,
            "vlT": a[B_ + "Wvl"].T, "kT": a[B_ + "Wk"].T, "vT": a[B_ + "Wv"].T,
            "g1T": Wg[:, 0:D].T, "g2T": Wg[:, D:].T, "oT": a[B_ + "Wo"].T, "tern": a["L0_ffn_weight"].T,
            "go": np.broadcast_to(a[B_ + "Wgo"].reshape(D, 1), (D, D))}
    for l in range(4):
        for n, m in (("hk", hk), ("hv", hv)):
            mats[f"{n}{l}"] = np.broadcast_to(m[l].T[None, :, None, :], (HEADS, DH, HEADS, DH)).reshape(D, D)
    mats = np.ascontiguousarray(np.concatenate([mats[n] for n in MATS], axis=1))
    cols = np.concatenate([a[A + "l_init_hidden"].T, a[B_ + "bg"].reshape(D, 1),
                           np.broadcast_to(a[B_ + "bgo"].reshape(1, 1), (D, 1)),
                           np.broadcast_to(a[B_ + "haar_scale"].reshape(1, 4), (D, 4)),
                           np.zeros((D, 4), np.float32)], axis=1)
    rows = np.zeros((2, 5 * 128 + 256), np.float32)
    rows[0:2, 0:128] = a[A + "lbhf"]
    rows[0, 128:256] = a[A + "gbhf"]
    rows[0, 256:384] = a[B_ + "bo"]
    rows[:, 640:896] = np.tile(np.repeat(np.eye(2, dtype=np.float32), BATCH, axis=1), (1, TC))
    s, t = np.arange(TC)[:, None], np.arange(TC)[None, :]
    means = np.zeros((128, LEVELS, 128), np.float32)
    for l in range(LEVELS):
        size = 2 ** l
        m = ((s <= t) & (s >= t // size * size)) / (t % size + 1.0)
        for b in range(BATCH):
            means[TC * b:TC * b + TC, l, TC * b:TC * b + TC] = m
    causal = np.tile((s <= t).astype(np.float32), (BATCH, 1))
    add = np.concatenate([np.where(s <= t, 0.0, NEG), np.zeros((TC, TC)), np.where(s > t, 0.0, NEG)], axis=1)
    consts = np.concatenate([np.eye(128), means.reshape(128, -1), causal,
                             np.repeat(np.eye(HEADS), DH, axis=0), np.repeat(np.eye(BATCH), TC, axis=0),
                             np.tile(add, (BATCH, 1)), np.full((128, 2), -0.5), np.ones((128, 128))],
                            axis=1).astype(np.float32)
    arrays = {"x": a[A + "x"], "gamma_rows": np.ascontiguousarray(np.broadcast_to(a[A + "gamma"][None], (128, D))),
              "cols": np.ascontiguousarray(cols), "rows": rows, "mats": mats, "consts": np.ascontiguousarray(consts)}
    nc = bacc.Bacc("TRN2", target_bir_lowering=False, num_devices=1)
    ins = {n: nc.dram_tensor("in_" + n, v.shape, mybir.dt.from_np(v.dtype), kind="ExternalInput").ap()
           for n, v in arrays.items()}
    out = nc.dram_tensor("out_0", (BATCH, TOKENS, D), F32, kind="ExternalOutput").ap()
    build(nc, ins, out)
    r = run_bass_kernel_spmd(nc, [{"in_" + n: v for n, v in arrays.items()}], core_ids=[0])
    return r.results[0]["out_0"]
```

```python
from contextlib import ExitStack

import concourse.bass as bass
from concourse import mybir

ALU = mybir.AluOpType
ACT = mybir.ActivationFunctionType
AX = mybir.AxisListType
F32 = mybir.dt.float32

BATCH, TOKENS, D = 4, 1024, 128
TC = 32
CHUNKS = TOKENS // TC
HEADS, DH = 16, 8
E9 = DH + 1
HG = 4
LEVELS = 5
LAG = 2
SCAN_TURNS = CHUNKS + LAG
FRONT = 3
PROJ = 4
ATTN = 5
TAIL = 6
TURNS = CHUNKS + TAIL
SV = BATCH * E9
VW = HEADS * SV
HALF = VW // 2
QW = HEADS * TC
OW = BATCH * HG * E9
NEG = -1.0e30
LN_EPS = 1.0e-5
ROUND = 1.5 * 2.0 ** 23
NORM_FLOOR = 1.0e-24 / D

MATS = ["i1", "f1", "r1", "i2", "f2", "r2", "gi", "gf", "gh", "wk", "wv", "qT", "klT", "vlT", "kT", "vT",
        "g1T", "g2T", "oT", "tern", "go"] + [f"hk{l}" for l in range(4)] + [f"hv{l}" for l in range(4)]
CONSTS = {"ident": 128, "means": LEVELS * 128, "causal": TC, "hmask": HEADS, "bmask": BATCH, "gmask": HG,
          "addmask": 3 * TC, "neghalf": 2, "ones": 128}



def build(nc, ins, out):
    with ExitStack() as ctx:
        def sb(name, shape):
            return ctx.enter_context(nc.sbuf_tensor(name, shape, F32))

        def ps(name, shape=(128, 512)):
            return ctx.enter_context(nc.psum_tensor(name, list(shape), F32))

        sems = {}

        def S(name):
            if name not in sems:
                sems[name] = ctx.enter_context(nc.semaphore(name))
            return sems[name]

        W = sb("W", [128, len(MATS) * 128])
        w = {n: W[:, 128 * k:128 * k + 128] for k, n in enumerate(MATS)}
        C = sb("C", [128, sum(CONSTS.values())])
        c_, at = {}, 0
        for n, k in CONSTS.items():
            c_[n] = C[:, at:at + k]
            at += k
        COLS = sb("COLS", [128, 12])
        ROWS = sb("ROWS", [2, 5 * 128 + 256])
        G1 = sb("G1", [128, 128])
        X = sb("X", [128, CHUNKS, 128])
        xn = sb("xn", [128, 128])
        XNT = sb("XNT", [128, CHUNKS, 128])
        GX = [sb(f"GX{p}", [128, 128]) for p in range(2)]
        HH = [sb(f"HH{p}", [128, TC + 1, 8, 2]) for p in range(2)]
        EF = [sb(f"EF{p}", [128, 8, 2]) for p in range(2)]
        TH = [sb(f"TH{p}", [128, 8, 2]) for p in range(2)]
        NH = [sb(f"NH{p}", [128, TC, 8]) for p in range(2)]
        TN = [sb(f"TN{p}", [128, TC, 8]) for p in range(2)]
        st = sb("st", [128, 6])
        sm = sb("sm", [128, 16])
        xl = sb("xl", [128, 128])

        wtmp = sb("wtmp", [128, 128])
        ws = sb("ws", [128, 18])
        hb = sb("hb", [128, 2])
        WL = sb("WL", [128, 6, BATCH * HG])
        WKL = W[:, 128 * MATS.index("hk0"):128 * MATS.index("hk0") + 512]
        WVL = W[:, 128 * MATS.index("hv0"):128 * MATS.index("hv0") + 512]
        lnb = {n: sb("ln_" + n, [128, 10]) for n in "abd"}
        VE = [sb(f"VE{p}", [128, LEVELS, HEADS, BATCH, E9]) for p in range(2)]
        VEL = [sb(f"VEL{p}", [128, HEADS, BATCH, E9]) for p in range(4)]
        KL = [sb(f"KL{p}", [128, 128]) for p in range(4)]
        KP = [sb(f"KP{p}", [128, 768]) for p in range(2)]
        KR = [sb(f"KR{p}", [128, 640]) for p in range(2)]
        QL = sb("QL", [128, BATCH, HEADS, TC])
        QG = [sb(f"QG{p}", [128, BATCH, HEADS, TC]) for p in range(2)]
        ST = sb("ST", [128, LEVELS, HEADS, BATCH, E9])
        DT = sb("DT", [128, LEVELS, HG * SV])
        qr = sb("qr", [128, 128])
        WARM_COLS = 256
        zeros = ctx.enter_context(nc.sbuf_tensor("zeros", [128, 256], mybir.dt.bfloat16))
        A = [sb(f"A{p}", [128, HEADS, TC]) for p in range(2)]
        SL, SR = sb("SL", [128, 3, HEADS, TC]), sb("SR", [128, 3, HEADS, TC])
        lmx, nmx = sb("lmx", [128, HEADS]), sb("nmx", [128, HEADS])
        RN, GO = sb("RN", [128, 96]), sb("GO", [128, 96, DH])
        GS, LT, GT, DF, h2s, xts, cd, la, laT, xb, gu, gu2, gt_, sg, ta, m2, mix, x3, ld, ldT = (
            sb(n, [128, 128]) for n in ("GS LT GT DF h2s xts cd la laT xb gu gu2 gt_ sg ta m2 mix x3 ld ldT").split())
        x4 = [sb(f"x4{p}", [128, 128]) for p in range(2)]
        ct = sb("ct", [128, 384])
        XM = sb("XM", [128, 640])
        EX = sb("EX", [128, 768])

        Z = [ps(f"Z{p}") for p in range(2)]
        PB = ps("PB")
        FR = ps("FR")
        RG = [ps(f"RG{p}") for p in range(2)]
        OB = ps("OB", (128, 2, 512))
        PN, PT, PE_ = PB[:, 0:256], PB[:, 256:384], PB[:, 384:512]

        ident, ones = c_["ident"], c_["ones"]
        zv = [Z[p][:, 0:256].rearrange("p (t l b) -> p t l b", l=2, b=4) for p in range(2)]
        pnv = PN.rearrange("p (t l b) -> p t l b", l=2, b=4)

        block = ctx.enter_context(nc.Block())

        def layers(i, j=None):
            return slice(0 if i < CHUNKS else 4, 8 if i >= LAG else 4)

        def turns(eng, body, last=None):
            for i in range(4):
                body(i, i % 2, i)
            with eng.Fori(4, CHUNKS - 3, 2) as i:
                for p in range(2):
                    body(i + p, p, 4)
            for i in range(CHUNKS - 2, TURNS):
                body(i, i % 2, i)

        def weights_vector(v):
            tern = w["tern"]
            v.wait_ge(S("mats"), 16)
            v.scalar_tensor_tensor(out=wtmp[:], in0=tern, scalar=-1.0, in1=tern, op0=ALU.mult, op1=ALU.max).then_inc(S("w1"), 1)
            v.wait_ge(S("w1"), 1)
            v.tensor_reduce(ws[:, 0:1], wtmp[:], AX.X, ALU.add).then_inc(S("w2"), 1)
            for n in ["hk0", "hk1", "hk2", "hk3", "hv0", "hv1", "hv2", "hv3"]:
                blk = w[n].rearrange("p (h e) -> p h e", e=DH)
                v.tensor_tensor(blk, blk, c_["hmask"].rearrange("p (h o) -> p h o", o=1).broadcast_to([128, HEADS, DH]),
                                ALU.mult).then_inc(S("w_blk"), 1)
            v.wait_ge(S("w_tot"), 1)
            v.tensor_scalar(ws[:, 1:2], PE_[:, 0:1], 1.0 / (D * D), LN_EPS, ALU.mult, ALU.max).then_inc(S("w3"), 1)
            v.wait_ge(S("w3"), 1)
            v.reciprocal(ws[:, 2:3], ws[:, 1:2]).then_inc(S("w4"), 1)
            v.wait_ge(S("w4"), 1)
            v.tensor_scalar(wtmp[:], tern, ws[:, 2:3], None, ALU.mult).then_inc(S("w5"), 1)
            v.wait_ge(S("w5"), 1)
            v.tensor_scalar(wtmp[:], wtmp[:], ROUND, None, ALU.add).then_inc(S("w5"), 1)
            v.wait_ge(S("w5"), 2)
            v.tensor_scalar(wtmp[:], wtmp[:], ROUND, None, ALU.subtract).then_inc(S("w5"), 1)
            v.wait_ge(S("w5"), 3)
            v.tensor_scalar(wtmp[:], wtmp[:], 1.0, -1.0, ALU.min, ALU.max).then_inc(S("w5"), 1)
            v.wait_ge(S("w5"), 4)
            v.tensor_scalar(tern, wtmp[:], ws[:, 1:2], None, ALU.mult).then_inc(S("w_tern"), 1)
            hs = COLS[:, 4:8]
            v.tensor_reduce(ws[:, 3:4], hs, AX.X, ALU.max).then_inc(S("w6"), 1)
            v.wait_ge(S("w6"), 1)
            v.tensor_scalar(ws[:, 4:8], hs, ws[:, 3:4], None, ALU.subtract).then_inc(S("w6"), 1)
            v.wait_ge(S("w_exp"), 1)
            v.tensor_reduce(ws[:, 12:13], ws[:, 8:12], AX.X, ALU.add).then_inc(S("w6"), 1)
            v.wait_ge(S("w6"), 3)
            v.reciprocal(ws[:, 13:14], ws[:, 12:13]).then_inc(S("w6"), 1)
            v.wait_ge(S("w6"), 4)
            v.tensor_scalar(ws[:, 14:18], ws[:, 8:12], ws[:, 13:14], None, ALU.mult).then_inc(S("w6"), 1)
            v.memset(WL[:], 1.0).then_inc(S("w6"), 1)
            v.wait_ge(S("w6"), 6)
            for l in range(1, LEVELS):
                v.tensor_scalar(WL[:, l, :], WL[:, l, :], ws[:, 13 + l:14 + l], None, ALU.mult).then_inc(S("w7"), 1)
            v.tensor_scalar(hb[:], COLS[:, 2:4], 0.5, None, ALU.mult).then_inc(S("w7"), 1)
            v.memset(ST[:], 0.0).then_inc(S("st0"), 1)
            for p in range(2):
                v.memset(VE[p][:], 1.0).then_inc(S("w7"), 1)
            for p in range(4):
                v.memset(VEL[p][:], 1.0).then_inc(S("w7"), 1)
            v.wait_ge(S("w7"), 11)
            for t_ in [VE[p][:, l] for p in range(2) for l in range(LEVELS)] + [VEL[p][:] for p in range(4)]:
                v.tensor_tensor(t_, t_, c_["bmask"].rearrange("p (o b q) -> p o b q", o=1, q=1).broadcast_to(
                    [128, HEADS, BATCH, E9]), ALU.mult).then_inc(S("w8"), 1)

        def weights_tensor(pe):
            pe.wait_ge(S("w2"), 1)
            nc.tensor.matmul(PE_[:, 0:1], ones, ws[:, 0:1], start=True, stop=True).then_inc(S("w_tot"), 1)
            pe.wait_ge(S("w_blk"), 8)
            for n in range(4):
                nc.tensor.matmul(FR[:, 128 * n:128 * n + 128], w["wk"], w[f"hk{n}"], start=True, stop=True)
            for n in range(4):
                mm = nc.tensor.matmul(RG[0][:, 128 * n:128 * n + 128], w["wv"], w[f"hv{n}"], start=True, stop=True)
            mm.then_inc(S("w_lev"), 1)

        def weights_scalar(act):
            act.wait_ge(S("w6"), 2)
            nc.scalar.activation(ws[:, 8:12], ws[:, 4:8], ACT.Exp).then_inc(S("w_exp"), 1)
            act.wait_ge(S("w_lev"), 1)
            nc.scalar.copy(WKL, FR[:]).then_inc(S("w_kvl"), 1)
            nc.scalar.copy(WVL, RG[0][:]).then_inc(S("w_kvl"), 1)

        def wk_of(l):
            return w["kT"] if l == 0 else WKL[:, 128 * l - 128:128 * l]

        def wv_of(l):
            return w["vT"] if l == 0 else WVL[:, 128 * l - 128:128 * l]

        def ln_stats(v, c, tag, src, ready):
            v.wait_ge(S("v_init"), 2)
            v.wait_ge(S(ready), c + 1)
            v.bn_stats(lnb[tag][:, 0:6], src).then_inc(S(tag + "_st"), 1)

        def ln_aggregate(v, c, tag):
            v.wait_ge(S(tag + "_st"), c + 1)
            v.sem_inc(S("alone"), 1)
            v.bn_aggr(lnb[tag][:, 6:8], lnb[tag][:, 0:6]).then_inc(S(tag + "_ag"), 1)

        def ln_epsilon(v, c, tag):
            v.wait_ge(S(tag + "_ag"), c + 1)
            v.tensor_scalar(lnb[tag][:, 8:9], lnb[tag][:, 7:8], LN_EPS, None, ALU.add).then_inc(S(tag + "_ve"), 1)

        def ln_root(g, c, tag):
            g.wait_ge(S(tag + "_ve"), c + 1)
            g.tensor_tensor(lnb[tag][:, 9:10], lnb[tag][:, 8:9], c_["neghalf"][:, 0:1], ALU.pow)\
                .then_inc(S(tag + "_rs"), 1)

        def ln_apply(v, c, tag, src, dst, used):
            v.wait_ge(S(tag + "_rs"), c + 1)
            v.wait_ge(S(used), c)
            v.tensor_scalar(dst, src, lnb[tag][:, 6:7], lnb[tag][:, 9:10], ALU.subtract, ALU.mult)\
                .then_inc(S(tag + "_ln"), 1)

        def layers(i):
            return slice(0 if i < CHUNKS else 4, 8 if i >= LAG else 4)

        def scan_tensor(pe, i, p, ii, t):
            if ii or t:
                pe.wait_ge(S("h"), i * TC + t)
            else:
                pe.wait_ge(S("v_init"), 5)
            prev = HH[p][:, t, :, 1] if t else HH[1 - p][:, TC, :, 1]
            for lay in range(2):
                if layers(ii).start <= 4 * lay < layers(ii).stop:
                    for m in range(0, 128, 32):
                        mm = nc.tensor.matmul(Z[p][m:m + 32, 8 * t + 4 * lay:8 * t + 4 * lay + 4],
                                              w[f"r{lay + 1}"][:, m:m + 32], prev[:, 4 * lay:4 * lay + 4],
                                              start=False, stop=False, skip_group_check=True)
            mm.then_inc(S("z"), 1)

        def keep_warm(pe, p, n):
            for _ in range(n):
                nc.tensor.matmul(Z[1 - p][:, 256:256 + WARM_COLS], zeros[:, 0:128], zeros[:, 0:WARM_COLS], start=False,
                                 stop=False, skip_group_check=True)

        def scan_scalar(act, i, p, ii, t):
            cols = layers(ii)
            act.wait_ge(S("z"), i * TC + t + 1)
            nc.scalar.activation(TH[t % 2][:, cols, 1], Z[p][:, 8 * t + cols.start:8 * t + cols.stop],
                                 ACT.Tanh, scale=0.5).then_inc(S("th"), 1)

        def halves(v, n, hprev, nh, cols):
            v.scalar_tensor_tensor(out=EF[n % 2][:, cols, 0], in0=hprev[:, cols], scalar=-0.5, in1=nh[:, cols],
                                   op0=ALU.mult, op1=ALU.add)
            v.scalar_tensor_tensor(out=EF[n % 2][:, cols, 1], in0=hprev[:, cols], scalar=0.5, in1=nh[:, cols],
                                   op0=ALU.mult, op1=ALU.add).then_inc(S("ef"), 1)

        def scan_vector(v, i, p, ii, t):
            cols = layers(ii)
            flat = lambda a: a.rearrange("p a b -> p (a b)")
            v.wait_ge(S("th"), i * TC + t + 1)
            v.wait_ge(S("ef"), i * TC + t + 1)
            if t == 0 and ii >= LAG + 2:
                v.wait_ge(S("h2"), i - LAG - 1)
            v.tensor_tensor_scan(out=flat(HH[p][:, t + 1, cols, :]), data0=flat(TH[t % 2][:, cols, :]),
                                 data1=flat(EF[t % 2][:, cols, :]), initial=0.0, op0=ALU.mult,
                                 op1=ALU.add).then_inc(S("h"), 1)
            v.wait_ge(S("h"), i * TC + t + 1)
            if t < TC - 1:
                halves(v, t + 1, HH[p][:, t + 1, :, 1], NH[p][:, t + 1, :], cols)
            elif ii < SCAN_TURNS - 1:
                v.wait_ge(S("nh"), i + 2)
                halves(v, 0, HH[p][:, TC, :, 1], NH[1 - p][:, 0, :], layers(ii + 1))

        def norm_stats(v, c):
            v.bn_stats(st[:], X[:, c, :]).then_inc(S("n_st"), 1)

        def norm_aggregate(v, c):
            v.wait_ge(S("n_st"), c + 1)
            v.sem_inc(S("alone"), 1)
            v.bn_aggr(sm[:, 0:2], st[:]).then_inc(S("n_ag"), 1)

        def norm_epsilon(v, c):
            v.wait_ge(S("n_ag"), c + 1)
            v.tensor_scalar(sm[:, 2:3], sm[:, 1:2], LN_EPS, None, ALU.add).then_inc(S("n_ve"), 1)

        def norm_root(g, c):
            g.wait_ge(S("n_ve"), c + 1)
            g.tensor_tensor(sm[:, 3:4], sm[:, 2:3], c_["neghalf"][:, 0:1], ALU.pow).then_inc(S("n_rs"), 1)

        def norm_apply(v, c):
            v.wait_ge(S("n_rs"), c + 1)
            v.tensor_scalar(xl[:], X[:, c, :], sm[:, 0:1], sm[:, 3:4], ALU.subtract, ALU.mult).then_inc(S("n_xl"), 1)
            v.scalar_tensor_tensor(out=sm[:, 4:5], in0=sm[:, 1:2], scalar=sm[:, 3:4], in1=sm[:, 3:4],
                                   op0=ALU.mult, op1=ALU.mult).then_inc(S("n_v2"), 1)

        def norm_floor(v, c):
            v.wait_ge(S("n_v2"), c + 1)
            v.tensor_scalar(sm[:, 5:6], sm[:, 4:5], NORM_FLOOR, None, ALU.max).then_inc(S("n_mx"), 1)

        def norm_root_2(g, c):
            g.wait_ge(S("n_mx"), c + 1)
            g.tensor_tensor(sm[:, 6:7], sm[:, 5:6], c_["neghalf"][:, 0:1], ALU.pow).then_inc(S("n_rn"), 1)

        def norm_rms(v, c):
            v.wait_ge(S("n_rn"), c + 1)
            v.wait_ge(S("n_xl"), c + 1)
            v.wait_ge(S("n_t"), c)
            v.scalar_tensor_tensor(out=xn[:], in0=xl[:], scalar=sm[:, 6:7], in1=G1[:],
                                   op0=ALU.mult, op1=ALU.mult).then_inc(S("n_xn"), 1)
            v.tensor_tensor(X[:, c, :], X[:, c, :], xl[:], ALU.add).then_inc(S("n_r1"), 1)

        def norm_residual(v, c):
            v.wait_ge(S("n_xn"), c + 1)
            v.wait_ge(S("n_r1"), c + 1)
            v.tensor_tensor(X[:, c, :], X[:, c, :], xn[:], ALU.add).then_inc(S("n_r2"), 1)

        def norm_tensor(pe, c, cc):
            pe.wait_ge(S("n_xn"), c + 1)
            if cc >= TAIL + 1:
                pe.wait_ge(S("x4"), c - TAIL)
            nc.tensor.transpose(PT, xn[:], ident).then_inc(S("n_t"), 1)

        def norm_scalar(act, c):
            act.wait_ge(S("n_t"), c + 1)
            nc.scalar.copy(XNT[:, c, :], PT).then_inc(S("n_xt"), 1)

        def bias_tensor(pe, q):
            for k in range(2):
                nc.tensor.matmul(Z[q][:, 128 * k:128 * k + 128], ROWS[0:2, 0:128], ROWS[0:2, 640 + 128 * k:768 + 128 * k],
                                 start=(k == 0), stop=False, skip_group_check=True)

        def scan_input(pe, j, jj, q, lay, cand):
            if lay == 0:
                if jj >= CHUNKS:
                    return
                pe.wait_ge(S("n_xt"), j + 1)
                rhs = XNT[:, j, :].rearrange("p (b t) -> p t b", b=BATCH)
            else:
                if jj < LAG:
                    return
                rhs = HH[q][:, 1:TC + 1, 0:4, 1]
            only = 1 if jj >= CHUNKS else 0
            if cand:
                mm = nc.tensor.matmul(pnv[:, :, lay, :], w[f"i{lay + 1}"], rhs, start=(lay == only), stop=False,
                                      skip_group_check=True)
                if lay == (1 if jj >= LAG else 0):
                    mm.then_inc(S("pre_mm"), 1)
            else:
                nc.tensor.matmul(zv[q][:, :, lay, :], w[f"f{lay + 1}"], rhs, start=False, stop=False,
                                 skip_group_check=True)

        def cand_scalar(act, j, jj, q, step):
            lo = layers(jj)
            if step == 0:
                act.wait_ge(S("pre_mm"), j + 1)
                nc.scalar.activation(TN[0][:, :, lo], PN.rearrange("p (t c) -> p t c", c=8)[:, :, lo],
                                     ACT.Tanh).then_inc(S("tn1"), 1)
            if step == 1:
                act.wait_ge(S("tn1"), j + 1)
                nc.scalar.activation(TN[1][:, :, lo], TN[0][:, :, lo], ACT.Tanh).then_inc(S("tn2"), 1)
            if step == 2:
                act.wait_ge(S("tn2"), j + 1)
                nc.scalar.mul(NH[q][:, :, lo], TN[1][:, :, lo], 0.5).then_inc(S("nh"), 1)

        def copy_states(g, i, c, p):
            g.wait_ge(S("h"), i * TC)
            g.wait_ge(S("cell_mm"), c)
            g.sem_inc(S("alone_g"), 1)
            g.tensor_copy(h2s[:].rearrange("p (b t) -> p b t", b=BATCH),
                          HH[p][:, 1:TC + 1, 4:8, 1].rearrange("p t b -> p b t")).then_inc(S("h2"), 1)
            g.tensor_copy(xts[:], XNT[:, c, :]).then_inc(S("f_in"), 1)

        def cell_tensor(pe, c):
            pe.wait_ge(S("h2"), c + 1)
            pe.wait_ge(S("f_in"), c + 1)
            pe.wait_ge(S("kr_out"), c - 1 if not isinstance(c, int) or c >= 1 else 0)
            nc.tensor.transpose(FR[:, 256:384], xts[:], ident)
            nc.tensor.matmul(FR[:, 0:128], h2s[:], w["gi"], start=True, stop=True)
            nc.tensor.matmul(FR[:, 128:256], ones[0:1, :], ROWS[0:1, 128:256], start=True, stop=False)
            nc.tensor.matmul(FR[:, 128:256], h2s[:], w["gf"], start=False, stop=False)
            nc.tensor.matmul(FR[:, 128:256], xts[:], w["gh"], start=False, stop=True).then_inc(S("cell_mm"), 1)

        def cell_scalar(act, c):
            act.wait_ge(S("cell_mm"), c + 1)
            act.wait_ge(S("x1"), c)
            nc.scalar.activation(ct[:, 0:128], FR[:, 0:128], ACT.Tanh).then_inc(S("ct1"), 1)
            nc.scalar.activation(ct[:, 256:384], FR[:, 128:256], ACT.Tanh, scale=0.5).then_inc(S("ct2"), 1)

        def cell_scalar_2(act, c):
            act.wait_ge(S("ct1"), c + 1)
            nc.scalar.activation(ct[:, 128:256], ct[:, 0:128], ACT.Tanh).then_inc(S("ct3"), 1)

        def cell_difference(v, c):
            v.wait_ge(S("ct2"), c + 1)
            v.wait_ge(S("ct3"), c + 1)
            v.tensor_tensor(cd[:], ct[:, 128:256], FR[:, 256:384], ALU.subtract).then_inc(S("cd1"), 1)

        def cell_gated(v, c):
            v.wait_ge(S("cd1"), c + 1)
            v.scalar_tensor_tensor(out=cd[:], in0=ct[:, 256:384], scalar=1.0, in1=cd[:], op0=ALU.add,
                                   op1=ALU.mult).then_inc(S("cd2"), 1)

        def cell_residual(v, c):
            v.wait_ge(S("cd2"), c + 1)
            v.scalar_tensor_tensor(out=X[:, c, :], in0=cd[:], scalar=0.5, in1=X[:, c, :], op0=ALU.mult,
                                   op1=ALU.add).then_inc(S("x1"), 1)

        def ffn1_transpose(pe, c):
            pe.wait_ge(S("a_ln"), c + 1)
            pe.wait_ge(S("cd1"), c + 1)
            if not isinstance(c, int) or c >= 1:
                pe.wait_ge(S("phi_a"), c)
            nc.tensor.transpose(FR[:, 256:384], la[:], ident).then_inc(S("t1"), 1)

        def ffn1_scalar(act, c):
            act.wait_ge(S("t1"), c + 1)
            nc.scalar.copy(laT[:], FR[:, 256:384]).then_inc(S("t1_out"), 1)

        def ffn1_tensor(pe, c):
            pe.wait_ge(S("t1_out"), c + 1)
            if not isinstance(c, int) or c >= 1:
                pe.wait_ge(S("gx"), c)
            nc.tensor.matmul(FR[:, 384:512], laT[:], w["tern"], start=True, stop=True).then_inc(S("y1"), 1)

        def ffn1_residual(v, c):
            v.wait_ge(S("y1"), c + 1)
            v.tensor_tensor(X[:, c, :], X[:, c, :], FR[:, 384:512], ALU.add).then_inc(S("x2"), 1)

        def means_tensor(pe, c, part):
            if part == 0:
                pe.wait_ge(S("b_ln"), c + 1)
                pe.wait_ge(S("x2"), c + 1)
                if not isinstance(c, int) or c >= 1:
                    pe.wait_ge(S("dd_out"), c)
                nc.tensor.matmul(FR[:], xb[:], c_["means"][:, 0:512], start=True, stop=True).then_inc(S("xm"), 1)
            else:
                pe.wait_ge(S("xm1"), c + 1)
                nc.tensor.matmul(FR[:, 0:128], xb[:], c_["means"][:, 512:640], start=True, stop=True)\
                    .then_inc(S("xm_b"), 1)

        def means_scalar(act, c, part):
            if part == 0:
                act.wait_ge(S("xm"), c + 1)
                act.wait_ge(S("pd"), c)
                nc.scalar.copy(XM[:, 0:512], FR[:]).then_inc(S("xm1"), 1)
            else:
                act.wait_ge(S("xm_b"), c + 1)
                nc.scalar.copy(XM[:, 512:640], FR[:, 0:128]).then_inc(S("xm2"), 1)

        def xm_(l):
            return XM[:, 128 * l:128 * l + 128]

        def values_tensor(pe, c, cc):
            pe.wait_ge(S("xm2"), c + 1)
            if cc < CHUNKS - 1:
                pe.wait_ge(S("cd1"), c + 2)
            elif cc > 0:
                pe.wait_ge(S("kr_out"), c)
            for l in range(4):
                m = nc.tensor.matmul(FR[:, 128 * l:128 * l + 128], xm_(l), wv_of(l), start=True, stop=True)
            m.then_inc(S("pc"), 1)

        def values_scalar(act, c, k, bs):
            act.wait_ge(S("pc"), c + 1)
            for b in bs:
                a = nc.scalar.activation(VE[k % 2][:, 0:4, :, b, 0:DH].rearrange("p l h e -> p (l h) e"),
                                         FR[:].rearrange("p (m e) -> p m e", e=DH), ACT.Copy,
                                         scale=c_["bmask"][:, b:b + 1])
            if b == BATCH - 1:
                a.then_inc(S("ve3"), 1)

        def queries_tensor(pe, c):
            pe.wait_ge(S("ve3"), c + 1)
            for n, (wt, l) in enumerate([(w["qT"], 0)] + [(wk_of(l), l) for l in range(3)]):
                m = nc.tensor.matmul(FR[:, 128 * n:128 * n + 128], wt, xm_(l), start=True, stop=True)
            m.then_inc(S("pa"), 1)

        def queries_copy(act, c):
            act.wait_ge(S("pa"), c + 1)
            nc.scalar.copy(qr[:], FR[:, 0:128]).then_inc(S("qr"), 1)

        def queries_expand(act, c, cc, hs):
            if hs[0] == 0:
                act.wait_ge(S("qr"), c + 1)
                if cc >= 1:
                    act.wait_ge(S("ring_mm"), use_of(c - 1, cc - 1, "l", blocks_of(cc - 1) - 1)[0] + 1)
            for h in hs:
                a = nc.scalar.activation(QL[:, :, h, :], qr[:].rearrange("p (b t) -> p b t", b=BATCH),
                                         ACT.Copy, scale=c_["hmask"][:, h:h + 1])
            if hs[-1] == HEADS - 1:
                a.then_inc(S("ql"), 1)

        def minimum(v, c, first):
            v.wait_ge(S("qr" if first else "pb"), c + 1)
            if first:
                v.tensor_scalar(EX[:, 0:512], FR[:], 0.0, None, ALU.min).then_inc(S("mna"), 1)
            else:
                v.tensor_scalar(EX[:, 512:768], FR[:, 0:256], 0.0, None, ALU.min).then_inc(S("mnb"), 1)

        def exponential(act, c, first):
            act.wait_ge(S("mna" if first else "mnb"), c + 1)
            part = EX[:, 0:512] if first else EX[:, 512:768]
            nc.scalar.activation(part, part, ACT.Exp).then_inc(S("ea" if first else "eb"), 1)

        def features(v, c, k, first):
            p = k % 2
            if first:
                v.wait_ge(S("ea"), c + 1)
                v.scalar_tensor_tensor(out=KP[p][:, 0:512], in0=FR[:], scalar=0.0, in1=EX[:, 0:512], op0=ALU.max,
                                       op1=ALU.add).then_inc(S("phi_a"), 1)
            else:
                v.wait_ge(S("eb"), c + 1)
                v.wait_ge(S("vl"), c + 1)
                v.scalar_tensor_tensor(out=KP[p][:, 512:768], in0=FR[:, 0:256], scalar=0.0, in1=EX[:, 512:768],
                                       op0=ALU.max, op1=ALU.add).then_inc(S("phi_b"), 1)

        def queries_pool(g, c, k, bs):
            if bs[0] == 0:
                g.wait_ge(S("phi_a"), c + 1)
            for b in bs:
                src = KP[k % 2][:, TC * b:TC * b + TC].rearrange("p (o t) -> p o t", o=1).broadcast_to([128, HEADS, TC])
                a = g.tensor_tensor(QG[k % 2][:, b, :, :], src, c_["hmask"].rearrange("p (h o) -> p h o", o=1)
                                    .broadcast_to([128, HEADS, TC]), ALU.mult)
            if bs[-1] == BATCH - 1:
                a.then_inc(S("qg"), 1)

        def gate_x_tensor(pe, c):
            pe.wait_ge(S("phi_a"), c + 1)
            nc.tensor.matmul(FR[:, 0:128], w["g1T"], xm_(0), start=True, stop=True).then_inc(S("gx_mm"), 1)

        def gate_x_scalar(act, c, cc, k):
            act.wait_ge(S("gx_mm"), c + 1)
            if cc < CHUNKS - 1:
                act.wait_ge(S("t1"), c + 2)
            nc.scalar.copy(GX[k % 2][:], FR[:, 0:128]).then_inc(S("gx"), 1)

        def keys_tensor(pe, c, cc):
            pe.wait_ge(S("gx"), c + 1)
            if cc < CHUNKS - 1:
                pe.wait_ge(S("x2"), c + 2)
            for n, (wt, l) in enumerate([(wk_of(3), 3), (wk_of(4), 4), (w["klT"], 0)]):
                nc.tensor.matmul(FR[:, 128 * n:128 * n + 128], wt, xm_(l), start=True, stop=True)
            nc.tensor.matmul(FR[:, 384:512], xm_(0), w["vlT"], start=True, stop=True).then_inc(S("pb"), 1)

        def expand_values(act, src, dst):
            for b in range(BATCH):
                a = nc.scalar.activation(dst[:, :, b, 0:DH], src.rearrange("p (h e) -> p h e", e=DH), ACT.Copy,
                                         scale=c_["bmask"][:, b:b + 1])
            return a

        def local_scalar(act, c, k):
            act.wait_ge(S("mnb"), c + 1)
            nc.scalar.copy(KL[k][:], FR[:, 256:384]).then_inc(S("kl"), 1)
            expand_values(act, FR[:, 384:512], VEL[k]).then_inc(S("vl"), 1)

        def rows_tensor(pe, c, cc, k, part):
            if part == 0:
                pe.wait_ge(S("phi_b"), c + 1)
                pe.wait_ge(S("vl"), c + 1)
                nc.tensor.matmul(FR[:, 0:128], xm_(4), wv_of(4), start=True, stop=True)
                for l in range(3):
                    m = nc.tensor.transpose(FR[:, 128 * l + 128:128 * l + 256],
                                            KP[k % 2][:, 128 * l + 128:128 * l + 256], ident)
                m.then_inc(S("pd"), 1)
            else:
                pe.wait_ge(S("dd_out"), c + 1)
                if cc < CHUNKS - 1:
                    pe.wait_ge(S("xm2"), c + 2)
                for l in range(3, 5):
                    m = nc.tensor.transpose(FR[:, 128 * l - 256:128 * l - 128],
                                            KP[k % 2][:, 128 * l + 128:128 * l + 256], ident)
                m.then_inc(S("kr4"), 1)

        def rows_scalar(act, c, k, part):
            p = k % 2
            if part == 0:
                act.wait_ge(S("pd"), c + 1)
                expand_values(act, FR[:, 0:128], VE[p][:, 4]).then_inc(S("ve4"), 1)
            if part == 1:
                nc.scalar.copy(KR[p][:, 0:384], FR[:, 128:512]).then_inc(S("dd_out"), 1)
            if part == 2:
                act.wait_ge(S("kr4"), c + 1)
                nc.scalar.copy(KR[p][:, 384:640], FR[:, 128:384]).then_inc(S("kr_out"), 1)

        def blocks_of(cc):
            return min(cc, 2) + 1

        def use_of(c, cc, what, n):
            R = blocks_of(cc)
            base = 10 * c - 3 if cc >= 2 else 8 * cc
            first = 1 if cc >= 2 else 0
            off = n if what == "l" else R + (n if n < 2 else n + 1) if what == "s" else R + (2 if n == 0 else 6)
            return base + off, (first + off) % 2

        def take(pe, c, cc, what, n):
            use, bank = use_of(c, cc, what, n)
            if not isinstance(use, int) or use >= 2:
                pe.wait_ge(S("ring_read"), use - 1)
            return RG[bank]

        def local_scores(pe, c, cc, k, r):
            if r == 0:
                pe.wait_ge(S("ql"), c + 1)
                pe.wait_ge(S("kl"), c + 1)
            bank = take(pe, c, cc, "l", r)
            for b in range(BATCH):
                m = nc.tensor.matmul(bank[TC * b:TC * b + TC, :], KL[(k - r) % 4][:, TC * b:TC * b + TC],
                                     QL[:, b, :, :].rearrange("p h t -> p (h t)"), start=True, stop=True)
            m.then_inc(S("ring_mm"), 1)

        def level_scores(pe, c, cc, k, l):
            p = k % 2
            if l == 0:
                pe.wait_ge(S("qg"), c + 1)
                pe.wait_ge(S("phi_b"), c + 1)
            bank = take(pe, c, cc, "s", l)
            for b in range(BATCH):
                m = nc.tensor.matmul(bank[TC * b:TC * b + TC, :],
                                     KP[p][:, 128 * l + 128 + TC * b:128 * l + 128 + TC * b + TC],
                                     QG[p][:, b, :, :].rearrange("p h t -> p (h t)"), start=True, stop=True)
            m.then_inc(S("ring_mm"), 1)

        def increase_tensor(pe, c, cc, k, n):
            p = k % 2
            if n == 0:
                pe.wait_ge(S("kr_out"), c + 1)
                pe.wait_ge(S("ve4"), c + 1)
            bank = take(pe, c, cc, "d", n)
            for l in range(3 * n, min(3 * n + 3, LEVELS)):
                for i in range(HG):
                    m = nc.tensor.matmul(bank[TC * i:TC * i + TC, HG * SV * (l - 3 * n):HG * SV * (l - 3 * n + 1)],
                                         KR[p][:, 128 * l + TC * i:128 * l + TC * i + TC],
                                         VE[p][:, l, HG * i:HG * i + HG].rearrange("p h b e -> p (h b e)"),
                                         start=True, stop=True)
            m.then_inc(S("ring_mm"), 1)

        def ring_ready(v, c, cc, what, n):
            use, bank = use_of(c, cc, what, n)
            v.wait_ge(S("ring_mm"), use + 1)
            return RG[bank]

        def increase_vector(v, c, cc, n):
            bank = ring_ready(v, c, cc, "d", n)
            if n == 0:
                v.wait_ge(S("st"), 8 * c)
            L = 3 - n
            v.tensor_tensor(DT[:, 3 * n:3 * n + L].rearrange("p l (g q) -> p l g q", g=HG),
                            bank[:, 0:HG * SV * L].rearrange("p (l g q) -> p l g q", g=HG, q=SV),
                            c_["gmask"].rearrange("p (o g q) -> p o g q", o=1, q=1).broadcast_to([128, L, HG, SV]),
                            ALU.mult).then_inc(S("ring_read"), 1)

        def state_pool(g, c, cc, n):
            g.wait_ge(S("ring_read"), use_of(c, cc, "d", n)[0] + 1)
            if cc >= 1:
                g.wait_ge(S("past"), 5 * c + 2 * n - 2)
            elif n == 0:
                g.wait_ge(S("st0"), 1)
            lv = slice(3 * n, min(3 * n + 3, LEVELS))
            for i in range(HG):
                blk = ST[TC * i:TC * i + TC, lv, HG * i:HG * i + HG].rearrange("p l h b e -> p l (h b e)")
                g.tensor_tensor(blk, blk, DT[TC * i:TC * i + TC, lv, :], ALU.add).then_inc(S("st"), 1)

        def out_of(n):
            return OB[:, n // 3, OW * (n % 3):OW * (n % 3) + OW].rearrange("p (b g e) -> p b g e", b=BATCH, e=E9)

        def past_tensor(pe, c, cc, k, l):
            if cc == 0:
                return
            if l == 0:
                pe.wait_ge(S("go"), c)
            pe.wait_ge(S("st"), 8 * c - (4 if l < 3 else 0))
            for b in range(BATCH):
                for i in range(HG):
                    m = nc.tensor.matmul(out_of(l)[TC * i:TC * i + TC, b, :, :], KP[k % 2][:, TC * b:TC * b + TC],
                                         ST[:, l, HG * i:HG * i + HG, b, :], start=l % 3 == 0 and b == 0, stop=False,
                                         skip_group_check=True)
            m.then_inc(S("past"), 1)

        def mask_vector(v, c, cc, l):
            bank = ring_ready(v, c, cc, "s", l)
            if cc >= 1 or l >= 2:
                v.wait_ge(S("av"), 5 * c + l - 1)
            v.tensor_tensor(A[l % 2][:], bank[:].rearrange("p (h t) -> p h t", t=TC),
                            c_["causal"].rearrange("p (o t) -> p o t", o=1).broadcast_to([128, HEADS, TC]),
                            ALU.mult).then_inc(S("ring_read"), 1)

        def own_tensor(pe, c, cc, k, l):
            pe.wait_ge(S("ring_read"), use_of(c, cc, "s", l)[0] + 1)
            pe.wait_ge(S("ve3") if l < 4 else S("ve4"), c + 1)
            for g in range(HG):
                for i in range(HG):
                    m = nc.tensor.matmul(out_of(l)[TC * i:TC * i + TC, :, g, :], A[l % 2][:, HG * i + g, :],
                                         VE[k % 2][:, l, HG * i + g, :, :],
                                         start=l % 3 == 0 and cc == 0 and g == 0, stop=True, skip_group_check=True)
            m.then_inc(S("av"), 1)

        def local_mask(v, c, cc, r):
            bank = ring_ready(v, c, cc, "l", r)
            if r == 0:
                v.wait_ge(S("avl"), c)
            v.tensor_tensor(SL[:, r], bank[:].rearrange("p (h t) -> p h t", t=TC),
                            c_["addmask"][:, TC * r:TC * r + TC].rearrange("p (o t) -> p o t", o=1)
                            .broadcast_to([128, HEADS, TC]), ALU.add).then_inc(S("ring_read"), 1)

        def local_turn(v, c, cc, r):
            flat = lambda a: a.rearrange("p h t -> p (h t)")
            if r == 1:
                v.transpose(flat(SR[:, 1]), ring_ready(v, c, cc, "l", 1)[:]).then_inc(S("ring_read"), 1)
            else:
                v.wait_ge(S("ring_read"), use_of(c, cc, "l", r)[0] + 1)
                v.transpose(flat(SR[:, r]), flat(SL[:, r])).then_inc(S("lt"), 1)

        def local_max(v, c, cc, half):
            R, hs = blocks_of(cc), slice(8 * half, 8 * half + 8)
            if half == 0:
                v.wait_ge(S("lt"), (2 * c - 2 if cc >= 2 else cc) + (2 if cc >= 2 else 1))
                if cc >= 1:
                    v.wait_ge(S("ring_read"), use_of(c, cc, "l", 1)[0] + 1)
            v.tensor_reduce(lmx[:, hs], SR[:, 0:R, hs].rearrange("p r h t -> p h r t"), AX.XY, ALU.max)\
                .then_inc(S("lm"), 1)

        def local_shift(v, c):
            v.wait_ge(S("lm"), 2 * c + 2)
            v.tensor_scalar(nmx[:], lmx[:], -(DH ** -0.5), None, ALU.mult).then_inc(S("nm"), 1)

        def local_exp(act, c, cc, hs):
            if hs[0] == 0:
                act.wait_ge(S("nm"), c + 1)
            for h in hs:
                part = SR[:, 0:blocks_of(cc), h, :]
                a = nc.scalar.activation(part, part, ACT.Exp, scale=DH ** -0.5, bias=nmx[:, h:h + 1])
            if hs[-1] == HEADS - 1:
                a.then_inc(S("lx"), 1)

        def local_back(v, c, cc, r):
            if r == 0:
                v.wait_ge(S("lx"), c + 1)
            m = v.transpose(SL[:, r].rearrange("p h t -> p (h t)"), SR[:, r].rearrange("p h t -> p (h t)"))
            if r == blocks_of(cc) - 1:
                m.then_inc(S("pl"), 1)

        def local_tensor(pe, c, cc, k, r):
            if r == 0:
                pe.wait_ge(S("pl"), c + 1)
                pe.wait_ge(S("vl"), c + 1)
            for g in range(HG):
                for i in range(HG):
                    m = nc.tensor.matmul(out_of(LEVELS)[TC * i:TC * i + TC, :, g, :], SL[:, r, HG * i + g, :],
                                         VEL[(k - r) % 4][:, HG * i + g, :, :], start=False, stop=True,
                                         skip_group_check=True)
            if r == blocks_of(cc) - 1:
                m.then_inc(S("avl"), 1)

        ob = OB[:, :, 0:3 * OW].rearrange("p n (m e) -> p n m e", e=E9)
        go = GO[:].rearrange("p (l m) e -> p l (m e)", l=6)

        def weigh(v, c, step):
            if step == 0:
                v.wait_ge(S("av"), 5 * c + 5)
                v.wait_ge(S("avl"), c + 1)
                v.tensor_scalar(RN[:].rearrange("p (n m) -> p n m", n=2), ob[:, :, :, DH], 1.0e-6, None,
                                ALU.max).then_inc(S("r1"), 1)
            if step == 1:
                v.wait_ge(S("r1"), c + 1)
                v.reciprocal(RN[:], RN[:]).then_inc(S("r2"), 1)
            if step == 2:
                v.wait_ge(S("r2"), c + 1)
                v.tensor_tensor(RN[:], RN[:], WL[:].rearrange("p l m -> p (l m)"), ALU.mult).then_inc(S("r3"), 1)
            if step == 3:
                v.wait_ge(S("r3"), c + 1)
                v.tensor_tensor(GO[:].rearrange("p (n m) e -> p n m e", n=2), ob[:, :, :, 0:DH],
                                RN[:].rearrange("p (n m o) -> p n m o", n=2, o=1)
                                .broadcast_to([128, 2, 3 * BATCH * HG, DH]), ALU.mult).then_inc(S("go"), 1)

        def levels_sum(v, c):
            v.wait_ge(S("go"), c + 1)
            v.tensor_reduce(GS[:], go[:, 0:LEVELS, :].rearrange("p l q -> p q l"), AX.X, ALU.add).then_inc(S("gs"), 1)

        def outputs_turn(v, c):
            v.transpose(LT[:], go[:, LEVELS, :]).then_inc(S("ltr"), 1)
            v.wait_ge(S("gs"), c + 1)
            v.transpose(GT[:], GS[:]).then_inc(S("gtr"), 1)

        def difference(v, c):
            v.wait_ge(S("gtr"), c + 1)
            v.wait_ge(S("ltr"), c + 1)
            v.tensor_tensor(DF[:], LT[:], GT[:], ALU.subtract).then_inc(S("df"), 1)

        def gate_tensor(pe, c, cc):
            pe.wait_ge(S("df"), c + 1)
            pe.wait_ge(S("tn1"), c + TAIL + 1 if cc + TAIL < SCAN_TURNS else SCAN_TURNS)
            nc.tensor.matmul(PE_, w["g2T"], DF[:], start=True, stop=True).then_inc(S("gh"), 1)

        def gate_sum(v, c, p):
            v.wait_ge(S("gh"), c + 1)
            v.tensor_tensor(gu[:], PE_, GX[p][:], ALU.add).then_inc(S("gu"), 1)

        def gate_tanh(act, c):
            act.wait_ge(S("gu"), c + 1)
            nc.scalar.activation(gt_[:], gu[:], ACT.Tanh, scale=0.5, bias=hb[:, 0:1]).then_inc(S("gth"), 1)

        def gate_biased(v, c):
            v.wait_ge(S("gu"), c + 1)
            v.tensor_scalar(gu2[:], gu[:], COLS[:, 2:3], None, ALU.add).then_inc(S("gu2"), 1)

        def gate_silu(v, c):
            v.wait_ge(S("gu2"), c + 1)
            v.wait_ge(S("gth"), c + 1)
            v.scalar_tensor_tensor(out=sg[:], in0=gt_[:], scalar=1.0, in1=gu2[:], op0=ALU.add,
                                   op1=ALU.mult).then_inc(S("sg"), 1)

        def alpha_tensor(pe, c):
            pe.wait_ge(S("sg"), c + 1)
            nc.tensor.matmul(PE_, w["go"], sg[:], start=True, stop=True).then_inc(S("al"), 1)

        def alpha_scalar(act, c):
            act.wait_ge(S("al"), c + 1)
            nc.scalar.activation(ta[:], PE_, ACT.Tanh, scale=0.25, bias=hb[:, 1:2]).then_inc(S("ta"), 1)

        def mix_gated(v, c):
            v.wait_ge(S("ta"), c + 1)
            v.scalar_tensor_tensor(out=m2[:], in0=ta[:], scalar=1.0, in1=DF[:], op0=ALU.add, op1=ALU.mult)\
                .then_inc(S("m2"), 1)

        def mix_sum(v, c):
            v.wait_ge(S("m2"), c + 1)
            v.scalar_tensor_tensor(out=mix[:], in0=m2[:], scalar=0.5, in1=GT[:], op0=ALU.mult, op1=ALU.add)\
                .then_inc(S("mix"), 1)

        def output_tensor(pe, c):
            pe.wait_ge(S("mix"), c + 1)
            nc.tensor.matmul(PE_, ones[0:1, :], ROWS[0:1, 256:384], start=True, stop=False)
            nc.tensor.matmul(PE_, mix[:], w["oT"], start=False, stop=True).then_inc(S("po"), 1)

        def output_residual(v, c):
            v.wait_ge(S("po"), c + 1)
            v.tensor_tensor(x3[:], PE_, X[:, c, :], ALU.add).then_inc(S("x3"), 1)

        def ffn2_transpose(pe, c):
            pe.wait_ge(S("d_ln"), c + 1)
            nc.tensor.transpose(PE_, ld[:], ident).then_inc(S("t2"), 1)

        def ffn2_scalar(act, c):
            act.wait_ge(S("t2"), c + 1)
            nc.scalar.copy(ldT[:], PE_).then_inc(S("t2_out"), 1)

        def ffn2_tensor(pe, c):
            pe.wait_ge(S("t2_out"), c + 1)
            nc.tensor.matmul(PE_, ldT[:], w["tern"], start=True, stop=True).then_inc(S("y2"), 1)

        def ffn2_residual(v, c, k):
            v.wait_ge(S("y2"), c + 1)
            v.wait_ge(S(f"out{k % 2}"), 32 * (c - k % 2) + 16)
            v.tensor_tensor(x4[k % 2][:], PE_, x3[:], ALU.add).then_inc(S("x4"), 1)

        def store(sp, c, k):
            sp.wait_ge(S("x4"), c + 1)
            for b in range(BATCH):
                sp.dma_start(out[b].rearrange("(c t) d -> t c d", t=TC)[:, c, :], x4[k % 2][TC * b:TC * b + TC, :])\
                    .then_inc(S(f"out{k % 2}"), 16)

        WARM = [3]*TC
        FIRST, LAST = 7, CHUNKS - 1

        def turns(eng, body):
            for i in range(FIRST):
                body(i, i % 4, i)
            with eng.Fori(FIRST, LAST - 3, 4) as i:
                for n in range(4):
                    body(i + n, (FIRST + n) % 4, FIRST)
            for i in range(LAST, TURNS):
                body(i, i % 4, i)

        def alive(ii, lag):
            return 0 <= ii - lag < CHUNKS

        @block.tensor
        def _(pe):
            pe.wait_ge(S("consts"), 48)
            for p in range(2):
                pe.wait_ge(S(f"out{p}"), 16)
            pe.wait_ge(S("mats"), 16)
            pe.wait_ge(S("zeros"), 1)
            for p in range(2):
                nc.tensor.matmul(Z[p][:, 256:512], zeros[:, 0:128], zeros[:], start=True, stop=False,
                                 skip_group_check=True)
            norm_tensor(pe, 0, 0)
            bias_tensor(pe, 0)
            scan_input(pe, 0, 0, 0, 0, False)
            scan_input(pe, 0, 0, 0, 0, True)
            weights_tensor(pe)

            def turn(i, m, ii):
                p, kp, ka = m % 2, (m - PROJ) % 4, (m - ATTN) % 4
                front, proj, attn, tail = (alive(ii, x) for x in (FRONT, PROJ, ATTN, TAIL))
                f, q, c, e = i - FRONT, i - PROJ, i - ATTN, i - TAIL
                qq, cc, ee = ii - PROJ, ii - ATTN, ii - TAIL
                for t in range(TC):
                    if ii < SCAN_TURNS:
                        scan_tensor(pe, i, p, ii, t)
                        keep_warm(pe, p, WARM[t])
                    if ii + 1 < CHUNKS and t == 22:
                        norm_tensor(pe, i + 1, ii + 1)
                    if ii + 1 < SCAN_TURNS:
                        if t == 22:
                            bias_tensor(pe, 1 - p)
                        if t == 23:
                            scan_input(pe, i + 1, ii + 1, 1 - p, 1, False)
                        if t == 24:
                            scan_input(pe, i + 1, ii + 1, 1 - p, 0, False)
                        if t == 25:
                            scan_input(pe, i + 1, ii + 1, 1 - p, 0, True)
                            scan_input(pe, i + 1, ii + 1, 1 - p, 1, True)
                    if tail:
                        if t == 3:
                            gate_tensor(pe, e, ee)
                        if t == 7:
                            alpha_tensor(pe, e)
                        if t == 11:
                            output_tensor(pe, e)
                        if t == 18:
                            ffn2_transpose(pe, e)
                        if t == 20:
                            ffn2_tensor(pe, e)
                    if proj and t == 12:
                        gate_x_tensor(pe, q)
                    if front:
                        if t == 0:
                            cell_tensor(pe, f)
                        if t == 12:
                            ffn1_transpose(pe, f)
                        if t == 14:
                            ffn1_tensor(pe, f)
                        if t == 23:
                            means_tensor(pe, f, 0)
                        if t == 25:
                            means_tensor(pe, f, 1)
                    if proj:
                        if t == 4:
                            values_tensor(pe, q, qq)
                        if t == 7:
                            queries_tensor(pe, q)
                        if t == 16:
                            keys_tensor(pe, q, qq)
                        if t == 20:
                            rows_tensor(pe, q, qq, kp, 0)
                        if t == 28:
                            rows_tensor(pe, q, qq, kp, 1)
                    if attn:
                        R = blocks_of(cc)
                        if t in (1, 2, 5) and (1, 2, 5).index(t) < R:
                            local_scores(pe, c, cc, ka, (1, 2, 5).index(t))
                        if t in (3, 8, 12, 15, 19):
                            past_tensor(pe, c, cc, ka, (3, 8, 12, 15, 19).index(t))
                        if t in (6, 9, 14, 18, 22):
                            level_scores(pe, c, cc, ka, (6, 9, 14, 18, 22).index(t))
                        if t in (10, 13, 17, 21, 25):
                            own_tensor(pe, c, cc, ka, (10, 13, 17, 21, 25).index(t))
                        if t in (11, 24):
                            increase_tensor(pe, c, cc, ka, (11, 24).index(t))
                        if t in (26, 27, 28) and t - 26 < R:
                            local_tensor(pe, c, cc, ka, t - 26)
            turns(pe, turn)

        @block.scalar
        def _(act):
            act.wait_ge(S("v_init"), 2)
            norm_scalar(act, 0)
            for n in range(3):
                cand_scalar(act, 0, 0, 0, n)
            weights_scalar(act)

            def turn(i, m, ii):
                p, kp = m % 2, (m - PROJ) % 4
                front, proj, attn, tail = (alive(ii, x) for x in (FRONT, PROJ, ATTN, TAIL))
                f, q, c, e = i - FRONT, i - PROJ, i - ATTN, i - TAIL
                cc = ii - ATTN
                for t in range(TC):
                    if ii < SCAN_TURNS:
                        scan_scalar(act, i, p, ii, t)
                    if ii + 1 < CHUNKS and t == 23:
                        norm_scalar(act, i + 1)
                    if ii + 1 < SCAN_TURNS and t in (27, 28, 29):
                        cand_scalar(act, i + 1, ii + 1, 1 - p, t - 27)
                    if tail:
                        if t == 5:
                            gate_tanh(act, e)
                        if t == 8:
                            alpha_scalar(act, e)
                        if t == 19:
                            ffn2_scalar(act, e)
                    if proj and t == 13:
                        gate_x_scalar(act, q, ii - PROJ, kp)
                    if front:
                        if t == 1:
                            cell_scalar(act, f)
                        if t == 2:
                            cell_scalar_2(act, f)
                        if t == 13:
                            ffn1_scalar(act, f)
                        if t == 24:
                            means_scalar(act, f, 0)
                        if t == 26:
                            means_scalar(act, f, 1)
                    if proj:
                        if t in (5, 6):
                            values_scalar(act, q, kp, (2 * t - 10, 2 * t - 9))
                        if t == 8:
                            queries_copy(act, q)
                        if t in (8, 9, 10, 11):
                            queries_expand(act, q, ii - PROJ, range(4 * t - 32, 4 * t - 28))
                        if t == 9:
                            exponential(act, q, True)
                        if t == 17:
                            local_scalar(act, q, kp)
                        if t == 18:
                            exponential(act, q, False)
                        if t in (21, 22):
                            rows_scalar(act, q, kp, t - 21)
                        if t == 29:
                            rows_scalar(act, q, kp, 2)
                    if attn and t in (15, 16, 17, 18):
                        local_exp(act, c, cc, range(4 * t - 60, 4 * t - 56))
            turns(act, turn)

        @block.vector
        def _(v):
            for p in range(2):
                v.memset(TH[p][:], 0.0).then_inc(S("v_init"), 1)
            v.memset(zeros[:], 0.0).then_inc(S("zeros"), 1)
            v.wait_ge(S("consts"), 48)
            for p in range(2):
                v.wait_ge(S(f"out{p}"), 16)
            for l in range(2):
                v.tensor_scalar(HH[1][:, TC, 4 * l:4 * l + 4, 1], ones[:, 0:4], COLS[:, l:l + 1], None,
                                ALU.mult).then_inc(S("v_init"), 1)
            v.tensor_scalar(G1[:], G1[:], 1.0, None, ALU.add).then_inc(S("v_init"), 1)
            v.wait_ge(S("x_in"), 64)
            norm_stats(v, 0)
            norm_aggregate(v, 0)
            norm_epsilon(v, 0)
            norm_apply(v, 0)
            norm_floor(v, 0)
            v.wait_ge(S("v_init"), 5)
            norm_rms(v, 0)
            norm_residual(v, 0)
            v.wait_ge(S("nh"), 1)
            halves(v, 0, HH[1][:, TC, :, 1], NH[0][:, 0, :], slice(0, 4))
            weights_vector(v)

            def turn(i, m, ii):
                p, kp, ke = m % 2, (m - PROJ) % 4, (m - TAIL) % 4
                front, proj, attn, tail = (alive(ii, x) for x in (FRONT, PROJ, ATTN, TAIL))
                f, q, c, e = i - FRONT, i - PROJ, i - ATTN, i - TAIL
                cc = ii - ATTN
                for t in range(TC):
                    if ii < SCAN_TURNS:
                        scan_vector(v, i, p, ii, t)
                    if ii + 1 < CHUNKS:
                        if t == 1:
                            norm_stats(v, i + 1)
                        if t == 2:
                            norm_aggregate(v, i + 1)
                        if t == 3:
                            norm_epsilon(v, i + 1)
                        if t == 5:
                            norm_apply(v, i + 1)
                        if t == 7:
                            norm_floor(v, i + 1)
                        if t == 11:
                            norm_rms(v, i + 1)
                        if t == 13:
                            norm_residual(v, i + 1)
                    if tail:
                        if t == 0:
                            levels_sum(v, e)
                        if t == 1:
                            outputs_turn(v, e)
                        if t == 2:
                            difference(v, e)
                        if t == 4:
                            gate_sum(v, e, ke % 2)
                        if t == 5:
                            gate_biased(v, e)
                        if t == 6:
                            gate_silu(v, e)
                        if t == 9:
                            mix_gated(v, e)
                        if t == 10:
                            mix_sum(v, e)
                        if t == 12:
                            output_residual(v, e)
                        if t == 13:
                            ln_stats(v, e, "d", x3[:], "x3")
                        if t == 14:
                            ln_aggregate(v, e, "d")
                        if t == 15:
                            ln_epsilon(v, e, "d")
                        if t == 17:
                            ln_apply(v, e, "d", x3[:], ld[:], "t2")
                        if t == 21:
                            ffn2_residual(v, e, ke)
                    if front:
                        if t == 3:
                            cell_difference(v, f)
                        if t == 4:
                            cell_gated(v, f)
                        if t == 5:
                            cell_residual(v, f)
                        if t == 6:
                            ln_stats(v, f, "a", X[:, f, :], "x1")
                        if t == 7:
                            ln_aggregate(v, f, "a")
                        if t == 8:
                            ln_epsilon(v, f, "a")
                        if t == 11:
                            ln_apply(v, f, "a", X[:, f, :], la[:], "t1")
                        if t == 15:
                            ffn1_residual(v, f)
                        if t == 16:
                            ln_stats(v, f, "b", X[:, f, :], "x2")
                        if t == 17:
                            ln_aggregate(v, f, "b")
                        if t == 18:
                            ln_epsilon(v, f, "b")
                        if t == 20:
                            ln_apply(v, f, "b", X[:, f, :], xb[:], "xm_b")
                    if proj:
                        if t == 8:
                            minimum(v, q, True)
                        if t == 11:
                            features(v, q, kp, True)
                        if t == 17:
                            minimum(v, q, False)
                        if t == 19:
                            features(v, q, kp, False)
                    if attn:
                        R = blocks_of(cc)
                        if t == 2:
                            local_mask(v, c, cc, 0)
                        if t == 3 and R > 1:
                            local_turn(v, c, cc, 1)
                        if t == 4:
                            local_turn(v, c, cc, 0)
                        if t == 6 and R > 2:
                            local_mask(v, c, cc, 2)
                        if t in (7, 10, 15, 19, 23):
                            mask_vector(v, c, cc, (7, 10, 15, 19, 23).index(t))
                        if t == 9 and R > 2:
                            local_turn(v, c, cc, 2)
                        if t in (12, 13):
                            local_max(v, c, cc, t - 12)
                        if t == 14:
                            local_shift(v, c)
                        if t in (14, 25):
                            increase_vector(v, c, cc, (14, 25).index(t))
                        if t in (20, 21, 22) and t - 20 < R:
                            local_back(v, c, cc, t - 20)
                        if t in (28, 29, 30, 31):
                            weigh(v, c, t - 28)
            turns(v, turn)

        @block.gpsimd
        def _(g):
            g.wait_ge(S("consts"), 48)
            norm_root(g, 0)
            norm_root_2(g, 0)

            def turn(i, m, ii):
                p, kp = m % 2, (m - PROJ) % 4
                front, proj, attn, tail = (alive(ii, x) for x in (FRONT, PROJ, ATTN, TAIL))
                f, q, c, e = i - FRONT, i - PROJ, i - ATTN, i - TAIL
                cc = ii - ATTN
                if attn and cc >= 1 or tail:
                    g.wait_ge(S("st"), 8 * c)
                if front:
                    copy_states(g, i, f, 1 - p)
                if ii + 1 < CHUNKS:
                    norm_root(g, i + 1)
                    norm_root_2(g, i + 1)
                if front:
                    ln_root(g, f, "a")
                if proj:
                    queries_pool(g, q, kp, (0, 1, 2, 3))
                if tail:
                    ln_root(g, e, "d")
                if front:
                    ln_root(g, f, "b")
                if attn:
                    if front:
                        g.wait_ge(S("b_rs"), f + 1)
                    else:
                        g.wait_ge(S("d_rs"), e + 1)
                    for n in range(2):
                        state_pool(g, c, cc, n)
            turns(g, turn)

        @block.sync
        def _(sp):
            sp.dma_start(C[:], ins["consts"]).then_inc(S("consts"), 16)
            for b in range(BATCH):
                sp.dma_start(X[TC * b:TC * b + TC, :, :],
                             ins["x"][b].rearrange("(c t) d -> t c d", t=TC)).then_inc(S("x_in"), 16)
            sp.dma_start(G1[:], ins["gamma_rows"]).then_inc(S("consts"), 16)
            sp.dma_start(COLS[:], ins["cols"]).then_inc(S("consts"), 16)
            sp.dma_start(ROWS[0:1, :], ins["rows"][0:1, :]).then_inc(S("out0"), 16)
            sp.dma_start(ROWS[1:2, :], ins["rows"][1:2, :]).then_inc(S("out1"), 16)
            sp.dma_start(W[:], ins["mats"]).then_inc(S("mats"), 16)

            def turn(i, m, ii):
                if alive(ii, TAIL):
                    store(sp, i - TAIL, (m - TAIL) % 4)
            turns(sp, turn)
            for p in range(2):
                sp.wait_ge(S(f"out{p}"), 32 * CHUNKS + 16)


def kernel(**inputs):
    import numpy as np
    import concourse.bacc as bacc
    from concourse.bass_utils import run_bass_kernel_spmd

    a = {k: np.asarray(v) for k, v in inputs.items()}
    A, B_ = "L0_attn_a_", "L0_attn_b_"
    lWi, lWif, lWhf = a[A + "lWi"], a[A + "lWif"], a[A + "lWhf"]
    Wg = a[B_ + "Wg"]
    hk, hv = a[B_ + "haar_Wk"], a[B_ + "haar_Wv"]
    mats = {"i1": lWi[0].T, "f1": lWif[0].T, "r1": lWhf[0].T, "i2": lWi[1].T, "f2": lWif[1].T, "r2": lWhf[1].T,
            "gi": a[A + "gWi"].T, "gf": a[A + "gWif"].T, "gh": a[A + "gWhf"].T,
            "wk": a[B_ + "Wk"], "wv": a[B_ + "Wv"], "qT": a[B_ + "Wq"].T, "klT": a[B_ + "Wkl"].T,
            "vlT": a[B_ + "Wvl"].T, "kT": a[B_ + "Wk"].T, "vT": a[B_ + "Wv"].T,
            "g1T": Wg[:, 0:D].T, "g2T": Wg[:, D:].T, "oT": a[B_ + "Wo"].T, "tern": a["L0_ffn_weight"].T,
            "go": np.broadcast_to(a[B_ + "Wgo"].reshape(D, 1), (D, D))}
    for l in range(4):
        for n, m in (("hk", hk), ("hv", hv)):
            mats[f"{n}{l}"] = np.broadcast_to(m[l].T[None, :, None, :], (HEADS, DH, HEADS, DH)).reshape(D, D)
    mats = np.ascontiguousarray(np.concatenate([mats[n] for n in MATS], axis=1))
    cols = np.concatenate([a[A + "l_init_hidden"].T, a[B_ + "bg"].reshape(D, 1),
                           np.broadcast_to(a[B_ + "bgo"].reshape(1, 1), (D, 1)),
                           np.broadcast_to(a[B_ + "haar_scale"].reshape(1, 4), (D, 4)),
                           np.zeros((D, 4), np.float32)], axis=1)
    rows = np.zeros((2, 5 * 128 + 256), np.float32)
    rows[0:2, 0:128] = a[A + "lbhf"]
    rows[0, 128:256] = a[A + "gbhf"]
    rows[0, 256:384] = a[B_ + "bo"]
    rows[:, 640:896] = np.tile(np.repeat(np.eye(2, dtype=np.float32), BATCH, axis=1), (1, TC))
    s, t = np.arange(TC)[:, None], np.arange(TC)[None, :]
    means = np.zeros((128, LEVELS, 128), np.float32)
    for l in range(LEVELS):
        size = 2 ** l
        m = ((s <= t) & (s >= t // size * size)) / (t % size + 1.0)
        for b in range(BATCH):
            means[TC * b:TC * b + TC, l, TC * b:TC * b + TC] = m
    causal = np.tile((s <= t).astype(np.float32), (BATCH, 1))
    add = np.concatenate([np.where(s <= t, 0.0, NEG), np.zeros((TC, TC)), np.where(s > t, 0.0, NEG)], axis=1)
    consts = np.concatenate([np.eye(128), means.reshape(128, -1), causal,
                             np.repeat(np.eye(HEADS), DH, axis=0), np.repeat(np.eye(BATCH), TC, axis=0),
                             np.tile(np.repeat(np.eye(HG), DH, axis=0), (HG, 1)),
                             np.tile(add, (BATCH, 1)), np.full((128, 2), -0.5), np.ones((128, 128))],
                            axis=1).astype(np.float32)
    arrays = {"x": a[A + "x"], "gamma_rows": np.ascontiguousarray(np.broadcast_to(a[A + "gamma"][None], (128, D))),
              "cols": np.ascontiguousarray(cols), "rows": rows, "mats": mats, "consts": np.ascontiguousarray(consts)}
    nc = bacc.Bacc("TRN2", target_bir_lowering=False, num_devices=1)
    ins = {n: nc.dram_tensor("in_" + n, v.shape, mybir.dt.from_np(v.dtype), kind="ExternalInput").ap()
           for n, v in arrays.items()}
    out = nc.dram_tensor("out_0", (BATCH, TOKENS, D), F32, kind="ExternalOutput").ap()
    build(nc, ins, out)
    r = run_bass_kernel_spmd(nc, [{"in_" + n: v for n, v in arrays.items()}], core_ids=[0])
    return r.results[0]["out_0"]
```

```python
from contextlib import ExitStack

import concourse.bass as bass
from concourse import mybir

ALU = mybir.AluOpType
ACT = mybir.ActivationFunctionType
AX = mybir.AxisListType
F32 = mybir.dt.float32

BATCH, TOKENS, D = 4, 1024, 128
TC = 32
CHUNKS = TOKENS // TC
HEADS, DH = 16, 8
E9 = DH + 1
HG = 4
LEVELS = 5
LAG = 2
SCAN_TURNS = CHUNKS + LAG
FRONT = 3
PROJ = 4
ATTN = 5
TAIL = 6
TURNS = CHUNKS + TAIL
SV = BATCH * E9
OW = BATCH * HG * E9
NEG = -1.0e30
LN_EPS = 1.0e-5
ROUND = 1.5 * 2.0 ** 23
NORM_FLOOR = 1.0e-24 / D

MATS = ["i1", "f1", "r1", "i2", "f2", "r2", "gi", "gf", "gh", "wk", "wv", "qT", "klT", "vlT", "kT", "vT",
        "g1T", "g2T", "oT", "tern", "go"] + [f"hk{l}" for l in range(4)] + [f"hv{l}" for l in range(4)]
CONSTS = {"ident": 128, "means": LEVELS * 128, "causal": TC, "hmask": HEADS, "bmask": BATCH, "gmask": HG,
          "addmask": 3 * TC, "neghalf": 2, "ones": 128}


def build(nc, ins, out):
    with ExitStack() as ctx:
        def sb(name, shape):
            return ctx.enter_context(nc.sbuf_tensor(name, shape, F32))

        def ps(name, shape=(128, 512)):
            return ctx.enter_context(nc.psum_tensor(name, list(shape), F32))

        sems = {}

        def S(name):
            if name not in sems:
                sems[name] = ctx.enter_context(nc.semaphore(name))
            return sems[name]

        W = sb("W", [128, len(MATS) * 128])
        w = {n: W[:, 128 * k:128 * k + 128] for k, n in enumerate(MATS)}
        C = sb("C", [128, sum(CONSTS.values())])
        c_, at = {}, 0
        for n, k in CONSTS.items():
            c_[n] = C[:, at:at + k]
            at += k
        COLS = sb("COLS", [128, 12])
        ROWS = sb("ROWS", [2, 5 * 128 + 256])
        G1 = sb("G1", [128, 128])
        X = sb("X", [128, CHUNKS, 128])
        xn = sb("xn", [128, 128])
        XNT = sb("XNT", [128, CHUNKS, 128])
        GX = [sb(f"GX{p}", [128, 128]) for p in range(2)]
        HH = [sb(f"HH{p}", [128, TC + 1, 8, 2]) for p in range(2)]
        EF = [sb(f"EF{p}", [128, 8, 2]) for p in range(2)]
        TH = [sb(f"TH{p}", [128, 8, 2]) for p in range(2)]
        NH = [sb(f"NH{p}", [128, TC, 8]) for p in range(2)]
        TN = [sb(f"TN{p}", [128, TC, 8]) for p in range(2)]
        st = sb("st", [128, 6])
        sm = sb("sm", [128, 16])
        xl = sb("xl", [128, 128])

        wtmp = sb("wtmp", [128, 128])
        ws = sb("ws", [128, 18])
        hb = sb("hb", [128, 2])
        WL = sb("WL", [128, 6, BATCH * HG])
        WKL = W[:, 128 * MATS.index("hk0"):128 * MATS.index("hk0") + 512]
        WVL = W[:, 128 * MATS.index("hv0"):128 * MATS.index("hv0") + 512]
        lnb = {n: sb("ln_" + n, [128, 10]) for n in "abd"}
        VE = [sb(f"VE{p}", [128, LEVELS, HEADS, BATCH, E9]) for p in range(2)]
        VEL = [sb(f"VEL{p}", [128, HEADS, BATCH, E9]) for p in range(4)]
        KL = [sb(f"KL{p}", [128, 128]) for p in range(4)]
        KP = [sb(f"KP{p}", [128, 768]) for p in range(2)]
        KR = [sb(f"KR{p}", [128, 640]) for p in range(2)]
        QL = sb("QL", [128, BATCH, HEADS, TC])
        QG = [sb(f"QG{p}", [128, BATCH, HEADS, TC]) for p in range(2)]
        ST = sb("ST", [128, LEVELS, HEADS, BATCH, E9])
        DT = sb("DT", [128, LEVELS, HG * SV])
        qr = sb("qr", [128, 128])
        zeros = ctx.enter_context(nc.sbuf_tensor("zeros", [128, 256], mybir.dt.bfloat16))
        A = [sb(f"A{p}", [128, HEADS, TC]) for p in range(2)]
        SL, SR = sb("SL", [128, 3, HEADS, TC]), sb("SR", [128, 3, HEADS, TC])
        lmx, nmx = sb("lmx", [128, HEADS]), sb("nmx", [128, HEADS])
        RN, GO = sb("RN", [128, 96]), sb("GO", [128, 96, DH])
        GS, LT, GT, DF, h2s, xts, cd, la, laT, xb, gu, gu2, gt_, sg, ta, m2, mix, x3, ld, ldT = (
            sb(n, [128, 128]) for n in ("GS LT GT DF h2s xts cd la laT xb gu gu2 gt_ sg ta m2 mix x3 ld ldT").split())
        x4 = [sb(f"x4{p}", [128, 128]) for p in range(2)]
        ct = sb("ct", [128, 384])
        XM = sb("XM", [128, 640])
        EX = sb("EX", [128, 768])

        Z = [ps(f"Z{p}") for p in range(2)]
        PB = ps("PB")
        FR = ps("FR")
        RG = [ps(f"RG{p}") for p in range(2)]
        OB = ps("OB", (128, 2, 512))
        PN, PT, PE_ = PB[:, 0:256], PB[:, 256:384], PB[:, 384:512]

        ident, ones = c_["ident"], c_["ones"]
        zv = [Z[p][:, 0:256].rearrange("p (t l b) -> p t l b", l=2, b=4) for p in range(2)]
        pnv = PN.rearrange("p (t l b) -> p t l b", l=2, b=4)

        block = ctx.enter_context(nc.Block())

        def weights_vector(v):
            tern = w["tern"]
            v.wait_ge(S("mats"), 16)
            v.scalar_tensor_tensor(out=wtmp[:], in0=tern, scalar=-1.0, in1=tern, op0=ALU.mult, op1=ALU.max)\
                .then_inc(S("w1"), 1)
            v.wait_ge(S("w1"), 1)
            v.tensor_reduce(ws[:, 0:1], wtmp[:], AX.X, ALU.add).then_inc(S("w2"), 1)
            for n in ["hk0", "hk1", "hk2", "hk3", "hv0", "hv1", "hv2", "hv3"]:
                blk = w[n].rearrange("p (h e) -> p h e", e=DH)
                v.tensor_tensor(blk, blk, c_["hmask"].rearrange("p (h o) -> p h o", o=1).broadcast_to([128, HEADS, DH]),
                                ALU.mult).then_inc(S("w_blk"), 1)
            v.wait_ge(S("w_tot"), 1)
            v.tensor_scalar(ws[:, 1:2], PE_[:, 0:1], 1.0 / (D * D), LN_EPS, ALU.mult, ALU.max).then_inc(S("w3"), 1)
            v.wait_ge(S("w3"), 1)
            v.reciprocal(ws[:, 2:3], ws[:, 1:2]).then_inc(S("w4"), 1)
            v.wait_ge(S("w4"), 1)
            v.tensor_scalar(wtmp[:], tern, ws[:, 2:3], None, ALU.mult).then_inc(S("w5"), 1)
            v.wait_ge(S("w5"), 1)
            v.tensor_scalar(wtmp[:], wtmp[:], ROUND, None, ALU.add).then_inc(S("w5"), 1)
            v.wait_ge(S("w5"), 2)
            v.tensor_scalar(wtmp[:], wtmp[:], ROUND, None, ALU.subtract).then_inc(S("w5"), 1)
            v.wait_ge(S("w5"), 3)
            v.tensor_scalar(wtmp[:], wtmp[:], 1.0, -1.0, ALU.min, ALU.max).then_inc(S("w5"), 1)
            v.wait_ge(S("w5"), 4)
            v.tensor_scalar(tern, wtmp[:], ws[:, 1:2], None, ALU.mult).then_inc(S("w_tern"), 1)
            hs = COLS[:, 4:8]
            v.tensor_reduce(ws[:, 3:4], hs, AX.X, ALU.max).then_inc(S("w6"), 1)
            v.wait_ge(S("w6"), 1)
            v.tensor_scalar(ws[:, 4:8], hs, ws[:, 3:4], None, ALU.subtract).then_inc(S("w6"), 1)
            v.wait_ge(S("w_exp"), 1)
            v.tensor_reduce(ws[:, 12:13], ws[:, 8:12], AX.X, ALU.add).then_inc(S("w6"), 1)
            v.wait_ge(S("w6"), 3)
            v.reciprocal(ws[:, 13:14], ws[:, 12:13]).then_inc(S("w6"), 1)
            v.wait_ge(S("w6"), 4)
            v.tensor_scalar(ws[:, 14:18], ws[:, 8:12], ws[:, 13:14], None, ALU.mult).then_inc(S("w6"), 1)
            v.memset(WL[:], 1.0).then_inc(S("w6"), 1)
            v.wait_ge(S("w6"), 6)
            for l in range(1, LEVELS):
                v.tensor_scalar(WL[:, l, :], WL[:, l, :], ws[:, 13 + l:14 + l], None, ALU.mult).then_inc(S("w7"), 1)
            v.tensor_scalar(hb[:], COLS[:, 2:4], 0.5, None, ALU.mult).then_inc(S("w7"), 1)
            v.memset(ST[:], 0.0).then_inc(S("st0"), 1)
            for p in range(2):
                v.memset(VE[p][:], 1.0).then_inc(S("w7"), 1)
            for p in range(4):
                v.memset(VEL[p][:], 1.0).then_inc(S("w7"), 1)
            v.wait_ge(S("w7"), 11)
            for t_ in [VE[p][:, l] for p in range(2) for l in range(LEVELS)] + [VEL[p][:] for p in range(4)]:
                v.tensor_tensor(t_, t_, c_["bmask"].rearrange("p (o b q) -> p o b q", o=1, q=1).broadcast_to(
                    [128, HEADS, BATCH, E9]), ALU.mult).then_inc(S("w8"), 1)

        def weights_tensor(pe):
            pe.wait_ge(S("w2"), 1)
            nc.tensor.matmul(PE_[:, 0:1], ones, ws[:, 0:1], start=True, stop=True).then_inc(S("w_tot"), 1)
            pe.wait_ge(S("w_blk"), 8)
            for n in range(4):
                nc.tensor.matmul(FR[:, 128 * n:128 * n + 128], w["wk"], w[f"hk{n}"], start=True, stop=True)
            for n in range(4):
                mm = nc.tensor.matmul(RG[0][:, 128 * n:128 * n + 128], w["wv"], w[f"hv{n}"], start=True, stop=True)
            mm.then_inc(S("w_lev"), 1)

        def weights_scalar(act):
            act.wait_ge(S("w6"), 2)
            nc.scalar.activation(ws[:, 8:12], ws[:, 4:8], ACT.Exp).then_inc(S("w_exp"), 1)
            act.wait_ge(S("w_lev"), 1)
            nc.scalar.copy(WKL, FR[:]).then_inc(S("w_kvl"), 1)
            nc.scalar.copy(WVL, RG[0][:]).then_inc(S("w_kvl"), 1)

        def wk_of(l):
            return w["kT"] if l == 0 else WKL[:, 128 * l - 128:128 * l]

        def wv_of(l):
            return w["vT"] if l == 0 else WVL[:, 128 * l - 128:128 * l]

        def later(c):
            return not isinstance(c, int) or c >= 1

        def ln_stats(v, c, tag, src, ready):
            v.wait_ge(S("v_init"), 2)
            v.wait_ge(S(ready), c + 1)
            v.bn_stats(lnb[tag][:, 0:6], src).then_inc(S(tag + "_st"), 1)

        def ln_aggregate(v, c, tag):
            v.wait_ge(S(tag + "_st"), c + 1)
            v.sem_inc(S("alone"), 1)
            v.bn_aggr(lnb[tag][:, 6:8], lnb[tag][:, 0:6]).then_inc(S(tag + "_ag"), 1)

        def ln_epsilon(v, c, tag):
            v.wait_ge(S(tag + "_ag"), c + 1)
            v.tensor_scalar(lnb[tag][:, 8:9], lnb[tag][:, 7:8], LN_EPS, None, ALU.add).then_inc(S(tag + "_ve"), 1)

        def ln_root(g, c, tag):
            g.wait_ge(S(tag + "_ve"), c + 1)
            g.tensor_tensor(lnb[tag][:, 9:10], lnb[tag][:, 8:9], c_["neghalf"][:, 0:1], ALU.pow)\
                .then_inc(S(tag + "_rs"), 1)

        def ln_apply(v, c, tag, src, dst, used):
            v.wait_ge(S(tag + "_rs"), c + 1)
            v.wait_ge(S(used), c)
            v.tensor_scalar(dst, src, lnb[tag][:, 6:7], lnb[tag][:, 9:10], ALU.subtract, ALU.mult)\
                .then_inc(S(tag + "_ln"), 1)

        def layers(i):
            return slice(0 if i < CHUNKS else 4, 8 if i >= LAG else 4)

        def scan_tensor(pe, i, p, ii, t):
            if ii or t:
                pe.wait_ge(S("h"), i * TC + t)
            else:
                pe.wait_ge(S("v_init"), 5)
            prev = HH[p][:, t, :, 1] if t else HH[1 - p][:, TC, :, 1]
            for lay in range(2):
                if layers(ii).start <= 4 * lay < layers(ii).stop:
                    for m in range(0, 128, 32):
                        mm = nc.tensor.matmul(Z[p][m:m + 32, 8 * t + 4 * lay:8 * t + 4 * lay + 4],
                                              w[f"r{lay + 1}"][:, m:m + 32], prev[:, 4 * lay:4 * lay + 4],
                                              start=False, stop=False, skip_group_check=True)
            mm.then_inc(S("z"), 1)

        def keep_warm(pe, p, n):
            for _ in range(n):
                nc.tensor.matmul(Z[1 - p][:, 256:512], zeros[:, 0:128], zeros[:], start=False,
                                 stop=False, skip_group_check=True)

        def scan_scalar(act, i, p, ii, t):
            cols = layers(ii)
            act.wait_ge(S("z"), i * TC + t + 1)
            nc.scalar.activation(TH[t % 2][:, cols, 1], Z[p][:, 8 * t + cols.start:8 * t + cols.stop],
                                 ACT.Tanh, scale=0.5).then_inc(S("th"), 1)

        def halves(v, n, hprev, nh, cols):
            v.scalar_tensor_tensor(out=EF[n % 2][:, cols, 0], in0=hprev[:, cols], scalar=-0.5, in1=nh[:, cols],
                                   op0=ALU.mult, op1=ALU.add)
            v.scalar_tensor_tensor(out=EF[n % 2][:, cols, 1], in0=hprev[:, cols], scalar=0.5, in1=nh[:, cols],
                                   op0=ALU.mult, op1=ALU.add).then_inc(S("ef"), 1)

        def scan_vector(v, i, p, ii, t):
            cols = layers(ii)
            flat = lambda a: a.rearrange("p a b -> p (a b)")
            v.wait_ge(S("th"), i * TC + t + 1)
            v.wait_ge(S("ef"), i * TC + t + 1)
            if t == 0 and ii >= LAG + 2:
                v.wait_ge(S("h2"), i - LAG - 1)
            v.tensor_tensor_scan(out=flat(HH[p][:, t + 1, cols, :]), data0=flat(TH[t % 2][:, cols, :]),
                                 data1=flat(EF[t % 2][:, cols, :]), initial=0.0, op0=ALU.mult,
                                 op1=ALU.add).then_inc(S("h"), 1)
            v.wait_ge(S("h"), i * TC + t + 1)
            if t < TC - 1:
                halves(v, t + 1, HH[p][:, t + 1, :, 1], NH[p][:, t + 1, :], cols)
            elif ii < SCAN_TURNS - 1:
                v.wait_ge(S("nh"), i + 2)
                halves(v, 0, HH[p][:, TC, :, 1], NH[1 - p][:, 0, :], layers(ii + 1))

        def norm_stats(v, c):
            v.bn_stats(st[:], X[:, c, :]).then_inc(S("n_st"), 1)

        def norm_aggregate(v, c):
            v.wait_ge(S("n_st"), c + 1)
            v.sem_inc(S("alone"), 1)
            v.bn_aggr(sm[:, 0:2], st[:]).then_inc(S("n_ag"), 1)

        def norm_epsilon(v, c):
            v.wait_ge(S("n_ag"), c + 1)
            v.tensor_scalar(sm[:, 2:3], sm[:, 1:2], LN_EPS, None, ALU.add).then_inc(S("n_ve"), 1)

        def norm_root(g, c):
            g.wait_ge(S("n_ve"), c + 1)
            g.tensor_tensor(sm[:, 3:4], sm[:, 2:3], c_["neghalf"][:, 0:1], ALU.pow).then_inc(S("n_rs"), 1)

        def norm_apply(v, c):
            v.wait_ge(S("n_rs"), c + 1)
            if later(c):
                v.wait_ge(S("n_r2"), c)
            v.tensor_scalar(xl[:], X[:, c, :], sm[:, 0:1], sm[:, 3:4], ALU.subtract, ALU.mult).then_inc(S("n_xl"), 1)
            v.scalar_tensor_tensor(out=sm[:, 4:5], in0=sm[:, 1:2], scalar=sm[:, 3:4], in1=sm[:, 3:4],
                                   op0=ALU.mult, op1=ALU.mult).then_inc(S("n_v2"), 1)

        def norm_floor(v, c):
            v.wait_ge(S("n_v2"), c + 1)
            v.tensor_scalar(sm[:, 5:6], sm[:, 4:5], NORM_FLOOR, None, ALU.max).then_inc(S("n_mx"), 1)

        def norm_root_2(g, c):
            g.wait_ge(S("n_mx"), c + 1)
            g.tensor_tensor(sm[:, 6:7], sm[:, 5:6], c_["neghalf"][:, 0:1], ALU.pow).then_inc(S("n_rn"), 1)

        def norm_rms(v, c):
            v.wait_ge(S("n_rn"), c + 1)
            v.wait_ge(S("n_xl"), c + 1)
            v.wait_ge(S("n_t"), c)
            v.scalar_tensor_tensor(out=xn[:], in0=xl[:], scalar=sm[:, 6:7], in1=G1[:],
                                   op0=ALU.mult, op1=ALU.mult).then_inc(S("n_xn"), 1)

        def norm_residual(g, c):
            g.wait_ge(S("n_xn"), c + 1)
            g.sem_inc(S("alone_g"), 1)
            g.tensor_tensor(X[:, c, :], X[:, c, :], xl[:], ALU.add).then_inc(S("n_r1"), 1)
            g.wait_ge(S("n_r1"), c + 1)
            g.sem_inc(S("alone_g"), 1)
            g.tensor_tensor(X[:, c, :], X[:, c, :], xn[:], ALU.add).then_inc(S("n_r2"), 1)

        def norm_tensor(pe, c, cc):
            pe.wait_ge(S("n_xn"), c + 1)
            if cc >= TAIL + 1:
                pe.wait_ge(S("x4"), c - TAIL)
            nc.tensor.transpose(PT, xn[:], ident).then_inc(S("n_t"), 1)

        def norm_scalar(act, c):
            act.wait_ge(S("n_t"), c + 1)
            nc.scalar.copy(XNT[:, c, :], PT).then_inc(S("n_xt"), 1)

        def bias_tensor(pe, q):
            for k in range(2):
                nc.tensor.matmul(Z[q][:, 128 * k:128 * k + 128], ROWS[0:2, 0:128],
                                 ROWS[0:2, 640 + 128 * k:768 + 128 * k],
                                 start=(k == 0), stop=False, skip_group_check=True)

        def scan_input(pe, j, jj, q, lay, cand):
            if lay == 0:
                if jj >= CHUNKS:
                    return
                pe.wait_ge(S("n_xt"), j + 1)
                rhs = XNT[:, j, :].rearrange("p (b t) -> p t b", b=BATCH)
            else:
                if jj < LAG:
                    return
                rhs = HH[q][:, 1:TC + 1, 0:4, 1]
            only = 1 if jj >= CHUNKS else 0
            if cand:
                mm = nc.tensor.matmul(pnv[:, :, lay, :], w[f"i{lay + 1}"], rhs, start=(lay == only), stop=False,
                                      skip_group_check=True)
                if lay == (1 if jj >= LAG else 0):
                    mm.then_inc(S("pre_mm"), 1)
            else:
                nc.tensor.matmul(zv[q][:, :, lay, :], w[f"f{lay + 1}"], rhs, start=False, stop=False,
                                 skip_group_check=True)

        def cand_scalar(act, j, jj, q, step):
            lo = layers(jj)
            if step == 0:
                act.wait_ge(S("pre_mm"), j + 1)
                nc.scalar.activation(TN[0][:, :, lo], PN.rearrange("p (t c) -> p t c", c=8)[:, :, lo],
                                     ACT.Tanh).then_inc(S("tn1"), 1)
            if step == 1:
                act.wait_ge(S("tn1"), j + 1)
                nc.scalar.activation(TN[1][:, :, lo], TN[0][:, :, lo], ACT.Tanh).then_inc(S("tn2"), 1)
            if step == 2:
                act.wait_ge(S("tn2"), j + 1)
                nc.scalar.mul(NH[q][:, :, lo], TN[1][:, :, lo], 0.5).then_inc(S("nh"), 1)

        def copy_states(g, i, c, p):
            g.wait_ge(S("h"), i * TC)
            g.wait_ge(S("cell_mm"), c)
            g.sem_inc(S("alone_g"), 1)
            g.tensor_copy(h2s[:].rearrange("p (b t) -> p b t", b=BATCH),
                          HH[p][:, 1:TC + 1, 4:8, 1].rearrange("p t b -> p b t")).then_inc(S("h2"), 1)
            g.tensor_copy(xts[:], XNT[:, c, :]).then_inc(S("f_in"), 1)

        def cell_tensor(pe, c):
            pe.wait_ge(S("h2"), c + 1)
            pe.wait_ge(S("f_in"), c + 1)
            pe.wait_ge(S("kr_out"), c - 1 if later(c) else 0)
            nc.tensor.transpose(FR[:, 256:384], xts[:], ident)
            nc.tensor.matmul(FR[:, 0:128], h2s[:], w["gi"], start=True, stop=True)
            nc.tensor.matmul(FR[:, 128:256], ones[0:1, :], ROWS[0:1, 128:256], start=True, stop=False)
            nc.tensor.matmul(FR[:, 128:256], h2s[:], w["gf"], start=False, stop=False)
            nc.tensor.matmul(FR[:, 128:256], xts[:], w["gh"], start=False, stop=True).then_inc(S("cell_mm"), 1)

        def cell_scalar(act, c):
            act.wait_ge(S("cell_mm"), c + 1)
            act.wait_ge(S("x1"), c)
            nc.scalar.activation(ct[:, 0:128], FR[:, 0:128], ACT.Tanh).then_inc(S("ct1"), 1)
            nc.scalar.activation(ct[:, 256:384], FR[:, 128:256], ACT.Tanh, scale=0.5).then_inc(S("ct2"), 1)

        def cell_scalar_2(act, c):
            act.wait_ge(S("ct1"), c + 1)
            nc.scalar.activation(ct[:, 128:256], ct[:, 0:128], ACT.Tanh).then_inc(S("ct3"), 1)

        def cell_difference(v, c):
            v.wait_ge(S("ct2"), c + 1)
            v.wait_ge(S("ct3"), c + 1)
            v.tensor_tensor(cd[:], ct[:, 128:256], FR[:, 256:384], ALU.subtract).then_inc(S("cd1"), 1)

        def cell_gated(v, c):
            v.wait_ge(S("cd1"), c + 1)
            v.scalar_tensor_tensor(out=cd[:], in0=ct[:, 256:384], scalar=1.0, in1=cd[:], op0=ALU.add,
                                   op1=ALU.mult).then_inc(S("cd2"), 1)

        def cell_residual(v, c):
            v.wait_ge(S("cd2"), c + 1)
            v.wait_ge(S("n_r2"), c + 1)
            v.scalar_tensor_tensor(out=X[:, c, :], in0=cd[:], scalar=0.5, in1=X[:, c, :], op0=ALU.mult,
                                   op1=ALU.add).then_inc(S("x1"), 1)

        def ffn1_transpose(pe, c):
            pe.wait_ge(S("a_ln"), c + 1)
            pe.wait_ge(S("cd1"), c + 1)
            if later(c):
                pe.wait_ge(S("phi_a"), c)
            nc.tensor.transpose(FR[:, 256:384], la[:], ident).then_inc(S("t1"), 1)

        def ffn1_scalar(act, c):
            act.wait_ge(S("t1"), c + 1)
            nc.scalar.copy(laT[:], FR[:, 256:384]).then_inc(S("t1_out"), 1)

        def ffn1_tensor(pe, c):
            pe.wait_ge(S("t1_out"), c + 1)
            if later(c):
                pe.wait_ge(S("gx"), c)
            nc.tensor.matmul(FR[:, 384:512], laT[:], w["tern"], start=True, stop=True).then_inc(S("y1"), 1)

        def ffn1_residual(v, c):
            v.wait_ge(S("y1"), c + 1)
            v.tensor_tensor(X[:, c, :], X[:, c, :], FR[:, 384:512], ALU.add).then_inc(S("x2"), 1)

        def means_tensor(pe, c, part):
            if part == 0:
                pe.wait_ge(S("b_ln"), c + 1)
                pe.wait_ge(S("x2"), c + 1)
                if later(c):
                    pe.wait_ge(S("dd_out"), c)
                nc.tensor.matmul(FR[:], xb[:], c_["means"][:, 0:512], start=True, stop=True).then_inc(S("xm"), 1)
            else:
                pe.wait_ge(S("xm1"), c + 1)
                nc.tensor.matmul(FR[:, 0:128], xb[:], c_["means"][:, 512:640], start=True, stop=True)\
                    .then_inc(S("xm_b"), 1)

        def means_scalar(act, c, part):
            if part == 0:
                act.wait_ge(S("xm"), c + 1)
                act.wait_ge(S("pd"), c)
                nc.scalar.copy(XM[:, 0:512], FR[:]).then_inc(S("xm1"), 1)
            else:
                act.wait_ge(S("xm_b"), c + 1)
                nc.scalar.copy(XM[:, 512:640], FR[:, 0:128]).then_inc(S("xm2"), 1)

        def xm_(l):
            return XM[:, 128 * l:128 * l + 128]

        def values_tensor(pe, c, cc):
            pe.wait_ge(S("xm2"), c + 1)
            if cc < CHUNKS - 1:
                pe.wait_ge(S("cd1"), c + 2)
            elif cc > 0:
                pe.wait_ge(S("kr_out"), c)
            for l in range(4):
                m = nc.tensor.matmul(FR[:, 128 * l:128 * l + 128], xm_(l), wv_of(l), start=True, stop=True)
            m.then_inc(S("pc"), 1)

        def values_scalar(act, c, k, bs):
            act.wait_ge(S("pc"), c + 1)
            for b in bs:
                a = nc.scalar.activation(VE[k % 2][:, 0:4, :, b, 0:DH].rearrange("p l h e -> p (l h) e"),
                                         FR[:].rearrange("p (m e) -> p m e", e=DH), ACT.Copy,
                                         scale=c_["bmask"][:, b:b + 1])
            if b == BATCH - 1:
                a.then_inc(S("ve3"), 1)

        def queries_tensor(pe, c):
            pe.wait_ge(S("ve3"), c + 1)
            for n, (wt, l) in enumerate([(w["qT"], 0)] + [(wk_of(l), l) for l in range(3)]):
                m = nc.tensor.matmul(FR[:, 128 * n:128 * n + 128], wt, xm_(l), start=True, stop=True)
            m.then_inc(S("pa"), 1)

        def queries_copy(act, c):
            act.wait_ge(S("pa"), c + 1)
            act.wait_ge(S("ql"), c)
            nc.scalar.copy(qr[:], FR[:, 0:128]).then_inc(S("qr"), 1)

        def exponential(act, c, first, step):
            part = EX[:, 0:512] if first else EX[:, 512:768]
            tag = "a" if first else "b"
            if step == 0:
                act.wait_ge(S("p" + tag), c + 1)
                nc.scalar.activation(part, FR[:] if first else FR[:, 0:256], ACT.Relu, scale=-1.0)\
                    .then_inc(S("mn" + tag), 1)
            else:
                act.wait_ge(S("mn" + tag), c + 1)
                nc.scalar.activation(part, part, ACT.Exp, scale=-1.0).then_inc(S("e" + tag), 1)

        def features(v, c, k, first):
            p = k % 2
            if first:
                v.wait_ge(S("ea"), c + 1)
                v.scalar_tensor_tensor(out=KP[p][:, 0:512], in0=FR[:], scalar=0.0, in1=EX[:, 0:512], op0=ALU.max,
                                       op1=ALU.add).then_inc(S("phi_a"), 1)
            else:
                v.wait_ge(S("eb"), c + 1)
                v.wait_ge(S("vl"), c + 1)
                v.scalar_tensor_tensor(out=KP[p][:, 512:768], in0=FR[:, 0:256], scalar=0.0, in1=EX[:, 512:768],
                                       op0=ALU.max, op1=ALU.add).then_inc(S("phi_b"), 1)

        def expand_queries(g, src, dst):
            for b in range(BATCH):
                a = g.tensor_tensor(dst[:, b, :, :], src[:, TC * b:TC * b + TC].rearrange("p (o t) -> p o t", o=1)
                                    .broadcast_to([128, HEADS, TC]),
                                    c_["hmask"].rearrange("p (h o) -> p h o", o=1).broadcast_to([128, HEADS, TC]),
                                    ALU.mult)
            return a

        def queries_pool(g, c, k):
            g.wait_ge(S("phi_a"), c + 1)
            expand_queries(g, KP[k % 2], QG[k % 2]).then_inc(S("qg"), 1)

        def local_queries_pool(g, c, cc):
            g.wait_ge(S("qr"), c + 1)
            if cc >= 1:
                g.wait_ge(S("ring_mm"), use_of(c - 1, cc - 1, "l", blocks_of(cc - 1) - 1)[0] + 1)
            expand_queries(g, qr, QL).then_inc(S("ql"), 1)

        def gate_x_tensor(pe, c):
            pe.wait_ge(S("phi_a"), c + 1)
            nc.tensor.matmul(FR[:, 0:128], w["g1T"], xm_(0), start=True, stop=True).then_inc(S("gx_mm"), 1)

        def gate_x_scalar(act, c, cc, k):
            act.wait_ge(S("gx_mm"), c + 1)
            if cc < CHUNKS - 1:
                act.wait_ge(S("t1"), c + 2)
            nc.scalar.copy(GX[k % 2][:], FR[:, 0:128]).then_inc(S("gx"), 1)

        def keys_tensor(pe, c, cc):
            pe.wait_ge(S("gx"), c + 1)
            if cc < CHUNKS - 1:
                pe.wait_ge(S("x2"), c + 2)
            for n, (wt, l) in enumerate([(wk_of(3), 3), (wk_of(4), 4), (w["klT"], 0)]):
                nc.tensor.matmul(FR[:, 128 * n:128 * n + 128], wt, xm_(l), start=True, stop=True)
            nc.tensor.matmul(FR[:, 384:512], xm_(0), w["vlT"], start=True, stop=True).then_inc(S("pb"), 1)

        def expand_values(act, src, dst, bs=range(BATCH)):
            for b in bs:
                a = nc.scalar.activation(dst[:, :, b, 0:DH], src.rearrange("p (h e) -> p h e", e=DH), ACT.Copy,
                                         scale=c_["bmask"][:, b:b + 1])
            return a

        def local_scalar(act, c, k, part):
            if part == 0:
                nc.scalar.copy(KL[k][:], FR[:, 256:384]).then_inc(S("kl"), 1)
                expand_values(act, FR[:, 384:512], VEL[k], range(2))
            else:
                expand_values(act, FR[:, 384:512], VEL[k], range(2, BATCH)).then_inc(S("vl"), 1)

        def rows_tensor(pe, c, cc, k, part):
            if part == 0:
                pe.wait_ge(S("phi_b"), c + 1)
                pe.wait_ge(S("vl"), c + 1)
                nc.tensor.matmul(FR[:, 0:128], xm_(4), wv_of(4), start=True, stop=True)
                for l in range(3):
                    m = nc.tensor.transpose(FR[:, 128 * l + 128:128 * l + 256],
                                            KP[k % 2][:, 128 * l + 128:128 * l + 256], ident)
                m.then_inc(S("pd"), 1)
            else:
                pe.wait_ge(S("dd_out"), c + 1)
                if cc < CHUNKS - 1:
                    pe.wait_ge(S("xm2"), c + 2)
                for l in range(3, 5):
                    m = nc.tensor.transpose(FR[:, 128 * l - 256:128 * l - 128],
                                            KP[k % 2][:, 128 * l + 128:128 * l + 256], ident)
                m.then_inc(S("kr4"), 1)

        def rows_scalar(act, c, k, part):
            p = k % 2
            if part == 0:
                act.wait_ge(S("pd"), c + 1)
                expand_values(act, FR[:, 0:128], VE[p][:, 4]).then_inc(S("ve4"), 1)
            if part == 1:
                nc.scalar.copy(KR[p][:, 0:384], FR[:, 128:512]).then_inc(S("dd_out"), 1)
            if part == 2:
                act.wait_ge(S("kr4"), c + 1)
                nc.scalar.copy(KR[p][:, 384:640], FR[:, 128:384]).then_inc(S("kr_out"), 1)

        def blocks_of(cc):
            return min(cc, 2) + 1

        def use_of(c, cc, what, n):
            R = blocks_of(cc)
            base = 10 * c - 3 if cc >= 2 else 8 * cc
            first = 1 if cc >= 2 else 0
            off = n if what == "l" else R + ((0, 1, 3, 4, 6)[n] if what == "s" else (2, 5)[n])
            return base + off, (first + off) % 2

        def take(pe, c, cc, what, n):
            use, bank = use_of(c, cc, what, n)
            if not isinstance(use, int) or use >= 2:
                pe.wait_ge(S("ring_read"), use - 1)
            return RG[bank]

        def local_scores(pe, c, cc, k, r):
            if r == 0:
                pe.wait_ge(S("ql"), c + 1)
                pe.wait_ge(S("kl"), c + 1)
            bank = take(pe, c, cc, "l", r)
            for b in range(BATCH):
                m = nc.tensor.matmul(bank[TC * b:TC * b + TC, :], KL[(k - r) % 4][:, TC * b:TC * b + TC],
                                     QL[:, b, :, :].rearrange("p h t -> p (h t)"), start=True, stop=True)
            m.then_inc(S("ring_mm"), 1)

        def level_scores(pe, c, cc, k, l):
            p = k % 2
            if l == 0:
                pe.wait_ge(S("qg"), c + 1)
                pe.wait_ge(S("phi_b"), c + 1)
            bank = take(pe, c, cc, "s", l)
            for b in range(BATCH):
                m = nc.tensor.matmul(bank[TC * b:TC * b + TC, :],
                                     KP[p][:, 128 * l + 128 + TC * b:128 * l + 128 + TC * b + TC],
                                     QG[p][:, b, :, :].rearrange("p h t -> p (h t)"), start=True, stop=True)
            m.then_inc(S("ring_mm"), 1)

        def increase_tensor(pe, c, cc, k, n):
            p = k % 2
            if n == 0:
                pe.wait_ge(S("kr_out"), c + 1)
                pe.wait_ge(S("ve4"), c + 1)
            bank = take(pe, c, cc, "d", n)
            for l in range(3 * n, min(3 * n + 3, LEVELS)):
                for i in range(HG):
                    m = nc.tensor.matmul(bank[TC * i:TC * i + TC, HG * SV * (l - 3 * n):HG * SV * (l - 3 * n + 1)],
                                         KR[p][:, 128 * l + TC * i:128 * l + TC * i + TC],
                                         VE[p][:, l, HG * i:HG * i + HG].rearrange("p h b e -> p (h b e)"),
                                         start=True, stop=True)
            m.then_inc(S("ring_mm"), 1)

        def ring_ready(v, c, cc, what, n):
            use, bank = use_of(c, cc, what, n)
            v.wait_ge(S("ring_mm"), use + 1)
            return RG[bank]

        def increase_vector(v, c, cc, n):
            bank = ring_ready(v, c, cc, "d", n)
            if n == 0:
                v.wait_ge(S("st"), 8 * c)
            L = 3 - n
            v.tensor_tensor(DT[:, 3 * n:3 * n + L].rearrange("p l (g q) -> p l g q", g=HG),
                            bank[:, 0:HG * SV * L].rearrange("p (l g q) -> p l g q", g=HG, q=SV),
                            c_["gmask"].rearrange("p (o g q) -> p o g q", o=1, q=1).broadcast_to([128, L, HG, SV]),
                            ALU.mult).then_inc(S("ring_read"), 1)

        def state_pool(g, c, cc, n):
            g.wait_ge(S("ring_read"), use_of(c, cc, "d", n)[0] + 1)
            if cc >= 1:
                g.wait_ge(S("past"), 2 * c + n - 1)
            elif n == 0:
                g.wait_ge(S("st0"), 1)
            lv = slice(3 * n, min(3 * n + 3, LEVELS))
            for i in range(HG):
                blk = ST[TC * i:TC * i + TC, lv, HG * i:HG * i + HG].rearrange("p l h b e -> p l (h b e)")
                g.tensor_tensor(blk, blk, DT[TC * i:TC * i + TC, lv, :], ALU.add).then_inc(S("st"), 1)

        def out_of(n):
            return OB[:, n // 3, OW * (n % 3):OW * (n % 3) + OW].rearrange("p (b g e) -> p b g e", b=BATCH, e=E9)

        def past_tensor(pe, c, cc, k, n, bs):
            if cc == 0:
                return
            if n == 0 and 0 in bs:
                pe.wait_ge(S("go"), c)
            pe.wait_ge(S("st"), 8 * c - 4 + 4 * n)
            L = 3 - n
            sums = OB[:, n, 0:OW * L].rearrange("p (l b q) -> p l b q", l=L, b=BATCH)
            for b in bs:
                for i in range(HG):
                    m = nc.tensor.matmul(sums[TC * i:TC * i + TC, :, b, :], KP[k % 2][:, TC * b:TC * b + TC],
                                         ST[:, 3 * n:3 * n + L, HG * i:HG * i + HG, b, :], start=b == 0, stop=False,
                                         skip_group_check=True)
            if BATCH - 1 in bs:
                m.then_inc(S("past"), 1)

        def mask_vector(v, c, cc, l):
            bank = ring_ready(v, c, cc, "s", l)
            if cc >= 1 or l >= 2:
                v.wait_ge(S("av"), 5 * c + l - 1)
            v.tensor_tensor(A[l % 2][:], bank[:].rearrange("p (h t) -> p h t", t=TC),
                            c_["causal"].rearrange("p (o t) -> p o t", o=1).broadcast_to([128, HEADS, TC]),
                            ALU.mult).then_inc(S("ring_read"), 1)

        def own_tensor(pe, c, cc, k, l):
            pe.wait_ge(S("ring_read"), use_of(c, cc, "s", l)[0] + 1)
            pe.wait_ge(S("ve3") if l < 4 else S("ve4"), c + 1)
            for g in range(HG):
                for i in range(HG):
                    m = nc.tensor.matmul(out_of(l)[TC * i:TC * i + TC, :, g, :], A[l % 2][:, HG * i + g, :],
                                         VE[k % 2][:, l, HG * i + g, :, :],
                                         start=l % 3 == 0 and cc == 0 and g == 0, stop=True, skip_group_check=True)
            m.then_inc(S("av"), 1)

        def local_mask(v, c, cc, r):
            bank = ring_ready(v, c, cc, "l", r)
            if r == 0:
                v.wait_ge(S("avl"), c)
            v.tensor_tensor(SL[:, r], bank[:].rearrange("p (h t) -> p h t", t=TC),
                            c_["addmask"][:, TC * r:TC * r + TC].rearrange("p (o t) -> p o t", o=1)
                            .broadcast_to([128, HEADS, TC]), ALU.add).then_inc(S("ring_read"), 1)

        def local_turn(v, c, cc, r):
            flat = lambda a: a.rearrange("p h t -> p (h t)")
            if r == 1:
                v.transpose(flat(SR[:, 1]), ring_ready(v, c, cc, "l", 1)[:]).then_inc(S("ring_read"), 1)
            else:
                v.wait_ge(S("ring_read"), use_of(c, cc, "l", r)[0] + 1)
                v.transpose(flat(SR[:, r]), flat(SL[:, r])).then_inc(S("lt"), 1)

        def local_max(v, c, cc, half):
            R, hs = blocks_of(cc), slice(8 * half, 8 * half + 8)
            if half == 0:
                v.wait_ge(S("lt"), (2 * c - 2 if cc >= 2 else cc) + (2 if cc >= 2 else 1))
                if cc >= 1:
                    v.wait_ge(S("ring_read"), use_of(c, cc, "l", 1)[0] + 1)
            v.tensor_reduce(lmx[:, hs], SR[:, 0:R, hs].rearrange("p r h t -> p h r t"), AX.XY, ALU.max)\
                .then_inc(S("lm"), 1)

        def local_shift(v, c):
            v.wait_ge(S("lm"), 2 * c + 2)
            v.tensor_scalar(nmx[:], lmx[:], -(DH ** -0.5), None, ALU.mult).then_inc(S("nm"), 1)

        def local_exp(act, c, cc, hs):
            if hs[0] == 0:
                act.wait_ge(S("nm"), c + 1)
            for h in hs:
                part = SR[:, 0:blocks_of(cc), h, :]
                a = nc.scalar.activation(part, part, ACT.Exp, scale=DH ** -0.5, bias=nmx[:, h:h + 1])
            if hs[-1] == HEADS - 1:
                a.then_inc(S("lx"), 1)

        def local_back(v, c, cc, r):
            if r == 0:
                v.wait_ge(S("lx"), c + 1)
            m = v.transpose(SL[:, r].rearrange("p h t -> p (h t)"), SR[:, r].rearrange("p h t -> p (h t)"))
            if r == blocks_of(cc) - 1:
                m.then_inc(S("pl"), 1)

        def local_tensor(pe, c, cc, k, r):
            if r == 0:
                pe.wait_ge(S("pl"), c + 1)
                pe.wait_ge(S("vl"), c + 1)
            for g in range(HG):
                for i in range(HG):
                    m = nc.tensor.matmul(out_of(LEVELS)[TC * i:TC * i + TC, :, g, :], SL[:, r, HG * i + g, :],
                                         VEL[(k - r) % 4][:, HG * i + g, :, :], start=False, stop=True,
                                         skip_group_check=True)
            if r == blocks_of(cc) - 1:
                m.then_inc(S("avl"), 1)

        ob = OB[:, :, 0:3 * OW].rearrange("p n (m e) -> p n m e", e=E9)
        go = GO[:].rearrange("p (l m) e -> p l (m e)", l=6)

        def weigh(v, c, step):
            if step == 0:
                v.wait_ge(S("av"), 5 * c + 5)
                v.wait_ge(S("avl"), c + 1)
                v.tensor_scalar(RN[:].rearrange("p (n m) -> p n m", n=2), ob[:, :, :, DH], 1.0e-6, None,
                                ALU.max).then_inc(S("r1"), 1)
            if step == 1:
                v.wait_ge(S("r1"), c + 1)
                v.reciprocal(RN[:], RN[:]).then_inc(S("r2"), 1)
            if step == 2:
                v.wait_ge(S("r2"), c + 1)
                v.tensor_tensor(RN[:], RN[:], WL[:].rearrange("p l m -> p (l m)"), ALU.mult).then_inc(S("r3"), 1)
            if step == 3:
                v.wait_ge(S("r3"), c + 1)
                v.tensor_tensor(GO[:].rearrange("p (n m) e -> p n m e", n=2), ob[:, :, :, 0:DH],
                                RN[:].rearrange("p (n m o) -> p n m o", n=2, o=1)
                                .broadcast_to([128, 2, 3 * BATCH * HG, DH]), ALU.mult).then_inc(S("go"), 1)

        def levels_sum(v, c):
            v.wait_ge(S("go"), c + 1)
            v.tensor_reduce(GS[:], go[:, 0:LEVELS, :].rearrange("p l q -> p q l"), AX.X, ALU.add).then_inc(S("gs"), 1)

        def outputs_turn(v, c):
            v.transpose(LT[:], go[:, LEVELS, :]).then_inc(S("ltr"), 1)
            v.wait_ge(S("gs"), c + 1)
            v.transpose(GT[:], GS[:]).then_inc(S("gtr"), 1)

        def difference(v, c):
            v.wait_ge(S("gtr"), c + 1)
            v.wait_ge(S("ltr"), c + 1)
            v.tensor_tensor(DF[:], LT[:], GT[:], ALU.subtract).then_inc(S("df"), 1)

        def gate_tensor(pe, c, cc):
            pe.wait_ge(S("df"), c + 1)
            pe.wait_ge(S("tn1"), c + TAIL + 1 if cc + TAIL < SCAN_TURNS else SCAN_TURNS)
            nc.tensor.matmul(PE_, w["g2T"], DF[:], start=True, stop=True).then_inc(S("gh"), 1)

        def gate_sum(v, c, p):
            v.wait_ge(S("gh"), c + 1)
            v.tensor_tensor(gu[:], PE_, GX[p][:], ALU.add).then_inc(S("gu"), 1)

        def gate_tanh(act, c):
            act.wait_ge(S("gu"), c + 1)
            nc.scalar.activation(gt_[:], gu[:], ACT.Tanh, scale=0.5, bias=hb[:, 0:1]).then_inc(S("gth"), 1)

        def gate_biased(v, c):
            v.wait_ge(S("gu"), c + 1)
            v.tensor_scalar(gu2[:], gu[:], COLS[:, 2:3], None, ALU.add).then_inc(S("gu2"), 1)

        def gate_silu(v, c):
            v.wait_ge(S("gu2"), c + 1)
            v.wait_ge(S("gth"), c + 1)
            v.scalar_tensor_tensor(out=sg[:], in0=gt_[:], scalar=1.0, in1=gu2[:], op0=ALU.add,
                                   op1=ALU.mult).then_inc(S("sg"), 1)

        def alpha_tensor(pe, c):
            pe.wait_ge(S("sg"), c + 1)
            nc.tensor.matmul(PE_, w["go"], sg[:], start=True, stop=True).then_inc(S("al"), 1)

        def alpha_scalar(act, c):
            act.wait_ge(S("al"), c + 1)
            nc.scalar.activation(ta[:], PE_, ACT.Tanh, scale=0.25, bias=hb[:, 1:2]).then_inc(S("ta"), 1)

        def mix_gated(v, c):
            v.wait_ge(S("ta"), c + 1)
            v.scalar_tensor_tensor(out=m2[:], in0=ta[:], scalar=1.0, in1=DF[:], op0=ALU.add, op1=ALU.mult)\
                .then_inc(S("m2"), 1)

        def mix_sum(v, c):
            v.wait_ge(S("m2"), c + 1)
            v.scalar_tensor_tensor(out=mix[:], in0=m2[:], scalar=0.5, in1=GT[:], op0=ALU.mult, op1=ALU.add)\
                .then_inc(S("mix"), 1)

        def output_tensor(pe, c):
            pe.wait_ge(S("mix"), c + 1)
            nc.tensor.matmul(PE_, ones[0:1, :], ROWS[0:1, 256:384], start=True, stop=False)
            nc.tensor.matmul(PE_, mix[:], w["oT"], start=False, stop=True).then_inc(S("po"), 1)

        def output_residual(v, c):
            v.wait_ge(S("po"), c + 1)
            v.tensor_tensor(x3[:], PE_, X[:, c, :], ALU.add).then_inc(S("x3"), 1)

        def ffn2_transpose(pe, c):
            pe.wait_ge(S("d_ln"), c + 1)
            nc.tensor.transpose(PE_, ld[:], ident).then_inc(S("t2"), 1)

        def ffn2_scalar(act, c):
            act.wait_ge(S("t2"), c + 1)
            nc.scalar.copy(ldT[:], PE_).then_inc(S("t2_out"), 1)

        def ffn2_tensor(pe, c):
            pe.wait_ge(S("t2_out"), c + 1)
            nc.tensor.matmul(PE_, ldT[:], w["tern"], start=True, stop=True).then_inc(S("y2"), 1)

        def ffn2_residual(v, c, k):
            v.wait_ge(S("y2"), c + 1)
            v.wait_ge(S(f"out{k % 2}"), 32 * (c - k % 2) + 16)
            v.tensor_tensor(x4[k % 2][:], PE_, x3[:], ALU.add).then_inc(S("x4"), 1)

        def store(sp, c, k):
            sp.wait_ge(S("x4"), c + 1)
            for b in range(BATCH):
                sp.dma_start(out[b].rearrange("(c t) d -> t c d", t=TC)[:, c, :], x4[k % 2][TC * b:TC * b + TC, :])\
                    .then_inc(S(f"out{k % 2}"), 16)

        WARM = [1, 1, 1, 1, 1, 1, 1, 2, 1, 1, 3, 2, 1, 3, 1, 3, 3, 1, 1, 2, 3, 3, 1, 2, 1, 1, 3, 1, 2, 4, 4, 5]
        FIRST, LAST = 7, CHUNKS - 1

        def turns(eng, body):
            for i in range(FIRST):
                body(i, i % 4, i)
            with eng.Fori(FIRST, LAST - 3, 4) as i:
                for n in range(4):
                    body(i + n, (FIRST + n) % 4, FIRST)
            for i in range(LAST, TURNS):
                body(i, i % 4, i)

        def alive(ii, lag):
            return 0 <= ii - lag < CHUNKS

        @block.tensor
        def _(pe):
            pe.wait_ge(S("consts"), 48)
            for p in range(2):
                pe.wait_ge(S(f"out{p}"), 16)
            pe.wait_ge(S("mats"), 16)
            pe.wait_ge(S("zeros"), 1)
            for p in range(2):
                nc.tensor.matmul(Z[p][:, 256:512], zeros[:, 0:128], zeros[:], start=True, stop=False,
                                 skip_group_check=True)
            norm_tensor(pe, 0, 0)
            bias_tensor(pe, 0)
            scan_input(pe, 0, 0, 0, 0, False)
            scan_input(pe, 0, 0, 0, 0, True)
            weights_tensor(pe)

            def turn(i, m, ii):
                p, kp, ka = m % 2, (m - PROJ) % 4, (m - ATTN) % 4
                front, proj, attn, tail = (alive(ii, x) for x in (FRONT, PROJ, ATTN, TAIL))
                f, q, c, e = i - FRONT, i - PROJ, i - ATTN, i - TAIL
                qq, cc, ee = ii - PROJ, ii - ATTN, ii - TAIL
                for t in range(TC):
                    if ii < SCAN_TURNS:
                        scan_tensor(pe, i, p, ii, t)
                        keep_warm(pe, p, max(WARM[t], 5) if ii < FRONT else max(WARM[t], 2) if ii < FIRST else WARM[t])
                    if ii + 1 < CHUNKS and t == 23:
                        norm_tensor(pe, i + 1, ii + 1)
                    if ii + 1 < SCAN_TURNS:
                        if t == 27:
                            scan_input(pe, i + 1, ii + 1, 1 - p, 0, True)
                            scan_input(pe, i + 1, ii + 1, 1 - p, 1, True)
                        if t == 21:
                            bias_tensor(pe, 1 - p)
                        if t == 30:
                            scan_input(pe, i + 1, ii + 1, 1 - p, 1, False)
                            scan_input(pe, i + 1, ii + 1, 1 - p, 0, False)
                    if tail:
                        if t == 3:
                            gate_tensor(pe, e, ee)
                        if t == 7:
                            alpha_tensor(pe, e)
                        if t == 12:
                            output_tensor(pe, e)
                        if t == 19:
                            ffn2_transpose(pe, e)
                        if t == 21:
                            ffn2_tensor(pe, e)
                    if proj and t == 13:
                        gate_x_tensor(pe, q)
                    if front:
                        if t == 1:
                            cell_tensor(pe, f)
                        if t == 13:
                            ffn1_transpose(pe, f)
                        if t == 15:
                            ffn1_tensor(pe, f)
                        if t == 25:
                            means_tensor(pe, f, 0)
                        if t == 28:
                            means_tensor(pe, f, 1)
                    if proj:
                        if t == 5:
                            values_tensor(pe, q, qq)
                        if t == 8:
                            queries_tensor(pe, q)
                        if t == 17:
                            keys_tensor(pe, q, qq)
                        if t == 22:
                            rows_tensor(pe, q, qq, kp, 0)
                        if t == 29:
                            rows_tensor(pe, q, qq, kp, 1)
                    if attn:
                        R = blocks_of(cc)
                        if t in (0, 2, 4) and (0, 2, 4).index(t) < R:
                            local_scores(pe, c, cc, ka, (0, 2, 4).index(t))
                        if t in (3, 7, 13, 15):
                            past_tensor(pe, c, cc, ka, t // 13, (0, 1) if t in (3, 13) else (2, 3))
                        if t in (6, 9, 14, 18, 24):
                            level_scores(pe, c, cc, ka, (6, 9, 14, 18, 24).index(t))
                        if t in (10, 12, 16, 20, 28):
                            own_tensor(pe, c, cc, ka, (10, 12, 16, 20, 28).index(t))
                        if t in (11, 19):
                            increase_tensor(pe, c, cc, ka, (11, 19).index(t))
                        if t in (23, 26, 27) and (23, 26, 27).index(t) < R:
                            local_tensor(pe, c, cc, ka, (23, 26, 27).index(t))
            turns(pe, turn)

        @block.scalar
        def _(act):
            act.wait_ge(S("v_init"), 2)
            norm_scalar(act, 0)
            for n in range(3):
                cand_scalar(act, 0, 0, 0, n)
            weights_scalar(act)

            def turn(i, m, ii):
                p, kp = m % 2, (m - PROJ) % 4
                front, proj, attn, tail = (alive(ii, x) for x in (FRONT, PROJ, ATTN, TAIL))
                f, q, c, e = i - FRONT, i - PROJ, i - ATTN, i - TAIL
                cc = ii - ATTN
                for t in range(TC):
                    if ii < SCAN_TURNS:
                        scan_scalar(act, i, p, ii, t)
                    if ii + 1 < CHUNKS and t == 24:
                        norm_scalar(act, i + 1)
                    if ii + 1 < SCAN_TURNS and t in (28, 29, 30):
                        cand_scalar(act, i + 1, ii + 1, 1 - p, t - 28)
                    if tail:
                        if t == 5:
                            gate_tanh(act, e)
                        if t == 8:
                            alpha_scalar(act, e)
                        if t == 20:
                            ffn2_scalar(act, e)
                    if proj and t == 14:
                        gate_x_scalar(act, q, ii - PROJ, kp)
                    if front:
                        if t == 2:
                            cell_scalar(act, f)
                        if t == 3:
                            cell_scalar_2(act, f)
                        if t == 14:
                            ffn1_scalar(act, f)
                        if t == 26:
                            means_scalar(act, f, 0)
                        if t == 29:
                            means_scalar(act, f, 1)
                    if proj:
                        if t in (6, 7):
                            values_scalar(act, q, kp, (2 * t - 12, 2 * t - 11))
                        if t == 9:
                            queries_copy(act, q)
                            exponential(act, q, True, 0)
                        if t == 10:
                            exponential(act, q, True, 1)
                        if t in (18, 19):
                            exponential(act, q, False, t - 18)
                        if t in (18, 20):
                            local_scalar(act, q, kp, t // 20)
                        if t in (23, 24):
                            rows_scalar(act, q, kp, t - 23)
                        if t == 30:
                            rows_scalar(act, q, kp, 2)
                    if attn and t in (12, 13, 15, 16):
                        local_exp(act, c, cc, range(4 * (12, 13, 15, 16).index(t), 4 * (12, 13, 15, 16).index(t) + 4))
            turns(act, turn)

        @block.vector
        def _(v):
            for p in range(2):
                v.memset(TH[p][:], 0.0).then_inc(S("v_init"), 1)
            v.memset(zeros[:], 0.0).then_inc(S("zeros"), 1)
            v.wait_ge(S("consts"), 48)
            for p in range(2):
                v.wait_ge(S(f"out{p}"), 16)
            for l in range(2):
                v.tensor_scalar(HH[1][:, TC, 4 * l:4 * l + 4, 1], ones[:, 0:4], COLS[:, l:l + 1], None,
                                ALU.mult).then_inc(S("v_init"), 1)
            v.tensor_scalar(G1[:], G1[:], 1.0, None, ALU.add).then_inc(S("v_init"), 1)
            v.wait_ge(S("x_in"), 64)
            norm_stats(v, 0)
            norm_aggregate(v, 0)
            norm_epsilon(v, 0)
            norm_apply(v, 0)
            norm_floor(v, 0)
            v.wait_ge(S("v_init"), 5)
            norm_rms(v, 0)
            v.wait_ge(S("nh"), 1)
            halves(v, 0, HH[1][:, TC, :, 1], NH[0][:, 0, :], slice(0, 4))
            weights_vector(v)

            def turn(i, m, ii):
                p, kp, ke = m % 2, (m - PROJ) % 4, (m - TAIL) % 4
                front, proj, attn, tail = (alive(ii, x) for x in (FRONT, PROJ, ATTN, TAIL))
                f, q, c, e = i - FRONT, i - PROJ, i - ATTN, i - TAIL
                cc = ii - ATTN
                for t in range(TC):
                    if ii < SCAN_TURNS:
                        scan_vector(v, i, p, ii, t)
                    if ii + 1 < CHUNKS:
                        if t == 4:
                            norm_stats(v, i + 1)
                        if t == 6:
                            norm_aggregate(v, i + 1)
                        if t == 7:
                            norm_epsilon(v, i + 1)
                        if t == 9:
                            norm_apply(v, i + 1)
                        if t == 11:
                            norm_floor(v, i + 1)
                        if t == 14:
                            norm_rms(v, i + 1)
                    if tail:
                        if t == 0:
                            levels_sum(v, e)
                        if t == 1:
                            outputs_turn(v, e)
                        if t == 2:
                            difference(v, e)
                        if t == 4:
                            gate_sum(v, e, ke % 2)
                        if t == 5:
                            gate_biased(v, e)
                        if t == 6:
                            gate_silu(v, e)
                        if t == 9:
                            mix_gated(v, e)
                        if t == 10:
                            mix_sum(v, e)
                        if t == 13:
                            output_residual(v, e)
                        if t == 14:
                            ln_stats(v, e, "d", x3[:], "x3")
                        if t == 15:
                            ln_aggregate(v, e, "d")
                        if t == 16:
                            ln_epsilon(v, e, "d")
                        if t == 18:
                            ln_apply(v, e, "d", x3[:], ld[:], "t2")
                        if t == 22:
                            ffn2_residual(v, e, ke)
                    if front:
                        if t == 4:
                            cell_difference(v, f)
                        if t == 5:
                            cell_gated(v, f)
                        if t == 6:
                            cell_residual(v, f)
                        if t == 7:
                            ln_stats(v, f, "a", X[:, f, :], "x1")
                        if t == 8:
                            ln_aggregate(v, f, "a")
                        if t == 9:
                            ln_epsilon(v, f, "a")
                        if t == 12:
                            ln_apply(v, f, "a", X[:, f, :], la[:], "t1")
                        if t == 16:
                            ffn1_residual(v, f)
                        if t == 17:
                            ln_stats(v, f, "b", X[:, f, :], "x2")
                        if t == 18:
                            ln_aggregate(v, f, "b")
                        if t == 19:
                            ln_epsilon(v, f, "b")
                        if t == 21:
                            ln_apply(v, f, "b", X[:, f, :], xb[:], "xm_b")
                    if proj:
                        if t == 12:
                            features(v, q, kp, True)
                        if t == 21:
                            features(v, q, kp, False)
                    if attn:
                        R = blocks_of(cc)
                        if t == 1:
                            local_mask(v, c, cc, 0)
                        if t == 3 and R > 1:
                            local_turn(v, c, cc, 1)
                        if t == 2:
                            local_turn(v, c, cc, 0)
                        if t == 5 and R > 2:
                            local_mask(v, c, cc, 2)
                        if t in (8, 11, 15, 19, 25):
                            mask_vector(v, c, cc, (8, 11, 15, 19, 25).index(t))
                        if t == 6 and R > 2:
                            local_turn(v, c, cc, 2)
                        if t in (7, 10):
                            local_max(v, c, cc, (7, 10).index(t))
                        if t == 11:
                            local_shift(v, c)
                        if t in (13, 21):
                            increase_vector(v, c, cc, (13, 21).index(t))
                        if t in (17, 20, 22) and (17, 20, 22).index(t) < R:
                            local_back(v, c, cc, (17, 20, 22).index(t))
                        if t == 29:
                            weigh(v, c, 0)
                        if t == 30:
                            weigh(v, c, 1)
                            weigh(v, c, 2)
                        if t == 31:
                            weigh(v, c, 3)
            turns(v, turn)

        @block.gpsimd
        def _(g):
            g.wait_ge(S("consts"), 48)
            norm_root(g, 0)
            norm_root_2(g, 0)
            norm_residual(g, 0)

            def turn(i, m, ii):
                p, kp = m % 2, (m - PROJ) % 4
                front, proj, attn, tail = (alive(ii, x) for x in (FRONT, PROJ, ATTN, TAIL))
                f, q, c, e = i - FRONT, i - PROJ, i - ATTN, i - TAIL
                cc = ii - ATTN
                if attn and cc >= 1 or tail:
                    g.wait_ge(S("st"), 8 * c)
                if front:
                    copy_states(g, i, f, 1 - p)
                if ii + 1 < CHUNKS:
                    norm_root(g, i + 1)
                if front:
                    ln_root(g, f, "a")
                if ii + 1 < CHUNKS:
                    norm_root_2(g, i + 1)
                if proj:
                    queries_pool(g, q, kp)
                if tail:
                    ln_root(g, e, "d")
                if ii + 1 < CHUNKS:
                    norm_residual(g, i + 1)
                if proj:
                    local_queries_pool(g, q, ii - PROJ)
                if front:
                    ln_root(g, f, "b")
                if attn:
                    if front:
                        g.wait_ge(S("b_rs"), f + 1)
                    elif proj:
                        g.wait_ge(S("ql"), q + 1)
                    else:
                        g.wait_ge(S("d_rs"), e + 1)
                    for n in range(2):
                        state_pool(g, c, cc, n)
            turns(g, turn)

        @block.sync
        def _(sp):
            sp.dma_start(C[:], ins["consts"]).then_inc(S("consts"), 16)
            for b in range(BATCH):
                sp.dma_start(X[TC * b:TC * b + TC, :, :],
                             ins["x"][b].rearrange("(c t) d -> t c d", t=TC)).then_inc(S("x_in"), 16)
            sp.dma_start(G1[:], ins["gamma_rows"]).then_inc(S("consts"), 16)
            sp.dma_start(COLS[:], ins["cols"]).then_inc(S("consts"), 16)
            sp.dma_start(ROWS[0:1, :], ins["rows"][0:1, :]).then_inc(S("out0"), 16)
            sp.dma_start(ROWS[1:2, :], ins["rows"][1:2, :]).then_inc(S("out1"), 16)
            sp.dma_start(W[:], ins["mats"]).then_inc(S("mats"), 16)

            def turn(i, m, ii):
                if alive(ii, TAIL):
                    store(sp, i - TAIL, (m - TAIL) % 4)
            turns(sp, turn)
            for p in range(2):
                sp.wait_ge(S(f"out{p}"), 32 * CHUNKS + 16)


def kernel(**inputs):
    import numpy as np
    import concourse.bacc as bacc
    from concourse.bass_utils import run_bass_kernel_spmd

    a = {k: np.asarray(v) for k, v in inputs.items()}
    A, B_ = "L0_attn_a_", "L0_attn_b_"
    lWi, lWif, lWhf = a[A + "lWi"], a[A + "lWif"], a[A + "lWhf"]
    Wg = a[B_ + "Wg"]
    hk, hv = a[B_ + "haar_Wk"], a[B_ + "haar_Wv"]
    mats = {"i1": lWi[0].T, "f1": lWif[0].T, "r1": lWhf[0].T, "i2": lWi[1].T, "f2": lWif[1].T, "r2": lWhf[1].T,
            "gi": a[A + "gWi"].T, "gf": a[A + "gWif"].T, "gh": a[A + "gWhf"].T,
            "wk": a[B_ + "Wk"], "wv": a[B_ + "Wv"], "qT": a[B_ + "Wq"].T, "klT": a[B_ + "Wkl"].T,
            "vlT": a[B_ + "Wvl"].T, "kT": a[B_ + "Wk"].T, "vT": a[B_ + "Wv"].T,
            "g1T": Wg[:, 0:D].T, "g2T": Wg[:, D:].T, "oT": a[B_ + "Wo"].T, "tern": a["L0_ffn_weight"].T,
            "go": np.broadcast_to(a[B_ + "Wgo"].reshape(D, 1), (D, D))}
    for l in range(4):
        for n, m in (("hk", hk), ("hv", hv)):
            mats[f"{n}{l}"] = np.broadcast_to(m[l].T[None, :, None, :], (HEADS, DH, HEADS, DH)).reshape(D, D)
    mats = np.ascontiguousarray(np.concatenate([mats[n] for n in MATS], axis=1))
    cols = np.concatenate([a[A + "l_init_hidden"].T, a[B_ + "bg"].reshape(D, 1),
                           np.broadcast_to(a[B_ + "bgo"].reshape(1, 1), (D, 1)),
                           np.broadcast_to(a[B_ + "haar_scale"].reshape(1, 4), (D, 4)),
                           np.zeros((D, 4), np.float32)], axis=1)
    rows = np.zeros((2, 5 * 128 + 256), np.float32)
    rows[0:2, 0:128] = a[A + "lbhf"]
    rows[0, 128:256] = a[A + "gbhf"]
    rows[0, 256:384] = a[B_ + "bo"]
    rows[:, 640:896] = np.tile(np.repeat(np.eye(2, dtype=np.float32), BATCH, axis=1), (1, TC))
    s, t = np.arange(TC)[:, None], np.arange(TC)[None, :]
    means = np.zeros((128, LEVELS, 128), np.float32)
    for l in range(LEVELS):
        size = 2 ** l
        m = ((s <= t) & (s >= t // size * size)) / (t % size + 1.0)
        for b in range(BATCH):
            means[TC * b:TC * b + TC, l, TC * b:TC * b + TC] = m
    causal = np.tile((s <= t).astype(np.float32), (BATCH, 1))
    add = np.concatenate([np.where(s <= t, 0.0, NEG), np.zeros((TC, TC)), np.where(s > t, 0.0, NEG)], axis=1)
    consts = np.concatenate([np.eye(128), means.reshape(128, -1), causal,
                             np.repeat(np.eye(HEADS), DH, axis=0), np.repeat(np.eye(BATCH), TC, axis=0),
                             np.tile(np.repeat(np.eye(HG), DH, axis=0), (HG, 1)),
                             np.tile(add, (BATCH, 1)), np.full((128, 2), -0.5), np.ones((128, 128))],
                            axis=1).astype(np.float32)
    arrays = {"x": a[A + "x"], "gamma_rows": np.ascontiguousarray(np.broadcast_to(a[A + "gamma"][None], (128, D))),
              "cols": np.ascontiguousarray(cols), "rows": rows, "mats": mats, "consts": np.ascontiguousarray(consts)}
    nc = bacc.Bacc("TRN2", target_bir_lowering=False, num_devices=1)
    ins = {n: nc.dram_tensor("in_" + n, v.shape, mybir.dt.from_np(v.dtype), kind="ExternalInput").ap()
           for n, v in arrays.items()}
    out = nc.dram_tensor("out_0", (BATCH, TOKENS, D), F32, kind="ExternalOutput").ap()
    build(nc, ins, out)
    r = run_bass_kernel_spmd(nc, [{"in_" + n: v for n, v in arrays.items()}], core_ids=[0])
    return r.results[0]["out_0"]
```
